# Optimizing a Trainium2 kernel written in Bass

```python
import numpy as np
import jax
import jax.numpy as jnp

def _softmax(x, axis=-1):
    return jax.nn.softmax(x, axis=axis)

def _gelu(x):
    return jax.nn.gelu(x, approximate=True)

def _silu(x):
    return jax.nn.silu(x)

def _sigmoid(x):
    return jax.nn.sigmoid(x)

def _layernorm(x, axis=-1, eps=1e-05):
    m = jnp.mean(x, axis=axis, keepdims=True)
    v = jnp.var(x, axis=axis, keepdims=True)
    return (x - m) / jnp.sqrt(v + eps)

def _scatter_add(tgt, idx, src, axis=0):
    return tgt.at[idx].add(src)

def _segment_sum(src, seg, n):
    return jax.ops.segment_sum(src, seg, n)
kernel_name = 'mk_conv_preact_d4_conv_nhwc256_r4_b1da8f'

def setup_inputs(seed: int=0):
    np.random.seed(seed)
    _w = jnp.asarray

    def _rec_inputs():
        import jax
        import jax.numpy as jnp
        _gk = jax.random.key(seed)
        x = -7.109e-05 + 0.9999 * jax.random.normal(jax.random.fold_in(_gk, 1), (2, 64, 64, 64), jnp.float32)
        return x
    x = _rec_inputs()

    def _L0_conv_setup():
        import jax, jax.numpy as jnp
        import numpy as np
        B, C, H, W = (4, 64, 64, 64)
        SG = 8
        PN = H // 4 * (W // 4)

        def _conv1d(w, b, x):
            return jnp.einsum('oi,bil->bol', w, x) + b[:, None]

        def _bilinear_align_corners(x, oh, ow):
            b, c, ih, iw = x.shape
            ys = jnp.linspace(0.0, ih - 1.0, oh)
            xs = jnp.linspace(0.0, iw - 1.0, ow)
            y0 = jnp.floor(ys).astype(jnp.int32)
            y1 = jnp.minimum(y0 + 1, ih - 1)
            wy = ys - y0.astype(x.dtype)
            x0 = jnp.floor(xs).astype(jnp.int32)
            x1 = jnp.minimum(x0 + 1, iw - 1)
            wx = xs - x0.astype(x.dtype)
            r0 = jnp.take(x, y0, axis=2)
            r1 = jnp.take(x, y1, axis=2)
            rows = r0 + (r1 - r0) * wy[None, None, :, None]
            c0 = jnp.take(rows, x0, axis=3)
            c1 = jnp.take(rows, x1, axis=3)
            return c0 + (c1 - c0) * wx[None, None, None, :]
        key = jax.random.key(seed)
        ks = jax.random.split(key, 16)
        s = 0.02
        return {'x': jax.random.normal(ks[0], (B, C, H, W), jnp.float32), 'se_groups': SG, 'gcn_weight': jax.random.normal(ks[1], (PN, PN), jnp.float32) * s, 'gcn_bias': jax.random.normal(ks[2], (PN,), jnp.float32) * s, 'gcn_qw': jax.random.normal(ks[3], (PN // 4, PN), jnp.float32) * s, 'gcn_qb': jax.random.normal(ks[4], (PN // 4,), jnp.float32) * s, 'gcn_kw': jax.random.normal(ks[5], (PN // 4, PN), jnp.float32) * s, 'gcn_kb': jax.random.normal(ks[6], (PN // 4,), jnp.float32) * s, 'gcn_vw': jax.random.normal(ks[7], (PN, PN), jnp.float32) * s, 'gcn_vb': jax.random.normal(ks[8], (PN,), jnp.float32) * s, 'qw': jax.random.normal(ks[9], (PN // 4, PN), jnp.float32) * s, 'qb': jax.random.normal(ks[10], (PN // 4,), jnp.float32) * s, 'kw': jax.random.normal(ks[11], (PN // 4, PN), jnp.float32) * s, 'kb': jax.random.normal(ks[12], (PN // 4,), jnp.float32) * s, 'vw': jax.random.normal(ks[13], (PN, PN), jnp.float32) * s, 'vb': jax.random.normal(ks[14], (PN,), jnp.float32) * s}
    _L0_conv_all = _L0_conv_setup()
    _L0_conv_in = {k: v for k, v in _L0_conv_all.items() if k in ('gcn_weight', 'gcn_bias', 'gcn_qw', 'gcn_qb', 'gcn_kw', 'gcn_kb', 'gcn_vw', 'gcn_vb', 'qw', 'qb', 'kw', 'kb', 'vw', 'vb')}
    del _L0_conv_all

    def _L1_conv_setup():
        import jax, jax.numpy as jnp
        import numpy as np
        from jax import lax
        D_MODEL = 64
        D_STATE = 16
        D_CONV = 4
        EXPAND = 2
        D_INNER = EXPAND * D_MODEL
        DT_RANK = (D_MODEL + 15) // 16
        B, T, N = (2, 32, 16)
        LN_EPS = 1e-05

        def _mamba_block(xr, W_in, W_conv, b_conv, W_xproj, W_dt, b_dt, A_log, D_param, W_out):
            xz = xr @ W_in.T
            xp, z = jnp.split(xz, 2, axis=-1)
            xc = lax.conv_general_dilated(xp.transpose(0, 2, 1), W_conv, (1,), [(D_CONV - 1, 0)], dimension_numbers=('NCH', 'OIH', 'NCH'), feature_group_count=D_INNER)
            u = jax.nn.silu(xc + b_conv[None, :, None]).transpose(0, 2, 1)
            x_dbl = u @ W_xproj.T
            dt_raw = x_dbl[..., :DT_RANK]
            Bm = x_dbl[..., DT_RANK:DT_RANK + D_STATE]
            Cm = x_dbl[..., DT_RANK + D_STATE:]
            dt = jax.nn.softplus(dt_raw @ W_dt.T + b_dt)
            A = -jnp.exp(A_log)

            def step(h, inps):
                dt_t, B_t, C_t, u_t = inps
                dA = jnp.exp(dt_t[..., None] * A)
                h = h * dA + dt_t[..., None] * B_t[:, None, :] * u_t[..., None]
                y = jnp.einsum('bds,bs->bd', h, C_t)
                return (h, y)
            BN = xr.shape[0]
            h0 = jnp.zeros((BN, D_INNER, D_STATE), xr.dtype)
            xs = (dt.transpose(1, 0, 2), Bm.transpose(1, 0, 2), Cm.transpose(1, 0, 2), u.transpose(1, 0, 2))
            _, ys = lax.scan(step, h0, xs)
            y = ys.transpose(1, 0, 2) + u * D_param
            y = y * jax.nn.silu(z)
            return y @ W_out.T
        key = jax.random.key(seed)
        ks = jax.random.split(key, 8)
        s = 0.02
        return {'x': jax.random.normal(ks[0], (B, T, N, D_MODEL), jnp.float32), 'W_in': jax.random.normal(ks[1], (2 * D_INNER, D_MODEL), jnp.float32) * s, 'W_conv': jax.random.normal(ks[2], (D_INNER, 1, D_CONV), jnp.float32) * s, 'b_conv': jnp.zeros((D_INNER,), jnp.float32), 'W_xproj': jax.random.normal(ks[3], (DT_RANK + 2 * D_STATE, D_INNER), jnp.float32) * s, 'W_dt': jax.random.normal(ks[4], (D_INNER, DT_RANK), jnp.float32) * s, 'b_dt': jax.random.normal(ks[5], (D_INNER,), jnp.float32) * 0.1, 'A_log': jnp.log(jnp.tile(jnp.arange(1, D_STATE + 1, dtype=jnp.float32), (D_INNER, 1))), 'D_param': jnp.ones((D_INNER,), jnp.float32), 'W_out': jax.random.normal(ks[6], (D_MODEL, D_INNER), jnp.float32) * s, 'gamma': jnp.ones((D_MODEL,), jnp.float32), 'beta': jnp.zeros((D_MODEL,), jnp.float32)}
    _L1_conv_all = _L1_conv_setup()
    _L1_conv_in = {k: v for k, v in _L1_conv_all.items() if k in ('W_in', 'W_conv', 'b_conv', 'W_xproj', 'W_dt', 'b_dt', 'A_log', 'D_param', 'W_out', 'gamma', 'beta')}
    del _L1_conv_all

    def _L2_conv_setup():
        import jax, jax.numpy as jnp
        import numpy as np
        HID, NL, DSTATE, DCONV, EXPAND = (64, 2, 16, 4, 2)
        DIN = EXPAND * HID
        NHEADS = DIN // 16
        HEADP = DIN // NHEADS
        CONVDIM = DIN + 2 * DSTATE
        PROJDIM = 2 * DIN + 2 * DSTATE + NHEADS
        B, T, NB = (2, 48, 62)

        def _rmsnorm(x, w, eps=1e-06):
            return x * jax.lax.rsqrt(jnp.mean(x * x, -1, keepdims=True) + eps) * w

        def _causal_conv(x, w, b):
            K = w.shape[1]
            L = x.shape[1]
            xp = jnp.pad(x, ((0, 0), (K - 1, 0), (0, 0)))
            y = b
            for k in range(K):
                y = y + xp[:, k:k + L, :] * w[:, k]
            return y

        def _ssd(xh, dt, A, Bm, Cm):
            cum = jnp.cumsum(dt * A, axis=1)
            diff = cum[:, :, None, :] - cum[:, None, :, :]
            mask = jnp.tril(jnp.ones((xh.shape[1], xh.shape[1]), bool))
            decay = jnp.where(mask[None, :, :, None], jnp.exp(diff), 0.0)
            scores = jnp.einsum('bln,bsn->bls', Cm, Bm)[..., None] * decay * dt[:, None, :, :]
            return jnp.einsum('blsh,bshp->blhp', scores, xh)

        def _mamba2(x, Win, Wconv, bconv, dt_bias, A_log, D, gn_w, Wout):
            b, l, _ = x.shape
            zxbcdt = x @ Win
            z = zxbcdt[..., :DIN]
            xBC = jax.nn.silu(_causal_conv(zxbcdt[..., DIN:DIN + CONVDIM], Wconv, bconv))
            xh = xBC[..., :DIN].reshape(b, l, NHEADS, HEADP)
            Bm = xBC[..., DIN:DIN + DSTATE]
            Cm = xBC[..., DIN + DSTATE:]
            dt = jax.nn.softplus(zxbcdt[..., -NHEADS:] + dt_bias)
            A = -jnp.exp(A_log)
            rev = lambda t: t[:, ::-1]
            y = _ssd(xh, dt, A, Bm, Cm) + rev(_ssd(rev(xh), rev(dt), A, rev(Bm), rev(Cm)))
            y = y + D[None, None, :, None] * xh
            y = _rmsnorm(y.reshape(b, l, DIN) * jax.nn.silu(z), gn_w)
            return y @ Wout

        def _forward(x, tp, bp):
            batch, T_, NB_, H_ = x.shape
            for i in range(NL):
                xt = jnp.transpose(x, (0, 2, 1, 3)).reshape(batch * NB_, T_, H_)
                xt = xt + _mamba2(_rmsnorm(xt, tp[0][i]), *(p[i] for p in tp[1:]))
                x = jnp.transpose(xt.reshape(batch, NB_, T_, H_), (0, 2, 1, 3))
                xb = x.reshape(batch * T_, NB_, H_)
                xb = xb + _mamba2(_rmsnorm(xb, bp[0][i]), *(p[i] for p in bp[1:]))
                x = xb.reshape(batch, T_, NB_, H_)
            return x
        key = jax.random.key(seed)
        ks = jax.random.split(key, 3)
        inp = {'x': jax.random.normal(ks[0], (B, T, NB, HID), jnp.float32)}
        for i, ax in enumerate(('t', 'b')):
            kk = jax.random.split(ks[1 + i], 5)
            inp[ax + '_norm_w'] = jnp.ones((NL, HID), jnp.float32)
            inp[ax + '_Win'] = jax.random.normal(kk[0], (NL, HID, PROJDIM), jnp.float32) * HID ** (-0.5)
            inp[ax + '_Wconv'] = jax.random.normal(kk[1], (NL, CONVDIM, DCONV), jnp.float32) * DCONV ** (-0.5)
            inp[ax + '_bconv'] = jnp.zeros((NL, CONVDIM), jnp.float32)
            dt = jnp.exp(jax.random.uniform(kk[2], (NL, NHEADS)) * (np.log(0.1) - np.log(0.001)) + np.log(0.001))
            inp[ax + '_dt_bias'] = jnp.log(jnp.expm1(dt)).astype(jnp.float32)
            inp[ax + '_A_log'] = jnp.log(jax.random.uniform(kk[3], (NL, NHEADS), minval=1.0, maxval=16.0)).astype(jnp.float32)
            inp[ax + '_D'] = jnp.ones((NL, NHEADS), jnp.float32)
            inp[ax + '_gn_w'] = jnp.ones((NL, DIN), jnp.float32)
            inp[ax + '_Wout'] = jax.random.normal(kk[4], (NL, DIN, HID), jnp.float32) * DIN ** (-0.5)
        return inp
    _L2_conv_all = _L2_conv_setup()
    _L2_conv_in = {k: v for k, v in _L2_conv_all.items() if k in ('t_norm_w', 't_Win', 't_Wconv', 't_bconv', 't_dt_bias', 't_A_log', 't_D', 't_gn_w', 't_Wout', 'b_norm_w', 'b_Win', 'b_Wconv', 'b_bconv', 'b_dt_bias', 'b_A_log', 'b_D', 'b_gn_w', 'b_Wout')}
    del _L2_conv_all

    def _L3_conv_setup():
        import jax, jax.numpy as jnp
        import numpy as np
        HID, NL, DSTATE, DCONV, EXPAND = (64, 2, 16, 4, 2)
        DIN = EXPAND * HID
        NHEADS = DIN // 16
        HEADP = DIN // NHEADS
        CONVDIM = DIN + 2 * DSTATE
        PROJDIM = 2 * DIN + 2 * DSTATE + NHEADS
        B, T, NB = (2, 48, 62)

        def _rmsnorm(x, w, eps=1e-06):
            return x * jax.lax.rsqrt(jnp.mean(x * x, -1, keepdims=True) + eps) * w

        def _causal_conv(x, w, b):
            K = w.shape[1]
            L = x.shape[1]
            xp = jnp.pad(x, ((0, 0), (K - 1, 0), (0, 0)))
            y = b
            for k in range(K):
                y = y + xp[:, k:k + L, :] * w[:, k]
            return y

        def _ssd(xh, dt, A, Bm, Cm):
            cum = jnp.cumsum(dt * A, axis=1)
            diff = cum[:, :, None, :] - cum[:, None, :, :]
            mask = jnp.tril(jnp.ones((xh.shape[1], xh.shape[1]), bool))
            decay = jnp.where(mask[None, :, :, None], jnp.exp(diff), 0.0)
            scores = jnp.einsum('bln,bsn->bls', Cm, Bm)[..., None] * decay * dt[:, None, :, :]
            return jnp.einsum('blsh,bshp->blhp', scores, xh)

        def _mamba2(x, Win, Wconv, bconv, dt_bias, A_log, D, gn_w, Wout):
            b, l, _ = x.shape
            zxbcdt = x @ Win
            z = zxbcdt[..., :DIN]
            xBC = jax.nn.silu(_causal_conv(zxbcdt[..., DIN:DIN + CONVDIM], Wconv, bconv))
            xh = xBC[..., :DIN].reshape(b, l, NHEADS, HEADP)
            Bm = xBC[..., DIN:DIN + DSTATE]
            Cm = xBC[..., DIN + DSTATE:]
            dt = jax.nn.softplus(zxbcdt[..., -NHEADS:] + dt_bias)
            A = -jnp.exp(A_log)
            rev = lambda t: t[:, ::-1]
            y = _ssd(xh, dt, A, Bm, Cm) + rev(_ssd(rev(xh), rev(dt), A, rev(Bm), rev(Cm)))
            y = y + D[None, None, :, None] * xh
            y = _rmsnorm(y.reshape(b, l, DIN) * jax.nn.silu(z), gn_w)
            return y @ Wout

        def _forward(x, tp, bp):
            batch, T_, NB_, H_ = x.shape
            for i in range(NL):
                xt = jnp.transpose(x, (0, 2, 1, 3)).reshape(batch * NB_, T_, H_)
                xt = xt + _mamba2(_rmsnorm(xt, tp[0][i]), *(p[i] for p in tp[1:]))
                x = jnp.transpose(xt.reshape(batch, NB_, T_, H_), (0, 2, 1, 3))
                xb = x.reshape(batch * T_, NB_, H_)
                xb = xb + _mamba2(_rmsnorm(xb, bp[0][i]), *(p[i] for p in bp[1:]))
                x = xb.reshape(batch, T_, NB_, H_)
            return x
        key = jax.random.key(seed)
        ks = jax.random.split(key, 3)
        inp = {'x': jax.random.normal(ks[0], (B, T, NB, HID), jnp.float32)}
        for i, ax in enumerate(('t', 'b')):
            kk = jax.random.split(ks[1 + i], 5)
            inp[ax + '_norm_w'] = jnp.ones((NL, HID), jnp.float32)
            inp[ax + '_Win'] = jax.random.normal(kk[0], (NL, HID, PROJDIM), jnp.float32) * HID ** (-0.5)
            inp[ax + '_Wconv'] = jax.random.normal(kk[1], (NL, CONVDIM, DCONV), jnp.float32) * DCONV ** (-0.5)
            inp[ax + '_bconv'] = jnp.zeros((NL, CONVDIM), jnp.float32)
            dt = jnp.exp(jax.random.uniform(kk[2], (NL, NHEADS)) * (np.log(0.1) - np.log(0.001)) + np.log(0.001))
            inp[ax + '_dt_bias'] = jnp.log(jnp.expm1(dt)).astype(jnp.float32)
            inp[ax + '_A_log'] = jnp.log(jax.random.uniform(kk[3], (NL, NHEADS), minval=1.0, maxval=16.0)).astype(jnp.float32)
            inp[ax + '_D'] = jnp.ones((NL, NHEADS), jnp.float32)
            inp[ax + '_gn_w'] = jnp.ones((NL, DIN), jnp.float32)
            inp[ax + '_Wout'] = jax.random.normal(kk[4], (NL, DIN, HID), jnp.float32) * DIN ** (-0.5)
        return inp
    _L3_conv_all = _L3_conv_setup()
    _L3_conv_in = {k: v for k, v in _L3_conv_all.items() if k in ('t_norm_w', 't_Win', 't_Wconv', 't_bconv', 't_dt_bias', 't_A_log', 't_D', 't_gn_w', 't_Wout', 'b_norm_w', 'b_Win', 'b_Wconv', 'b_bconv', 'b_dt_bias', 'b_A_log', 'b_D', 'b_gn_w', 'b_Wout')}
    del _L3_conv_all
    return {'x': x, 'L0_conv_gcn_weight': _L0_conv_in['gcn_weight'], 'L0_conv_gcn_bias': _L0_conv_in['gcn_bias'], 'L0_conv_gcn_qw': _L0_conv_in['gcn_qw'], 'L0_conv_gcn_qb': _L0_conv_in['gcn_qb'], 'L0_conv_gcn_kw': _L0_conv_in['gcn_kw'], 'L0_conv_gcn_kb': _L0_conv_in['gcn_kb'], 'L0_conv_gcn_vw': _L0_conv_in['gcn_vw'], 'L0_conv_gcn_vb': _L0_conv_in['gcn_vb'], 'L0_conv_qw': _L0_conv_in['qw'], 'L0_conv_qb': _L0_conv_in['qb'], 'L0_conv_kw': _L0_conv_in['kw'], 'L0_conv_kb': _L0_conv_in['kb'], 'L0_conv_vw': _L0_conv_in['vw'], 'L0_conv_vb': _L0_conv_in['vb'], 'L1_conv_W_in': _L1_conv_in['W_in'], 'L1_conv_W_conv': _L1_conv_in['W_conv'], 'L1_conv_b_conv': _L1_conv_in['b_conv'], 'L1_conv_W_xproj': _L1_conv_in['W_xproj'], 'L1_conv_W_dt': _L1_conv_in['W_dt'], 'L1_conv_b_dt': _L1_conv_in['b_dt'], 'L1_conv_A_log': _L1_conv_in['A_log'], 'L1_conv_D_param': _L1_conv_in['D_param'], 'L1_conv_W_out': _L1_conv_in['W_out'], 'L1_conv_gamma': _L1_conv_in['gamma'], 'L1_conv_beta': _L1_conv_in['beta'], 'L2_conv_t_norm_w': _L2_conv_in['t_norm_w'], 'L2_conv_t_Win': _L2_conv_in['t_Win'], 'L2_conv_t_Wconv': _L2_conv_in['t_Wconv'], 'L2_conv_t_bconv': _L2_conv_in['t_bconv'], 'L2_conv_t_dt_bias': _L2_conv_in['t_dt_bias'], 'L2_conv_t_A_log': _L2_conv_in['t_A_log'], 'L2_conv_t_D': _L2_conv_in['t_D'], 'L2_conv_t_gn_w': _L2_conv_in['t_gn_w'], 'L2_conv_t_Wout': _L2_conv_in['t_Wout'], 'L2_conv_b_norm_w': _L2_conv_in['b_norm_w'], 'L2_conv_b_Win': _L2_conv_in['b_Win'], 'L2_conv_b_Wconv': _L2_conv_in['b_Wconv'], 'L2_conv_b_bconv': _L2_conv_in['b_bconv'], 'L2_conv_b_dt_bias': _L2_conv_in['b_dt_bias'], 'L2_conv_b_A_log': _L2_conv_in['b_A_log'], 'L2_conv_b_D': _L2_conv_in['b_D'], 'L2_conv_b_gn_w': _L2_conv_in['b_gn_w'], 'L2_conv_b_Wout': _L2_conv_in['b_Wout'], 'L3_conv_t_norm_w': _L3_conv_in['t_norm_w'], 'L3_conv_t_Win': _L3_conv_in['t_Win'], 'L3_conv_t_Wconv': _L3_conv_in['t_Wconv'], 'L3_conv_t_bconv': _L3_conv_in['t_bconv'], 'L3_conv_t_dt_bias': _L3_conv_in['t_dt_bias'], 'L3_conv_t_A_log': _L3_conv_in['t_A_log'], 'L3_conv_t_D': _L3_conv_in['t_D'], 'L3_conv_t_gn_w': _L3_conv_in['t_gn_w'], 'L3_conv_t_Wout': _L3_conv_in['t_Wout'], 'L3_conv_b_norm_w': _L3_conv_in['b_norm_w'], 'L3_conv_b_Win': _L3_conv_in['b_Win'], 'L3_conv_b_Wconv': _L3_conv_in['b_Wconv'], 'L3_conv_b_bconv': _L3_conv_in['b_bconv'], 'L3_conv_b_dt_bias': _L3_conv_in['b_dt_bias'], 'L3_conv_b_A_log': _L3_conv_in['b_A_log'], 'L3_conv_b_D': _L3_conv_in['b_D'], 'L3_conv_b_gn_w': _L3_conv_in['b_gn_w'], 'L3_conv_b_Wout': _L3_conv_in['b_Wout']}

def reference(x, L0_conv_gcn_weight, L0_conv_gcn_bias, L0_conv_gcn_qw, L0_conv_gcn_qb, L0_conv_gcn_kw, L0_conv_gcn_kb, L0_conv_gcn_vw, L0_conv_gcn_vb, L0_conv_qw, L0_conv_qb, L0_conv_kw, L0_conv_kb, L0_conv_vw, L0_conv_vb, L1_conv_W_in, L1_conv_W_conv, L1_conv_b_conv, L1_conv_W_xproj, L1_conv_W_dt, L1_conv_b_dt, L1_conv_A_log, L1_conv_D_param, L1_conv_W_out, L1_conv_gamma, L1_conv_beta, L2_conv_t_norm_w, L2_conv_t_Win, L2_conv_t_Wconv, L2_conv_t_bconv, L2_conv_t_dt_bias, L2_conv_t_A_log, L2_conv_t_D, L2_conv_t_gn_w, L2_conv_t_Wout, L2_conv_b_norm_w, L2_conv_b_Win, L2_conv_b_Wconv, L2_conv_b_bconv, L2_conv_b_dt_bias, L2_conv_b_A_log, L2_conv_b_D, L2_conv_b_gn_w, L2_conv_b_Wout, L3_conv_t_norm_w, L3_conv_t_Win, L3_conv_t_Wconv, L3_conv_t_bconv, L3_conv_t_dt_bias, L3_conv_t_A_log, L3_conv_t_D, L3_conv_t_gn_w, L3_conv_t_Wout, L3_conv_b_norm_w, L3_conv_b_Win, L3_conv_b_Wconv, L3_conv_b_bconv, L3_conv_b_dt_bias, L3_conv_b_A_log, L3_conv_b_D, L3_conv_b_gn_w, L3_conv_b_Wout):
    import jax
    import jax.numpy as jnp

    def _L0_conv_ref(x, se_groups, gcn_weight, gcn_bias, gcn_qw, gcn_qb, gcn_kw, gcn_kb, gcn_vw, gcn_vb, qw, qb, kw, kb, vw, vb):
        import jax, jax.numpy as jnp
        import numpy as np
        B, C, H, W = (4, 64, 64, 64)
        SG = 8
        PN = H // 4 * (W // 4)

        def _conv1d(w, b, x):
            return jnp.einsum('oi,bil->bol', w, x) + b[:, None]

        def _bilinear_align_corners(x, oh, ow):
            b, c, ih, iw = x.shape
            ys = jnp.linspace(0.0, ih - 1.0, oh)
            xs = jnp.linspace(0.0, iw - 1.0, ow)
            y0 = jnp.floor(ys).astype(jnp.int32)
            y1 = jnp.minimum(y0 + 1, ih - 1)
            wy = ys - y0.astype(x.dtype)
            x0 = jnp.floor(xs).astype(jnp.int32)
            x1 = jnp.minimum(x0 + 1, iw - 1)
            wx = xs - x0.astype(x.dtype)
            r0 = jnp.take(x, y0, axis=2)
            r1 = jnp.take(x, y1, axis=2)
            rows = r0 + (r1 - r0) * wy[None, None, :, None]
            c0 = jnp.take(rows, x0, axis=3)
            c1 = jnp.take(rows, x1, axis=3)
            return c0 + (c1 - c0) * wx[None, None, None, :]
        b, c, h, w = x.shape
        h4, w4 = (h // 4, w // 4)
        pn = h4 * w4
        xp = x.reshape(b, c, h4, 4, w4, 4).mean(axis=(3, 5))
        length = c // se_groups
        xpre = xp.reshape(b, se_groups, length, pn).mean(axis=2)
        xt = jnp.swapaxes(xpre, 1, 2)
        q = _conv1d(gcn_qw, gcn_qb, xt)
        k = _conv1d(gcn_kw, gcn_kb, xt)
        adj = jax.nn.softmax(jnp.einsum('bds,bdt->bst', k, q), axis=-1)
        v = _conv1d(gcn_vw, gcn_vb, xt)
        support = jnp.einsum('bps,po->bso', v, gcn_weight)
        gcn_out = jnp.einsum('bst,bto->bso', adj, support) + gcn_bias
        xpos = jnp.swapaxes(gcn_out, 1, 2)
        query = _conv1d(qw, qb, xpos)
        xflat = xp.reshape(b, c, pn)
        keyT = jnp.einsum('op,bcp->bco', kw, xflat) + kb
        atten = jax.nn.softmax(jnp.einsum('bcd,bds->bcs', keyT, query), axis=-1)
        valueT = jnp.swapaxes(_conv1d(vw, vb, xpos), 1, 2)
        y = jnp.einsum('bcs,bsp->bcp', atten, valueT)
        y = jnp.swapaxes(y, 1, 2).reshape(b, c, h4, w4)
        return _bilinear_align_corners(y, h, w)

    def _L1_conv_ref(x, W_in, W_conv, b_conv, W_xproj, W_dt, b_dt, A_log, D_param, W_out, gamma, beta):
        import jax, jax.numpy as jnp
        import numpy as np
        from jax import lax
        D_MODEL = 64
        D_STATE = 16
        D_CONV = 4
        EXPAND = 2
        D_INNER = EXPAND * D_MODEL
        DT_RANK = (D_MODEL + 15) // 16
        B, T, N = (2, 32, 16)
        LN_EPS = 1e-05

        def _mamba_block(xr, W_in, W_conv, b_conv, W_xproj, W_dt, b_dt, A_log, D_param, W_out):
            xz = xr @ W_in.T
            xp, z = jnp.split(xz, 2, axis=-1)
            xc = lax.conv_general_dilated(xp.transpose(0, 2, 1), W_conv, (1,), [(D_CONV - 1, 0)], dimension_numbers=('NCH', 'OIH', 'NCH'), feature_group_count=D_INNER)
            u = jax.nn.silu(xc + b_conv[None, :, None]).transpose(0, 2, 1)
            x_dbl = u @ W_xproj.T
            dt_raw = x_dbl[..., :DT_RANK]
            Bm = x_dbl[..., DT_RANK:DT_RANK + D_STATE]
            Cm = x_dbl[..., DT_RANK + D_STATE:]
            dt = jax.nn.softplus(dt_raw @ W_dt.T + b_dt)
            A = -jnp.exp(A_log)

            def step(h, inps):
                dt_t, B_t, C_t, u_t = inps
                dA = jnp.exp(dt_t[..., None] * A)
                h = h * dA + dt_t[..., None] * B_t[:, None, :] * u_t[..., None]
                y = jnp.einsum('bds,bs->bd', h, C_t)
                return (h, y)
            BN = xr.shape[0]
            h0 = jnp.zeros((BN, D_INNER, D_STATE), xr.dtype)
            xs = (dt.transpose(1, 0, 2), Bm.transpose(1, 0, 2), Cm.transpose(1, 0, 2), u.transpose(1, 0, 2))
            _, ys = lax.scan(step, h0, xs)
            y = ys.transpose(1, 0, 2) + u * D_param
            y = y * jax.nn.silu(z)
            return y @ W_out.T
        B_, T_, N_, Dm = x.shape
        xr = x.transpose(0, 2, 1, 3).reshape(B_ * N_, T_, Dm)
        out = _mamba_block(xr, W_in, W_conv, b_conv, W_xproj, W_dt, b_dt, A_log, D_param, W_out)
        mu = out.mean(-1, keepdims=True)
        var = out.var(-1, keepdims=True)
        out = (out - mu) / jnp.sqrt(var + LN_EPS) * gamma + beta
        return out.reshape(B_, N_, T_, Dm).transpose(0, 2, 1, 3)

    def _L2_conv_ref(x, t_norm_w, t_Win, t_Wconv, t_bconv, t_dt_bias, t_A_log, t_D, t_gn_w, t_Wout, b_norm_w, b_Win, b_Wconv, b_bconv, b_dt_bias, b_A_log, b_D, b_gn_w, b_Wout):
        import jax, jax.numpy as jnp
        import numpy as np
        HID, NL, DSTATE, DCONV, EXPAND = (64, 2, 16, 4, 2)
        DIN = EXPAND * HID
        NHEADS = DIN // 16
        HEADP = DIN // NHEADS
        CONVDIM = DIN + 2 * DSTATE
        PROJDIM = 2 * DIN + 2 * DSTATE + NHEADS
        B, T, NB = (2, 48, 62)

        def _rmsnorm(x, w, eps=1e-06):
            return x * jax.lax.rsqrt(jnp.mean(x * x, -1, keepdims=True) + eps) * w

        def _causal_conv(x, w, b):
            K = w.shape[1]
            L = x.shape[1]
            xp = jnp.pad(x, ((0, 0), (K - 1, 0), (0, 0)))
            y = b
            for k in range(K):
                y = y + xp[:, k:k + L, :] * w[:, k]
            return y

        def _ssd(xh, dt, A, Bm, Cm):
            cum = jnp.cumsum(dt * A, axis=1)
            diff = cum[:, :, None, :] - cum[:, None, :, :]
            mask = jnp.tril(jnp.ones((xh.shape[1], xh.shape[1]), bool))
            decay = jnp.where(mask[None, :, :, None], jnp.exp(diff), 0.0)
            scores = jnp.einsum('bln,bsn->bls', Cm, Bm)[..., None] * decay * dt[:, None, :, :]
            return jnp.einsum('blsh,bshp->blhp', scores, xh)

        def _mamba2(x, Win, Wconv, bconv, dt_bias, A_log, D, gn_w, Wout):
            b, l, _ = x.shape
            zxbcdt = x @ Win
            z = zxbcdt[..., :DIN]
            xBC = jax.nn.silu(_causal_conv(zxbcdt[..., DIN:DIN + CONVDIM], Wconv, bconv))
            xh = xBC[..., :DIN].reshape(b, l, NHEADS, HEADP)
            Bm = xBC[..., DIN:DIN + DSTATE]
            Cm = xBC[..., DIN + DSTATE:]
            dt = jax.nn.softplus(zxbcdt[..., -NHEADS:] + dt_bias)
            A = -jnp.exp(A_log)
            rev = lambda t: t[:, ::-1]
            y = _ssd(xh, dt, A, Bm, Cm) + rev(_ssd(rev(xh), rev(dt), A, rev(Bm), rev(Cm)))
            y = y + D[None, None, :, None] * xh
            y = _rmsnorm(y.reshape(b, l, DIN) * jax.nn.silu(z), gn_w)
            return y @ Wout

        def _forward(x, tp, bp):
            batch, T_, NB_, H_ = x.shape
            for i in range(NL):
                xt = jnp.transpose(x, (0, 2, 1, 3)).reshape(batch * NB_, T_, H_)
                xt = xt + _mamba2(_rmsnorm(xt, tp[0][i]), *(p[i] for p in tp[1:]))
                x = jnp.transpose(xt.reshape(batch, NB_, T_, H_), (0, 2, 1, 3))
                xb = x.reshape(batch * T_, NB_, H_)
                xb = xb + _mamba2(_rmsnorm(xb, bp[0][i]), *(p[i] for p in bp[1:]))
                x = xb.reshape(batch, T_, NB_, H_)
            return x
        tp = (t_norm_w, t_Win, t_Wconv, t_bconv, t_dt_bias, t_A_log, t_D, t_gn_w, t_Wout)
        bp = (b_norm_w, b_Win, b_Wconv, b_bconv, b_dt_bias, b_A_log, b_D, b_gn_w, b_Wout)
        return _forward(x, tp, bp)

    def _L3_conv_ref(x, t_norm_w, t_Win, t_Wconv, t_bconv, t_dt_bias, t_A_log, t_D, t_gn_w, t_Wout, b_norm_w, b_Win, b_Wconv, b_bconv, b_dt_bias, b_A_log, b_D, b_gn_w, b_Wout):
        import jax, jax.numpy as jnp
        import numpy as np
        HID, NL, DSTATE, DCONV, EXPAND = (64, 2, 16, 4, 2)
        DIN = EXPAND * HID
        NHEADS = DIN // 16
        HEADP = DIN // NHEADS
        CONVDIM = DIN + 2 * DSTATE
        PROJDIM = 2 * DIN + 2 * DSTATE + NHEADS
        B, T, NB = (2, 48, 62)

        def _rmsnorm(x, w, eps=1e-06):
            return x * jax.lax.rsqrt(jnp.mean(x * x, -1, keepdims=True) + eps) * w

        def _causal_conv(x, w, b):
            K = w.shape[1]
            L = x.shape[1]
            xp = jnp.pad(x, ((0, 0), (K - 1, 0), (0, 0)))
            y = b
            for k in range(K):
                y = y + xp[:, k:k + L, :] * w[:, k]
            return y

        def _ssd(xh, dt, A, Bm, Cm):
            cum = jnp.cumsum(dt * A, axis=1)
            diff = cum[:, :, None, :] - cum[:, None, :, :]
            mask = jnp.tril(jnp.ones((xh.shape[1], xh.shape[1]), bool))
            decay = jnp.where(mask[None, :, :, None], jnp.exp(diff), 0.0)
            scores = jnp.einsum('bln,bsn->bls', Cm, Bm)[..., None] * decay * dt[:, None, :, :]
            return jnp.einsum('blsh,bshp->blhp', scores, xh)

        def _mamba2(x, Win, Wconv, bconv, dt_bias, A_log, D, gn_w, Wout):
            b, l, _ = x.shape
            zxbcdt = x @ Win
            z = zxbcdt[..., :DIN]
            xBC = jax.nn.silu(_causal_conv(zxbcdt[..., DIN:DIN + CONVDIM], Wconv, bconv))
            xh = xBC[..., :DIN].reshape(b, l, NHEADS, HEADP)
            Bm = xBC[..., DIN:DIN + DSTATE]
            Cm = xBC[..., DIN + DSTATE:]
            dt = jax.nn.softplus(zxbcdt[..., -NHEADS:] + dt_bias)
            A = -jnp.exp(A_log)
            rev = lambda t: t[:, ::-1]
            y = _ssd(xh, dt, A, Bm, Cm) + rev(_ssd(rev(xh), rev(dt), A, rev(Bm), rev(Cm)))
            y = y + D[None, None, :, None] * xh
            y = _rmsnorm(y.reshape(b, l, DIN) * jax.nn.silu(z), gn_w)
            return y @ Wout

        def _forward(x, tp, bp):
            batch, T_, NB_, H_ = x.shape
            for i in range(NL):
                xt = jnp.transpose(x, (0, 2, 1, 3)).reshape(batch * NB_, T_, H_)
                xt = xt + _mamba2(_rmsnorm(xt, tp[0][i]), *(p[i] for p in tp[1:]))
                x = jnp.transpose(xt.reshape(batch, NB_, T_, H_), (0, 2, 1, 3))
                xb = x.reshape(batch * T_, NB_, H_)
                xb = xb + _mamba2(_rmsnorm(xb, bp[0][i]), *(p[i] for p in bp[1:]))
                x = xb.reshape(batch, T_, NB_, H_)
            return x
        tp = (t_norm_w, t_Win, t_Wconv, t_bconv, t_dt_bias, t_A_log, t_D, t_gn_w, t_Wout)
        bp = (b_norm_w, b_Win, b_Wconv, b_bconv, b_dt_bias, b_A_log, b_D, b_gn_w, b_Wout)
        return _forward(x, tp, bp)

    def _gn(v, G=32, eps=1e-05):
        B_, H_, W_, C_ = v.shape
        g = v.reshape(B_, H_, W_, G, C_ // G)
        m = jnp.mean(g, axis=(1, 2, 4), keepdims=True)
        s = jnp.var(g, axis=(1, 2, 4), keepdims=True)
        return ((g - m) / jnp.sqrt(s + eps)).reshape(v.shape)

    def _ln_c(v, eps=1e-06):
        m = jnp.mean(v, axis=-1, keepdims=True)
        s = jnp.var(v, axis=-1, keepdims=True)
        return (v - m) / jnp.sqrt(s + eps)

    def _ln_t(v, eps=1e-05):
        m = jnp.mean(v, axis=-1, keepdims=True)
        s = jnp.var(v, axis=-1, keepdims=True)
        return (v - m) / jnp.sqrt(s + eps)

    def _to_tokens(v):
        B_, H_, W_, C_ = v.shape
        return v.reshape(B_, H_ * W_, C_)

    def _from_tokens(t, like):
        return t.reshape(like.shape)
    x = x + _L0_conv_ref(_gn(x), 8, L0_conv_gcn_weight, L0_conv_gcn_bias, L0_conv_gcn_qw, L0_conv_gcn_qb, L0_conv_gcn_kw, L0_conv_gcn_kb, L0_conv_gcn_vw, L0_conv_gcn_vb, L0_conv_qw, L0_conv_qb, L0_conv_kw, L0_conv_kb, L0_conv_vw, L0_conv_vb)
    x = x + _L1_conv_ref(_gn(x), L1_conv_W_in, L1_conv_W_conv, L1_conv_b_conv, L1_conv_W_xproj, L1_conv_W_dt, L1_conv_b_dt, L1_conv_A_log, L1_conv_D_param, L1_conv_W_out, L1_conv_gamma, L1_conv_beta)
    x = x + _L2_conv_ref(_gn(x), L2_conv_t_norm_w, L2_conv_t_Win, L2_conv_t_Wconv, L2_conv_t_bconv, L2_conv_t_dt_bias, L2_conv_t_A_log, L2_conv_t_D, L2_conv_t_gn_w, L2_conv_t_Wout, L2_conv_b_norm_w, L2_conv_b_Win, L2_conv_b_Wconv, L2_conv_b_bconv, L2_conv_b_dt_bias, L2_conv_b_A_log, L2_conv_b_D, L2_conv_b_gn_w, L2_conv_b_Wout)
    x = x + _L3_conv_ref(_gn(x), L3_conv_t_norm_w, L3_conv_t_Win, L3_conv_t_Wconv, L3_conv_t_bconv, L3_conv_t_dt_bias, L3_conv_t_A_log, L3_conv_t_D, L3_conv_t_gn_w, L3_conv_t_Wout, L3_conv_b_norm_w, L3_conv_b_Win, L3_conv_b_Wconv, L3_conv_b_bconv, L3_conv_b_dt_bias, L3_conv_b_A_log, L3_conv_b_D, L3_conv_b_gn_w, L3_conv_b_Wout)
    return x

_drawn_inputs = setup_inputs


def setup_inputs(seed=0):
    import zlib

    import numpy as np

    out = dict(_drawn_inputs(seed))
    spreads = {'L1_conv_b_conv': (0.0, 0.1),
     'L1_conv_D_param': (1.0, 0.2),
     'L1_conv_gamma': (1.0, 0.2),
     'L1_conv_beta': (0.0, 0.1),
     'L2_conv_t_norm_w': (1.0, 0.2),
     'L2_conv_t_bconv': (0.0, 0.1),
     'L2_conv_t_D': (1.0, 0.2),
     'L2_conv_t_gn_w': (1.0, 0.2),
     'L2_conv_b_norm_w': (1.0, 0.2),
     'L2_conv_b_bconv': (0.0, 0.1),
     'L2_conv_b_D': (1.0, 0.2),
     'L2_conv_b_gn_w': (1.0, 0.2),
     'L3_conv_t_norm_w': (1.0, 0.2),
     'L3_conv_t_bconv': (0.0, 0.1),
     'L3_conv_t_D': (1.0, 0.2),
     'L3_conv_t_gn_w': (1.0, 0.2),
     'L3_conv_b_norm_w': (1.0, 0.2),
     'L3_conv_b_bconv': (0.0, 0.1),
     'L3_conv_b_D': (1.0, 0.2),
     'L3_conv_b_gn_w': (1.0, 0.2)}
    factors = {'L0_conv_gcn_weight': 8.0,
     'L0_conv_gcn_bias': 3.68,
     'L0_conv_gcn_qw': 8.0,
     'L0_conv_gcn_qb': 64.0,
     'L0_conv_gcn_kw': 8.0,
     'L0_conv_gcn_kb': 8.0,
     'L0_conv_gcn_vw': 8.0,
     'L0_conv_gcn_vb': 8.0,
     'L0_conv_qw': 8.0,
     'L0_conv_qb': 64.0,
     'L0_conv_kw': 8.0,
     'L0_conv_kb': 30.442,
     'L0_conv_vw': 4.079,
     'L1_conv_W_xproj': 39.192,
     'L1_conv_W_dt': 64.0,
     'L1_conv_b_dt': 64.0,
     'L1_conv_A_log': 64.0}
    for name, (base, spread) in spreads.items():
        noise = np.random.default_rng([zlib.crc32(name.encode()), seed]).standard_normal(out[name].shape)
        drawn = base * np.exp(spread * noise) if base else spread * noise
        out[name] = jnp.asarray(drawn.astype(out[name].dtype))
    for name, factor in factors.items():
        out[name] = (out[name] * factor).astype(out[name].dtype)
    return out
```

```python
from contextlib import ExitStack

import concourse.bass as bass
from concourse import mybir

F32 = mybir.dt.float32
ALU = mybir.AluOpType
ACT = mybir.ActivationFunctionType
AX = mybir.AxisListType

NB, L, CH = 2, 64, 64
P = NB * CH
TOK = L * L
BANK = 512
NCHUNK = TOK // BANK
NH, HP, NS = 8, 16, 16
PADL = L + 3
S1 = 16
J1 = 4
NK1 = L // J1
SEQ1 = NB * J1
LOG1P = (2.00000000788, 0.666663159351, 0.400248537234, 0.279614188352, 0.281746572615)

CONST_COLS = [("ident", 128), ("mean64", 128), ("pair", 128), ("later", 128), ("earlier", 128), ("ssum", 128),
              ("upto", 64), ("from_", 64), ("diag2", 64), ("stack", 64), ("seldt", 24), ("maskdt", 8), ("maskb", 16),
              ("mask16", 16), ("maskbc", 16), ("ones", 128), ("eps6", 1), ("eps6x4", 1), ("eps5", 1),
              ("interp", 512), ("wy", 64)]
CALL_COLS = [("wx", 128), ("cxa", 128), ("cxb", 128), ("wbc0", 128), ("wbc1", 128), ("cbca", 128), ("cbcb", 128),
             ("bx", 128), ("bbc", 128), ("wz0", 128), ("wz1", 128), ("wdt", 32), ("bdt", 1), ("alog", 8), ("dh", 8),
             ("nw", 1), ("gnw", 2), ("wo0", 128), ("wo1", 128)]
L0_COLS = [("gq", 128), ("gk", 128), ("gv", 512), ("gw", 512), ("gb", 2), ("gqb", 1), ("gkb", 1), ("gvb", 2),
           ("q", 128), ("qb", 1), ("k", 128), ("kb", 1), ("v", 512), ("vb", 256)]
L1_COLS = [("winx_a", 128), ("winx_b", 128), ("wca", 128), ("wcb", 128), ("wz", 128), ("wxp", 80), ("wdt", 128), ("bconv", 1),
           ("bdt", 1), ("alog", 16), ("dp", 1), ("wout", 64), ("gamma", 1), ("beta", 1)]


def width(cols):
    return sum(n for _, n in cols)


def spans(cols):
    at, out = 0, {}
    for name, n in cols:
        out[name] = (at, at + n)
        at += n
    return out


def program(nc, x, consts, pool_sel, state_sel, l0w, l1w, callw, out):
    ctx = ExitStack()
    with ctx:
        sems = {}

        def sb(name, cols):
            return ctx.enter_context(nc.sbuf_tensor(name, [128, cols], F32))[:, :]

        def sg(name):
            if name not in sems:
                sems[name] = ctx.enter_context(nc.semaphore(name))
            return sems[name]

        class Order:

            def __init__(self, eng, name, base=0):
                self.eng, self.name, self.base, self.n = eng, name, base, 0

            def __call__(self, ins):
                self.n += 1
                ins.then_inc(sg(self.name), 1)
                self.eng.wait_ge(sg(self.name), self.base + self.n)

        bank = [ctx.enter_context(nc.psum_tensor(f"bank{i}", [128, BANK], F32))[:, :] for i in range(8)]

        X = sb("X", TOK)
        Y = sb("Y", TOK)
        XN = sb("XN", TOK)
        Z2 = sb("Z2", 2 * TOK)
        O = sb("O", TOK)
        SS = sb("SS", TOK)
        SQ = sb("SQ", TOK)
        cst = sb("cst", width(CONST_COLS))
        raws = [sb(f"raw{i}", width(CALL_COLS)) for i in range(2)]
        FW = sb("folded_weights", 1312)
        small = sb("small", 64)
        ring4 = sb("ring4", 4 * 512)
        work = sb("work", 6400)
        Cs, Ws, W0s, W1s = spans(CONST_COLS), spans(CALL_COLS), spans(L0_COLS), spans(L1_COLS)

        def C(name, parts=128):
            a, b = Cs[name]
            return cst[0:parts, a:b]

        ident = C("ident")
        X3, XN3, O3, SS3 = (t.rearrange("p (i j) -> p i j", j=L) for t in (X, XN, O, SS))
        Z24 = Z2.rearrange("p (h i j) -> p h i j", h=2, j=L)

        def axis(t3, direction, q, n=1):
            return t3[:, :, bass.ds(q, n)] if direction == 0 else t3[:, bass.ds(q, n), :]

        taken = [0]

        def part(cols):
            taken[0] += cols
            assert taken[0] <= 6400
            return work[:, taken[0] - cols:taken[0]]

        SA = [part(NB * L) for _ in range(2)]
        SB = [part(NB * L) for _ in range(2)]
        DTB = [part(128) for _ in range(2)]
        TX = [part(192) for _ in range(2)]
        X2 = [part(128) for _ in range(2)]
        BB = [part(128) for _ in range(2)]
        C2 = [part(64) for _ in range(2)]
        DA = [part(24) for _ in range(2)]
        AM1 = [part(512) for _ in range(2)]
        AM2 = [part(512) for _ in range(2)]
        GM = [part(64) for _ in range(2)]
        YZ = [part(128) for _ in range(2)]
        YQ = [part(128) for _ in range(2)]
        DK = [part(512) for _ in range(2)]
        MM = [ring4[:, 0:0] for _ in range(0)]
        XB = [ring4[:, 512 * r:512 * r + 256] for r in range(4)]
        XD = [ring4[:, 512 * r + 256:512 * r + 512] for r in range(4)]
        MM = [sb(f"scores_times_decays{i}", 512) for i in range(2)]
        DT = sb("DT", 1024)
        dtw = [SS[:, 1024 * i:1024 * i + 1024] for i in range(3)]
        tz = [SQ[:, 512 * i:512 * i + 512] for i in range(2)]

        wxa, wxb = FW[:, 0:128], FW[:, 128:256]
        wbc = [[FW[:, 256 + 256 * t + 128 * b:384 + 256 * t + 128 * b] for b in range(2)] for t in range(2)]
        wog = [FW[:, 768 + 128 * h:896 + 128 * h] for h in range(2)]
        expA, dhalf = FW[:, 1024:1032], FW[:, 1296:1312]
        bxr, bbcr = FW[0:1, 1040:1168], FW[0:1, 1168:1296]

        w0, w1 = Y[:, 0:width(L0_COLS)], Y[:, 2320:2320 + width(L1_COLS)]
        assert width(L0_COLS) <= 2320 and 2320 + width(L1_COLS) <= TOK
        poolS, stateS = Z2[:, 0:2048], Z2[:, 2048:2048 + 4096]

        def W0(name, parts=128):
            a, b = W0s[name]
            return w0[0:parts, a:b]

        def W1(name, parts=128):
            a, b = W1s[name]
            return w1[0:parts, a:b]

        x_tok = x.rearrange("b i j c -> b (i j) c")
        out_tok = out.rearrange("b i j c -> b (i j) c")
        Otok = O.rearrange("p (t b c) -> p t b c", b=2, c=64)
        ctx.enter_context(nc.allow_non_contiguous_dma("token-major rows of 64 channels"))
        block = ctx.enter_context(nc.Block())

        def rounds(eng, mod_pre, call, mod_post):
            with eng.Fori(0, 2) as m:
                mod_pre(m)
                with eng.Fori(0, 2) as n:
                    for d in range(2):
                        call(m, n, d, eng.snap(m * 4 + n * 2 + d))
                mod_post(m)

        def tiles(eng, c, first, last, step, lead=0):
            T0 = eng.snap(c * L)
            for tau in range(first, 4 - lead):
                step(tau, T0, tau)
            with eng.Fori(0, 15) as it:
                q0 = eng.snap(it * 4)
                T = eng.snap(T0 + q0)
                for u in range(4):
                    step(u + 4 - lead, T, None, q0)
            for tau in range(L - lead, last):
                step(tau, T0, tau)

        def part_of(known, offset):
            return known is None or 0 <= known + offset < L

        def later(known, offset, k):
            return known is None or known + offset >= k

        def y_value(m, n, d):
            return m * 5 + n * 2 + d + 1

        @block.sync
        def _(sp):
            sp.dma_start(cst, consts).then_inc(sg("constants_loaded"), 16)
            for b in range(NB):
                sp.dma_start(Otok[:, :, b, :], x_tok[b].rearrange("(t p) c -> p t c", p=128)).then_inc(
                    sg("x_loaded"), 16)
            sp.dma_start(w0, l0w).then_inc(sg("stage0_weights_loaded"), 16)
            sp.dma_start(poolS, pool_sel).then_inc(sg("stage0_weights_loaded"), 16)
            sp.dma_start(w1, l1w).then_inc(sg("stage1_weights_loaded"), 16)
            sp.dma_start(stateS, state_sel).then_inc(sg("stage1_weights_loaded"), 16)
            for d in range(2):
                sp.dma_start(raws[d], callw[d]).then_inc(sg(f"block_weights_loaded{d}"), 16)

            def call(m, n, d, c):
                nxt = sp.snap(m * 4 + n * 2 + 2) if False else None
                return None

            with sp.Fori(0, 3) as r:
                for d in range(2):
                    sp.wait_ge(sg(f"block_done{d}"), r + 1)
                    sp.dma_start(raws[d], callw[bass.ds(r * 2 + d + 2, 1)].rearrange("a p n -> p (a n)")).then_inc(
                        sg(f"block_weights_loaded{d}"), 16)
            for b in range(NB):
                sp.wait_ge(sg("out_turned"), 8)
                sp.dma_start(out_tok[b].rearrange("(t p) c -> p t c", p=128), Otok[:, :, b, :]).then_inc(
                    sg("output_stored"), 16)
            sp.wait_ge(sg("output_stored"), 32)

        PE0 = ["xp", "qk", "adj", "adjT", "v", "support", "xpos", "query", "key", "at", "atT", "val", "y", "z"]
        DVE0 = ["xj", "xp", "xpre", "qk", "adj", "neg", "e1", "adjT", "v", "support", "xpos", "query", "key", "at",
                "neg2", "e2", "atT", "val", "y", "z"]
        ACT0 = ["exp", "exp2"]

        @block.tensor
        def _(pe):
            mm, tr = nc.tensor.matmul, nc.tensor.transpose

            def groupnorm(g):
                pe.wait_ge(sg("gn_sum"), g + 1)
                mm(bank[7][:, 0:1], C("pair"), small[:, 0:1], start=True, stop=True).then_inc(sg("gn_mean"), 1)
                pe.wait_ge(sg("gn_square"), g + 1)
                mm(bank[7][:, 8:9], C("pair"), small[:, 2:3], start=True, stop=True).then_inc(sg("gn_var"), 1)

            def turn_in():
                pe.wait_ge(sg("constants_loaded"), 16)
                pe.wait_ge(sg("x_loaded"), 32)
                for k in range(8):
                    for t in range(4):
                        a = BANK * k + 128 * t
                        last = tr(bank[k][:, 128 * t:128 * t + 128], O[:, a:a + 128], ident)
                    last.then_inc(sg("in_turned"), 1)

            def turn_out():
                pe.wait_ge(sg("x_final"), 1)
                for k in range(8):
                    for t in range(4):
                        a = BANK * k + 128 * t
                        last = tr(bank[k][:, 128 * t:128 * t + 128], X[:, a:a + 128], ident)
                    last.then_inc(sg("out_in_psum"), 1)

            def stage0():
                def need(name):
                    pe.wait_ge(sg("stage0_dve"), DVE0.index(name) + 1)

                def done(ins):
                    ins.then_inc(sg("stage0_pe"), 1)
                pe.wait_ge(sg("stage0_weights_loaded"), 32)
                need("xj")
                Xj = SQ[:, 0:1024].rearrange("p (i j) -> p i j", j=16)
                for hf in range(2):
                    for b in range(NB):
                        for jj in range(8):
                            r = b * 8 + jj
                            last = mm(bank[0][:, 128 * hf + 64 * b:128 * hf + 64 * b + 64],
                                      poolS[:, 128 * r:128 * r + 128], Xj[:, :, hf * 8 + jj],
                                      start=(jj == 0), stop=(jj == 7))
                done(last)
                xpT, xpre = SQ[:, 1024:1280], SQ[:, 1280:1312]
                need("xpre")
                for w, o in (("gq", 0), ("gk", 16)):
                    for hf in range(2):
                        last = mm(bank[1][0:64, o:o + 16], W0(w)[:, 64 * hf:64 * hf + 64],
                                  xpre[:, 16 * hf:16 * hf + 16], start=(hf == 0), stop=(hf == 1))
                done(last)
                need("qk")
                q, k = SQ[0:64, 1312:1328], SQ[0:64, 1328:1344]
                done(mm(bank[2][0:16, 0:16], k, q, start=True, stop=True))
                need("e1")
                done(tr(bank[3][0:16, 0:16], SQ[0:16, 1344:1360], ident[0:16, 0:16]))
                for ho in range(2):
                    for hf in range(2):
                        last = mm(bank[4][:, 16 * ho:16 * ho + 16],
                                  W0("gv")[:, 256 * hf + 128 * ho:256 * hf + 128 * ho + 128],
                                  xpre[:, 16 * hf:16 * hf + 16], start=(hf == 0), stop=(hf == 1))
                done(last)
                need("v")
                v = SQ[:, 1392:1424]
                for hf in range(2):
                    last = mm(bank[5][0:16, 0:256], v[:, 16 * hf:16 * hf + 16],
                              W0("gw")[:, 256 * hf:256 * hf + 256], start=(hf == 0), stop=(hf == 1))
                done(last)
                need("support")
                for ho in range(2):
                    last = mm(bank[6][:, 16 * ho:16 * ho + 16], SQ[0:16, 1424 + 128 * ho:1552 + 128 * ho],
                              SQ[0:16, 1376:1392], start=True, stop=True)
                done(last)
                need("xpos")
                xpos = SQ[:, 1680:1712]
                for hf in range(2):
                    last = mm(bank[1][0:64, 0:16], W0("q")[:, 64 * hf:64 * hf + 64],
                              xpos[:, 16 * hf:16 * hf + 16], start=(hf == 0), stop=(hf == 1))
                done(last)
                for hf in range(2):
                    last = mm(bank[2][0:64, 0:128], W0("k")[:, 64 * hf:64 * hf + 64],
                              xpT[:, 128 * hf:128 * hf + 128], start=(hf == 0), stop=(hf == 1))
                done(last)
                need("key")
                done(mm(bank[3][:, 0:16], SQ[0:64, 1728:1856], SQ[0:64, 1712:1728], start=True, stop=True))
                need("e2")
                done(tr(bank[4][0:16, 0:128], SQ[:, 1856:1872], ident))
                for hf in range(2):
                    mm(bank[5][0:16, 0:256], xpos[:, 16 * hf:16 * hf + 16], W0("v")[:, 256 * hf:256 * hf + 256],
                       start=(hf == 0), stop=False)
                done(mm(bank[5][0:16, 0:256], C("ones", 1)[:, 0:16], W0("vb", 1), start=False, stop=True))
                need("val")
                done(mm(bank[6][:, 0:256], SQ[0:16, 1888:2016], SQ[0:16, 2016:2272], start=True, stop=True))
                need("y")
                for hlo in range(4):
                    last = mm(bank[hlo // 2][:, 256 * (hlo % 2):256 * (hlo % 2) + 256],
                              C("interp")[:, 128 * hlo:128 * hlo + 128], SQ[:, 2272:2528], start=True, stop=True)
                done(last)

            def stage1():
                pe.wait_ge(sg("stage1_weights_loaded"), 32)
                st = SQ[:, 0:SEQ1 * PADL].rearrange("p (s l) -> p s l", l=PADL)
                u, xd, yz = SQ[:, 2048:2560], SQ[0:80, 3072:3584], work[:, 1024:1536]
                with pe.Fori(0, NK1) as k:
                    pe.wait_ge(sg("s1_staged"), k + 1)
                    pe.wait_ge(sg("s1_u"), k)
                    pe.wait_ge(sg("s1_z"), k)
                    mm(bank[0], W1("winx_a"), st[:, :, 3:3 + L], start=True, stop=False)
                    mm(bank[0], W1("winx_b"), st[:, :, 1:1 + L], start=False, stop=True)
                    mm(bank[1], W1("wz"), st[:, :, 3:3 + L], start=True, stop=True).then_inc(sg("s1_front"), 1)
                    pe.wait_ge(sg("s1_u"), k + 1)
                    pe.wait_ge(sg("s1_stored"), k)
                    mm(bank[2][0:80, :], W1("wxp"), u, start=True, stop=True).then_inc(sg("s1_dbl"), 1)
                    pe.wait_ge(sg("s1_xd"), k + 1)
                    mm(bank[3], W1("wdt", 80), xd, start=True, stop=True).then_inc(sg("s1_dtp"), 1)
                    s0 = pe.snap(k * S1)
                    for s in range(S1):
                        pe.wait_ge(sg("s1_dbu"), s0 + (s - 1 if s >= 2 else 0))
                        mm(bank[4 + s % 2], stateS[0:80, 128 * s:128 * s + 128], xd, start=True,
                           stop=True).then_inc(sg("s1_B"), 1)
                        pe.wait_ge(sg("s1_hc"), s0 + (s - 1 if s >= 2 else 0))
                        mm(bank[6 + s % 2], stateS[0:80, 2048 + 128 * s:2176 + 128 * s], xd, start=True,
                           stop=True).then_inc(sg("s1_C"), 1)
                    pe.wait_ge(sg("s1_gated"), k + 1)
                    for b in range(NB):
                        last = mm(bank[2][64 * b:64 * b + 64, 0:256], W1("wout"), yz[:, 256 * b:256 * b + 256],
                                  start=True, stop=True)
                    last.then_inc(sg("s1_out"), 1)
                for ch in range(NCHUNK):
                    pe.wait_ge(sg("s1_stored"), NK1)
                    if ch >= 2:
                        pe.wait_ge(sg("ln_centred"), ch - 1)
                    mm(bank[6 + ch % 2], C("mean64"), O[:, BANK * ch:BANK * ch + BANK], start=True,
                       stop=True).then_inc(sg("ln_mean"), 1)
                pe.wait_ge(sg("ln_square"), 1)
                for ch in range(NCHUNK):
                    if ch >= 2:
                        pe.wait_ge(sg("ln_log"), ch - 1)
                    mm(bank[6 + ch % 2], C("mean64"), SQ[:, BANK * ch:BANK * ch + BANK], start=True,
                       stop=True).then_inc(sg("ln_var"), 1)

            def call(m, n, d, c):
                raw = raws[d]

                def W(name):
                    a, b = Ws[name]
                    return raw[:, a:b]
                pe.wait_ge(sg("squared"), c + 1)
                for ch in range(NCHUNK):
                    if ch >= 2:
                        pe.wait_ge(sg("norm_log"), c * 8 + ch - 1)
                    mm(bank[6 + ch % 2], C("mean64"), SQ[:, BANK * ch:BANK * ch + BANK], start=True,
                       stop=True).then_inc(sg("norm_ms"), 1)
                pe.wait_ge(sg(f"block_weights_loaded{d}"), (m * 2 + n) * 16 + 16)
                pe.wait_ge(sg("normed"), c + 1)
                for hq in range(2):
                    for g in range(4):
                        if d == 0:
                            cols = XN3[:, 16 * g:16 * g + 16, 32 * hq:32 * hq + 32].rearrange("p i j -> p j i")
                        else:
                            cols = XN3[:, 32 * hq:32 * hq + 32, 16 * g:16 * g + 16]
                        last = mm(bank[4 + hq][32 * g:32 * g + 32, :], W("wdt"), cols, start=True, stop=True,
                                  tile_position=(0, 32 * g))
                last.then_inc(sg("dt_psum"), 1)
                for ch in range(NCHUNK):
                    for hd in range(2):
                        i = 2 * ch + hd
                        if i >= 2:
                            pe.wait_ge(sg("z_ready"), c * 16 + i - 1)
                        mm(bank[6 + i % 2], W(f"wz{hd}"), XN[:, BANK * ch:BANK * ch + BANK], start=True,
                           stop=True).then_inc(sg("z_psum"), 1)
                pe.wait_ge(sg("folded"), c + 1)
                pe.wait_ge(sg("dt_added"), c + 1)

                def step(tau, T, known, q0=None):
                    if part_of(known, 0):
                        p = tau % 2
                        fx, fbc, fdt = bank[p][:, 0:128], bank[p][:, 128:192], bank[p][:, 192:216]
                        pe.wait_ge(sg("staged_straight"), T + (tau + 1))
                        pe.wait_ge(sg("staged_shifted"), T + (tau + 1))
                        if later(known, 0, 2):
                            pe.wait_ge(sg("x_ready"), T + (tau - 1))
                            pe.wait_ge(sg("bc_ready"), T + (tau - 1))
                            pe.wait_ge(sg("a_ready"), T + (tau - 1))
                            pe.wait_ge(sg("gm_ready"), T + (tau - 1))
                        mm(fx, SA[p], wxa, start=True, stop=False)
                        mm(fx, SB[p], wxb, start=False, stop=False)
                        mm(fx, C("ones", 1), bxr, start=False, stop=True)
                        for b in range(NB):
                            mm(fbc, wbc[0][b], SA[p][:, L * b:L * b + L], start=(b == 0), stop=False)
                            mm(fbc, wbc[1][b], SB[p][:, L * b:L * b + L], start=False, stop=False)
                        mm(fbc, bbcr, C("ones", 1)[:, 0:L], start=False, stop=True)
                        mm(fdt, DTB[p], C("seldt"), start=True, stop=True).then_inc(sg("projected"), 1)
                    if part_of(known, -1):
                        p = (tau - 1) % 2
                        pe.wait_ge(sg("bc_ready"), T + tau)
                        pe.wait_ge(sg("am1_ready"), T + tau)
                        pe.wait_ge(sg("am2_ready"), T + tau)
                        if later(known, -1, 2):
                            pe.wait_ge(sg("gm_ready"), T + (tau - 2))
                            pe.wait_ge(sg("decay_ready"), T + (tau - 2))
                        mm(bank[p][:, 256:320], BB[p][0:64, :], C2[p][0:64, :], start=True, stop=True)
                        mm(bank[2 + p], C("later"), AM1[p], start=True, stop=False)
                        mm(bank[2 + p], C("earlier"), AM2[p], start=False, stop=True).then_inc(sg("scored"), 1)
                    if part_of(known, -2):
                        p, r = (tau - 2) % 2, (tau - 2) % 4
                        y = bank[4 + p][:, 0:128]
                        pe.wait_ge(sg("xb_ready"), T + (tau - 1))
                        pe.wait_ge(sg("mixed"), T + (tau - 1))
                        if later(known, -2, 2):
                            pe.wait_ge(sg("tile_stored"), T + (tau - 3))
                        for hd in range(2):
                            mm(y[:, 64 * hd:64 * hd + 64], XD[r][:, 128 * hd:128 * hd + 128], C("stack"),
                               start=True, stop=False, skip_group_check=True)
                            for h4 in range(4):
                                h = 4 * hd + h4
                                last = mm(y[32 * h4:32 * h4 + 32, 64 * hd:64 * hd + 64],
                                          XB[r][:, 32 * h:32 * h + 32], MM[p][:, 64 * h:64 * h + 64],
                                          start=False, stop=True, tile_position=(0, 32 * h4),
                                          skip_group_check=True)
                        last.then_inc(sg("y_psum"), 1)
                    if part_of(known, -3):
                        p = (tau - 3) % 2
                        pe.wait_ge(sg("gated_squared"), T + (tau - 2))
                        if later(known, -3, 2):
                            pe.wait_ge(sg("tile_stored"), T + (tau - 4))
                        for hd in range(2):
                            mm(bank[4 + p][:, 128:192], wog[hd], YZ[p][:, 64 * hd:64 * hd + 64],
                               start=(hd == 0), stop=(hd == 1))
                        for hd in range(2):
                            last = mm(bank[4 + p][:, 192:256], C("ssum"), YQ[p][:, 64 * hd:64 * hd + 64],
                                      start=(hd == 0), stop=(hd == 1))
                        last.then_inc(sg("out_psum"), 1)

                tiles(pe, c, 0, L + 3, step)

            turn_in()
            groupnorm(0)
            stage0()
            groupnorm(1)
            stage1()
            rounds(pe, lambda m: groupnorm(m + 2), call, lambda m: None)
            turn_out()

        @block.scalar
        def _(act):
            A = nc.scalar.activation

            def groupnorm(g):
                act.wait_ge(sg("gn_centre"), g + 1)
                A(SQ, X, ACT.Square, bias=small[:, 1:2], accum_out=small[:, 2:3]).then_inc(sg("gn_square"), 1)
                act.wait_ge(sg("gn_var"), g + 1)
                A(small[:, 3:4], bank[7][:, 8:9], ACT.Ln, bias=C("eps5")).then_inc(sg("gn_log"), 1)
                act.wait_ge(sg("gn_log"), g + 1)
                A(small[:, 4:5], small[:, 3:4], ACT.Exp, scale=-0.5).then_inc(sg("gn_scale"), 1)

            def softplus_exp(prefix, v, w, base):
                act.wait_ge(sg(prefix + "_added"), base + 1)
                A(w, v, ACT.Abs).then_inc(sg(prefix + "_abs"), 1)
                act.wait_ge(sg(prefix + "_abs"), base + 1)
                A(w, w, ACT.Exp, scale=-1.0).then_inc(sg(prefix + "_exp"), 1)

            act.wait_ge(sg("constants_loaded"), 16)
            for k in range(1, 8, 2):
                act.wait_ge(sg("in_turned"), k + 1)
                A(X[:, BANK * k:BANK * k + BANK], bank[k], ACT.Copy).then_inc(sg("x_placed"), 1)
            groupnorm(0)
            act.wait_ge(sg("stage0_dve"), DVE0.index("neg") + 1)
            A(SQ[0:16, 1344:1360], SQ[0:16, 1344:1360], ACT.Exp, bias=small[0:16, 9:10],
              accum_out=small[0:16, 10:11]).then_inc(sg("stage0_act"), 1)
            act.wait_ge(sg("stage0_dve"), DVE0.index("neg2") + 1)
            A(SQ[:, 1856:1872], SQ[:, 1856:1872], ACT.Exp, bias=small[:, 13:14],
              accum_out=small[:, 14:15]).then_inc(sg("stage0_act"), 1)
            groupnorm(1)

            act.wait_ge(sg("stage1_weights_loaded"), 32)
            negA, hb = small[:, 32:48], small[:, 48:49]
            act.wait_ge(sg("s1_alog"), 1)
            A(negA, negA, ACT.Exp).then_inc(sg("s1_expA"), 1)
            act.wait_ge(sg("s1_consts"), 1)
            t, dt = SQ[:, 1536:2048], SQ[:, 3584:4096]
            w0_, w1_, w2_ = SS[:, 0:512], SS[:, 512:1024], SS[:, 1024:1536]
            dA = [SS[:, 2048 + 512 * i:2560 + 512 * i].rearrange("p (s l) -> p s l", l=L) for i in range(2)]
            with act.Fori(0, NK1) as k:
                act.wait_ge(sg("s1_front"), k + 1)
                A(t, bank[0], ACT.Tanh, bias=hb, scale=0.5).then_inc(sg("s1_tanh"), 1)
                A(w0_, bank[1], ACT.Tanh, scale=0.5).then_inc(sg("s1_tanhz"), 1)
                act.wait_ge(sg("s1_z"), k + 1)
                softplus_exp("s1dt", dt, w0_, k)
                act.wait_ge(sg("s1dt_ready"), k + 1)
                s0 = act.snap(k * S1)
                for s in range(S1):
                    if s >= 2:
                        act.wait_ge(sg("s1_h"), s0 + (s - 1))
                    A(dA[s % 2][:, :, 1:L], dt.rearrange("p (s l) -> p s l", l=L)[:, :, 1:L], ACT.Exp,
                      scale=negA[:, s:s + 1]).then_inc(sg("s1_dA"), 1)
                act.wait_ge(sg("s1_out"), k + 1)
                A(O3[:, :, bass.ds(k * J1, J1)].rearrange("p i j -> p j i"),
                  bank[2][:, 0:256].rearrange("p (j i) -> p j i", i=L), ACT.Copy).then_inc(sg("s1_stored"), 1)
            act.wait_ge(sg("ln_centred"), NCHUNK)
            A(SQ, O, ACT.Square).then_inc(sg("ln_square"), 1)
            for ch in range(NCHUNK):
                act.wait_ge(sg("ln_var"), ch + 1)
                A(SS[:, BANK * ch:BANK * ch + BANK], bank[6 + ch % 2], ACT.Ln, bias=C("eps5")).then_inc(
                    sg("ln_log"), 1)
            act.wait_ge(sg("ln_log"), NCHUNK)
            A(SS, SS, ACT.Exp, scale=-0.5).then_inc(sg("ln_scale"), 1)

            def call(m, n, d, c):
                raw = raws[d]
                act.wait_ge(sg(f"block_weights_loaded{d}"), (m * 2 + n) * 16 + 16)
                act.wait_ge(sg("y_ready"), y_value(m, n, d))
                a, b = Ws["alog"]
                A(expA, raw[:, a:b], ACT.Exp).then_inc(sg("expA_ready"), 1)
                A(SQ, Y, ACT.Square).then_inc(sg("squared"), 1)
                for ch in range(NCHUNK):
                    act.wait_ge(sg("norm_ms"), c * 8 + (ch + 1))
                    A(O[:, BANK * ch:BANK * ch + BANK], bank[6 + ch % 2], ACT.Ln, bias=C("eps6")).then_inc(
                        sg("norm_log"), 1)
                act.wait_ge(sg("norm_log"), c * 8 + 8)
                A(O, O, ACT.Exp, scale=-0.5).then_inc(sg("norm_scale"), 1)
                softplus_exp("dt", DT, dtw[0], c)
                for i in range(16):
                    act.wait_ge(sg("z_psum"), c * 16 + (i + 1))
                    if i >= 2:
                        act.wait_ge(sg("z_ready"), c * 16 + (i - 1))
                    A(tz[i % 2], bank[6 + i % 2], ACT.Tanh, scale=0.5).then_inc(sg("z_tanh"), 1)

                act.wait_ge(sg("normed"), c + 1)
                act.wait_ge(sg("zeroed"), 1)

                def stage(t, T, q, free):
                    if free:
                        act.wait_ge(sg("projected"), T + (t - 1))
                    s = SA[t % 2]
                    src = axis(XN3, d, q).rearrange("p i j -> p (i j)")
                    A(s[0:64, 0:L], src[0:64, :], ACT.Copy)
                    A(s[64:128, L + 1:2 * L], src[64:128, 0:L - 1], ACT.Copy).then_inc(sg("staged_own"), 1)

                def step(tau, T, known, q0=None):
                    if part_of(known, 1):
                        q = (q0 + (tau + 1)) if known is None else tau + 1
                        stage(tau + 1, T, q, later(known, 1, 2))
                    if part_of(known, 0):
                        p = tau % 2
                        act.wait_ge(sg("projected"), T + (tau + 1))
                        if later(known, 0, 2):
                            act.wait_ge(sg("x_ready"), T + (tau - 1))
                            act.wait_ge(sg("bc_ready"), T + (tau - 1))
                        A(TX[p], bank[p][:, 0:192], ACT.Tanh, scale=0.5).then_inc(sg("tanh_ready"), 1)
                    if part_of(known, -1):
                        p = (tau - 1) % 2
                        act.wait_ge(sg("scored"), T + tau)
                        if later(known, -1, 2):
                            act.wait_ge(sg("mixed"), T + (tau - 2))
                        A(DK[p], bank[2 + p], ACT.Exp).then_inc(sg("decay_ready"), 1)
                    if part_of(known, -2):
                        p = (tau - 2) % 2
                        act.wait_ge(sg("gated"), T + (tau - 1))
                        if later(known, -2, 2):
                            act.wait_ge(sg("out_psum"), T + (tau - 3))
                        A(YQ[p], YZ[p], ACT.Square).then_inc(sg("gated_squared"), 1)
                    if part_of(known, -3):
                        p = (tau - 3) % 2
                        q = (q0 + (tau - 3)) if known is None else tau - 3
                        act.wait_ge(sg("out_psum"), T + (tau - 2))
                        src = bank[4 + p][:, 128:256].rearrange("p (k l) -> p k l", k=2)
                        if d == 0:
                            A(O3[:, :, bass.ds(q, 1)], src[:, 0, :].unsqueeze(2), ACT.Copy)
                            A(SS3[:, :, bass.ds(q, 1)], src[:, 1, :].unsqueeze(2), ACT.Copy).then_inc(
                                sg("tile_stored"), 1)
                        else:
                            A(O3[:, bass.ds(q, 1), :], src[:, 0, :].unsqueeze(1), ACT.Copy)
                            A(SS3[:, bass.ds(q, 1), :], src[:, 1, :].unsqueeze(1), ACT.Copy).then_inc(
                                sg("tile_stored"), 1)

                tiles(act, c, -1, L + 3, step, lead=1)
                act.wait_ge(sg("tile_stored"), c * L + L)
                A(SS, SS, ACT.Ln, bias=C("eps6x4")).then_inc(sg("gate_log"), 1)
                act.wait_ge(sg("gate_log"), c + 1)
                A(SS, SS, ACT.Exp, scale=-0.5).then_inc(sg("gate_scale"), 1)

            rounds(act, lambda m: groupnorm(m + 2), call, lambda m: None)
            for k in range(1, 8, 2):
                act.wait_ge(sg("out_in_psum"), k + 1)
                A(O[:, BANK * k:BANK * k + BANK], bank[k], ACT.Copy).then_inc(sg("out_turned"), 1)

        @block.gpsimd
        def _(pool):
            g = nc.gpsimd
            pool.wait_ge(sg("constants_loaded"), 16)
            hc = [Y[:, 512 * i:512 * i + 512] for i in range(2)]
            acc = Y[:, 1024:1536]
            with pool.Fori(0, NK1) as k:
                s0 = pool.snap(k * S1)
                pool.wait_ge(sg("s1_gated"), k)
                for s in range(S1):
                    pool.wait_ge(sg("s1_hc"), s0 + (s + 1))
                    if s == 0:
                        g.tensor_tensor(acc, hc[0], C("ones")[:, 0:1].broadcast_to([128, 512]), ALU.mult).then_inc(sg("s1_acc"), 1)
                    else:
                        pool.wait_ge(sg("s1_acc"), s0 + s)
                        g.tensor_tensor(acc, acc, hc[s % 2], ALU.add).then_inc(sg("s1_acc"), 1)
            pool.wait_ge(sg("s1_out"), NK1)
            for t in SA + SB + BB:
                last = g.memset(t, 0.0)
            last.then_inc(sg("zeroed"), 1)
            pool.wait_ge(sg("zeroed"), 1)

            def call(m, n, d, c):
                pool.wait_ge(sg("normed"), c + 1)
                pool.wait_ge(sg("dt_ready"), c + 1)
                pool.wait_ge(sg("folded"), c + 1)

                def stage(t, T, q, free):
                    p = t % 2
                    if free:
                        pool.wait_ge(sg("projected"), T + (t - 1))
                    pool.wait_ge(sg("staged_own"), T + (t + 1))
                    pool.wait_ge(sg("staged_shifted"), T + (t + 1))
                    a, later_ = (x_[p].rearrange("p (b l) -> p b l", l=L) for x_ in (SA, SB))
                    g.tensor_tensor(later_[:, :, 2:L], a[:, :, 0:L - 2],
                                    C("ones")[:, 0:1].unsqueeze(2).broadcast_to([128, 2, L - 2]), ALU.mult)
                    dtq = DT.rearrange("p (q l) -> p q l", l=16)[:, bass.ds(q, 1), :]
                    g.tensor_tensor(DTB[p].rearrange("p (k l) -> p k l", l=16), dtq.broadcast_to([128, 8, 16]),
                                    C("maskdt").unsqueeze(2).broadcast_to([128, 8, 16]), ALU.mult).then_inc(
                        sg("staged_straight"), 1)

                def step(tau, T, known, q0=None):
                    if part_of(known, 1):
                        q = (q0 + (tau + 1)) if known is None else tau + 1
                        stage(tau + 1, T, q, later(known, 1, 2))
                    if part_of(known, 0):
                        p, r = tau % 2, tau % 4
                        pool.wait_ge(sg("a_ready"), T + (tau + 1))
                        if later(known, 0, 2):
                            pool.wait_ge(sg("scored"), T + (tau - 1))
                        g.tensor_tensor(AM2[p].rearrange("p (h l) -> p h l", l=L),
                                        DA[p][:, 0:8].unsqueeze(2).broadcast_to([128, 8, L]),
                                        C("from_").unsqueeze(1).broadcast_to([128, 8, L]), ALU.mult).then_inc(
                            sg("am2_ready"), 1)
                        pool.wait_ge(sg("x_ready"), T + (tau + 1))
                        if later(known, 0, 4):
                            pool.wait_ge(sg("y_psum"), T + (tau - 3))
                        x2 = X2[p].rearrange("p (h e) -> p h e", e=HP).unsqueeze(2).broadcast_to([128, 8, 2, HP])
                        for dst, by in ((XD[r], dhalf), (XB[r], DA[p][:, 8:24])):
                            last = g.tensor_tensor(
                                dst.rearrange("p (h b e) -> p h b e", b=2, e=HP), x2,
                                by.rearrange("p (h b) -> p h b", b=2).unsqueeze(3).broadcast_to([128, 8, 2, HP]),
                                ALU.mult)
                        last.then_inc(sg("xb_ready"), 1)

                tiles(pool, c, -1, L, step, lead=1)

            rounds(pool, lambda m: None, call, lambda m: None)

        @block.vector
        def _(dve):
            v = nc.vector
            for k in range(0, 8, 2):
                dve.wait_ge(sg("in_turned"), k + 1)
                v.tensor_copy(X[:, BANK * k:BANK * k + BANK], bank[k]).then_inc(sg("x_placed"), 1)
            dve.wait_ge(sg("x_placed"), 8)

            def groupnorm(g, dst, ready):
                v.tensor_reduce(small[:, 0:1], X, AX.X, ALU.add).then_inc(sg("gn_sum"), 1)
                dve.wait_ge(sg("gn_mean"), g + 1)
                v.tensor_scalar(small[:, 1:2], bank[7][:, 0:1], -1.0, None, ALU.mult).then_inc(sg("gn_centre"), 1)
                dve.wait_ge(sg("gn_scale"), g + 1)
                v.tensor_scalar(dst, X, small[:, 1:2], small[:, 4:5], ALU.add, ALU.mult).then_inc(sg(ready), 1)

            groupnorm(0, XN, "xn0")

            n0 = [0]

            def done(ins, name):
                assert DVE0[n0[0]] == name
                n0[0] += 1
                ins.then_inc(sg("stage0_dve"), 1)

            def pe_did(name):
                dve.wait_ge(sg("stage0_pe"), PE0.index(name) + 1)

            def did(name):
                dve.wait_ge(sg("stage0_dve"), DVE0.index(name) + 1)
            order = Order(dve, "stage0_order")
            dve.wait_ge(sg("xn0"), 1)
            done(v.tensor_reduce(SQ[:, 0:1024], XN.rearrange("p (n f) -> p n f", f=4), AX.X, ALU.add), "xj")
            pe_did("xp")
            dve.wait_ge(sg("stage0_weights_loaded"), 32)
            xpT, xpre = SQ[:, 1024:1280], SQ[:, 1280:1312]
            done(v.tensor_copy(xpT, bank[0][:, 0:256]), "xp")
            did("xp")
            order(v.tensor_reduce(xpre, xpT.rearrange("p (n f) -> p n f", f=8), AX.X, ALU.add))
            done(v.tensor_scalar(xpre, xpre, 0.125, None, ALU.mult), "xpre")
            pe_did("qk")
            v.tensor_scalar(SQ[0:64, 1312:1328], bank[1][0:64, 0:16], W0("gqb", 64), None, ALU.add)
            done(v.tensor_scalar(SQ[0:64, 1328:1344], bank[1][0:64, 16:32], W0("gkb", 64), None, ALU.add), "qk")

            def softmax(tile, src, mask, cols, names):
                parts = tile.shape[0]
                mx, ng, sm, rc = (small[0:parts, cols + i:cols + i + 1] for i in range(4))
                done(v.tensor_tensor(tile, src, mask, ALU.add), names[0])
                did(names[0])
                order(v.tensor_reduce(mx, tile, AX.X, ALU.max))
                done(v.tensor_scalar(ng, mx, -1.0, None, ALU.mult), names[1])
                dve.wait_ge(sg("stage0_act"), ACT0.index(names[3]) + 1)
                order(v.reciprocal(rc, sm))
                done(v.tensor_scalar(tile, tile, rc, None, ALU.mult), names[2])
            pe_did("adj")
            softmax(SQ[0:16, 1344:1360], bank[2][0:16, 0:16], C("mask16", 16), 8, ("adj", "neg", "e1", "exp"))
            pe_did("adjT")
            done(v.tensor_copy(SQ[0:16, 1376:1392], bank[3][0:16, 0:16]), "adjT")
            pe_did("v")
            for ho in range(2):
                last = v.tensor_scalar(SQ[:, 1392 + 16 * ho:1408 + 16 * ho], bank[4][:, 16 * ho:16 * ho + 16],
                                       W0("gvb")[:, ho:ho + 1], None, ALU.add)
            done(last, "v")
            pe_did("support")
            done(v.tensor_copy(SQ[0:16, 1424:1680], bank[5][0:16, 0:256]), "support")
            pe_did("xpos")
            for ho in range(2):
                last = v.tensor_scalar(SQ[:, 1680 + 16 * ho:1696 + 16 * ho], bank[6][:, 16 * ho:16 * ho + 16],
                                       W0("gb")[:, ho:ho + 1], None, ALU.add)
            done(last, "xpos")
            pe_did("query")
            done(v.tensor_scalar(SQ[0:64, 1712:1728], bank[1][0:64, 0:16], W0("qb", 64), None, ALU.add), "query")
            pe_did("key")
            done(v.tensor_scalar(SQ[0:64, 1728:1856], bank[2][0:64, 0:128], W0("kb", 64), None, ALU.add), "key")
            pe_did("at")
            softmax(SQ[:, 1856:1872], bank[3][:, 0:16], C("maskbc"), 12, ("at", "neg2", "e2", "exp2"))
            pe_did("atT")
            done(v.tensor_copy(SQ[0:16, 1888:2016], bank[4][0:16, 0:128]), "atT")
            pe_did("val")
            done(v.tensor_copy(SQ[0:16, 2016:2272], bank[5][0:16, 0:256]), "val")
            pe_did("y")
            done(v.tensor_copy(SQ[:, 2272:2528], bank[6][:, 0:256]), "y")
            pe_did("z")
            Z = SS[:, 0:1024].rearrange("p (i h) -> p i h", h=16)
            D = SS[:, 1024:2048].rearrange("p (i h) -> p i h", h=16)
            Zv = SS[:, 0:1024].rearrange("p (n h) -> p n h", h=4)
            for hlo in range(4):
                last = v.tensor_copy(Zv[:, :, hlo], bank[hlo // 2][:, 256 * (hlo % 2):256 * (hlo % 2) + 256])
            done(last, "z")
            did("z")
            order(v.tensor_tensor(D[:, :, 0:15], Z[:, :, 1:16], Z[:, :, 0:15], ALU.subtract))
            up = O3[:, :, 0:63].rearrange("p i (a r) -> p i a r", a=3)
            wy = C("wy")[:, 0:63].rearrange("p (a r) -> p a r", a=3)
            D5 = D[:, :, 0:15].rearrange("p i (a k) -> p i a k", a=3)
            Z5 = Z[:, :, 0:15].rearrange("p i (a k) -> p i a k", a=3)
            dve.wait_ge(sg("in_turned"), 8)
            for k in range(5):
                rs = [r for r in range(21) if 5 * r // 21 == k]
                a, b = rs[0], rs[-1] + 1
                for ph in range(3):
                    d_ = D5[:, :, ph, k].unsqueeze(2).broadcast_to([128, L, b - a])
                    z_ = Z5[:, :, ph, k].unsqueeze(2).broadcast_to([128, L, b - a])
                    w_ = wy[:, ph, a:b].unsqueeze(1).broadcast_to([128, L, b - a])
                    order(v.tensor_tensor(up[:, :, ph, a:b], d_, w_, ALU.mult))
                    order(v.tensor_tensor(up[:, :, ph, a:b], up[:, :, ph, a:b], z_, ALU.add))
            order(v.tensor_copy(O3[:, :, 63:64], Z[:, :, 15:16]))
            order(v.tensor_tensor(X, X, O, ALU.add))
            groupnorm(1, XN, "xn1")
            dve.wait_ge(sg("xn1"), 1)

            dve.wait_ge(sg("stage1_weights_loaded"), 32)
            negA, hb = small[:, 32:48], small[:, 48:49]
            st = SQ[:, 0:SEQ1 * PADL].rearrange("p (s l) -> p s l", l=PADL)
            vv, t, u, z2, xd, dt = (SQ[:, 1024 + 512 * i:1536 + 512 * i] for i in range(6))
            w0_, w1_, w2_, dtu = (SS[:, 512 * i:512 * i + 512] for i in range(4))
            dA = [SS[:, 2048 + 512 * i:2560 + 512 * i] for i in range(2)]
            dbu = [SS[:, 3072 + 512 * i:3584 + 512 * i] for i in range(2)]
            hs = [work[:, 1536 + 512 * i:2048 + 512 * i] for i in range(2)]
            yz = work[:, 1024:1536]
            hc = [Y[:, 512 * i:512 * i + 512] for i in range(2)]
            acc = Y[:, 1024:1536]
            order = Order(dve, "s1_setup")
            v.tensor_scalar(negA, W1("alog"), 80.0, None, ALU.min).then_inc(sg("s1_alog"), 1)
            dve.wait_ge(sg("s1_expA"), 1)
            order(v.tensor_scalar(negA, negA, -1.0, None, ALU.mult))
            order(v.tensor_tensor(W1("winx_b"), W1("winx_a"), W1("wcb"), ALU.mult))
            order(v.tensor_tensor(W1("winx_a"), W1("winx_a"), W1("wca"), ALU.mult))
            v.memset(SQ[:, 0:SEQ1 * PADL], 0.0)
            v.memset(SS[:, 2048:3072], 0.0)
            order(v.tensor_scalar(hb, W1("bconv"), 0.5, None, ALU.mult))
            v.tensor_scalar(small[:, 49:50], hb, 1.0, None, ALU.mult).then_inc(sg("s1_consts"), 1)

            def softplus(prefix, base, x, e, r, y, ready, order):
                dve.wait_ge(sg(prefix + "_exp"), base + 1)
                order(v.tensor_scalar(r, e, 2.0, None, ALU.add))
                order(v.reciprocal(r, r))
                order(v.tensor_tensor(r, r, e, ALU.mult))
                order(v.tensor_tensor(y, r, r, ALU.mult))
                order(v.tensor_scalar(e, y, LOG1P[4], None, ALU.mult))
                for i in (3, 2, 1):
                    order(v.scalar_tensor_tensor(e, e, LOG1P[i], y, ALU.add, ALU.mult))
                order(v.scalar_tensor_tensor(e, e, LOG1P[0], r, ALU.add, ALU.mult))
                v.scalar_tensor_tensor(x, x, 0.0, e, ALU.max, ALU.add).then_inc(sg(ready), 1)

            with dve.Fori(0, NK1) as k:
                order = Order(dve, "s1_order", dve.snap(k * 12))
                dve.wait_ge(sg("s1_front"), k)
                cols = XN3[:, :, bass.ds(k * J1, J1)].rearrange("p i j -> p j i")
                for tp in range(2):
                    for b in range(NB):
                        last = v.tensor_copy(st[64 * tp:64 * tp + 64, J1 * b:J1 * b + J1, 3 + tp:3 + L],
                                             cols[64 * b:64 * b + 64, :, 0:L - tp])
                last.then_inc(sg("s1_staged"), 1)
                dve.wait_ge(sg("s1_front"), k + 1)
                dve.wait_ge(sg("s1_tanh"), k + 1)
                order(v.tensor_scalar(vv, bank[0], W1("bconv"), 0.5, ALU.add, ALU.mult))
                v.scalar_tensor_tensor(u, t, 1.0, vv, ALU.add, ALU.mult).then_inc(sg("s1_u"), 1)
                dve.wait_ge(sg("s1_tanhz"), k + 1)
                v.scalar_tensor_tensor(z2, w0_, 1.0, bank[1], ALU.add, ALU.mult).then_inc(sg("s1_z"), 1)
                dve.wait_ge(sg("s1_dbl"), k + 1)
                v.tensor_copy(xd[0:80, :], bank[2][0:80, :]).then_inc(sg("s1_xd"), 1)
                dve.wait_ge(sg("s1_dtp"), k + 1)
                v.tensor_scalar(dt, bank[3], W1("bdt"), None, ALU.add).then_inc(sg("s1dt_added"), 1)
                softplus("s1dt", k, dt, w0_, w1_, w2_, "s1dt_ready", order)
                dve.wait_ge(sg("s1dt_ready"), k + 1)
                order(v.tensor_tensor(dtu, dt, u, ALU.mult))
                s0 = dve.snap(k * S1)
                for s in range(-1, S1 + 1):
                    if s + 1 < S1:
                        dve.wait_ge(sg("s1_B"), s0 + (s + 2))
                        if s >= 1:
                            dve.wait_ge(sg("s1_h"), s0 + s)
                        v.tensor_tensor(dbu[(s + 1) % 2], dtu, bank[4 + (s + 1) % 2], ALU.mult).then_inc(
                            sg("s1_dbu"), 1)
                    if 0 <= s < S1:
                        dve.wait_ge(sg("s1_dbu"), s0 + (s + 1))
                        dve.wait_ge(sg("s1_dA"), s0 + (s + 1))
                        if s >= 2:
                            dve.wait_ge(sg("s1_hc"), s0 + (s - 1))
                        v.tensor_tensor_scan(hs[s % 2], dA[s % 2], dbu[s % 2], 0.0, ALU.mult, ALU.add).then_inc(
                            sg("s1_h"), 1)
                    if s >= 1:
                        dve.wait_ge(sg("s1_h"), s0 + s)
                        dve.wait_ge(sg("s1_C"), s0 + s)
                        if s >= 3:
                            dve.wait_ge(sg("s1_acc"), s0 + (s - 2))
                        v.tensor_tensor(hc[(s - 1) % 2], hs[(s - 1) % 2], bank[6 + (s - 1) % 2],
                                        ALU.mult).then_inc(sg("s1_hc"), 1)
                dve.wait_ge(sg("s1_acc"), s0 + S1)
                order(v.scalar_tensor_tensor(vv, u, W1("dp"), acc, ALU.mult, ALU.add))
                v.scalar_tensor_tensor(yz, vv, 0.5, z2, ALU.mult, ALU.mult).then_inc(sg("s1_gated"), 1)
            for ch in range(NCHUNK):
                dve.wait_ge(sg("ln_mean"), ch + 1)
                o = O[:, BANK * ch:BANK * ch + BANK]
                v.tensor_tensor(o, o, bank[6 + ch % 2], ALU.subtract).then_inc(sg("ln_centred"), 1)
            dve.wait_ge(sg("ln_centred"), NCHUNK)
            dve.wait_ge(sg("ln_scale"), 1)
            order = Order(dve, "ln_order")
            order(v.scalar_tensor_tensor(O, O, W1("gamma"), SS, ALU.mult, ALU.mult))
            order(v.scalar_tensor_tensor(X, O, W1("beta"), X, ALU.add, ALU.add))

            def call(m, n, d, c):
                raw = raws[d]

                def W(name):
                    a, b = Ws[name]
                    return raw[:, a:b]
                dve.wait_ge(sg("zeroed"), 1)
                dve.wait_ge(sg(f"block_weights_loaded{d}"), (m * 2 + n) * 16 + 16)
                v.tensor_tensor(wxa, W("wx"), W("cxa"), ALU.mult)
                v.tensor_tensor(wxb, W("wx"), W("cxb"), ALU.mult)
                for tp, cw in ((0, "cbca"), (1, "cbcb")):
                    for b in range(NB):
                        v.tensor_tensor(wbc[tp][b], W(f"wbc{b}"), W(cw), ALU.mult)
                for hd in range(2):
                    v.tensor_scalar(wog[hd], W(f"wo{hd}"), W("gnw")[:, hd:hd + 1], None, ALU.mult)
                v.scalar_tensor_tensor(dhalf.rearrange("p (h b) -> p h b", b=2),
                                       W("dh").unsqueeze(2).broadcast_to([128, 8, 2]), 0.5,
                                       C("maskb").rearrange("p (h b) -> p h b", b=2), ALU.mult, ALU.mult)
                v.tensor_copy(bxr, W("bx")[0:1, :])
                v.tensor_copy(bbcr, W("bbc")[0:1, :]).then_inc(sg("folded"), 1)
                dve.wait_ge(sg("norm_scale"), c + 1)
                dve.wait_ge(sg("y_ready"), y_value(m, n, d))
                v.scalar_tensor_tensor(XN, Y, W("nw"), O, ALU.mult, ALU.mult).then_inc(sg("normed"), 1)
                dve.wait_ge(sg("dt_psum"), c + 1)
                for hq in range(2):
                    last = v.tensor_scalar(DT[:, 512 * hq:512 * hq + 512], bank[4 + hq], W("bdt"), None, ALU.add)
                last.then_inc(sg("dt_added"), 1)
                order = Order(dve, "block_order", dve.snap(c * 10))
                softplus("dt", c, DT, dtw[0], dtw[1], dtw[2], "dt_ready", order)
                dve.wait_ge(sg("dt_ready"), c + 1)
                dve.wait_ge(sg("normed"), c + 1)
                for i in range(16):
                    ch, hd = i // 2, i % 2
                    dve.wait_ge(sg("z_tanh"), c * 16 + (i + 1))
                    v.scalar_tensor_tensor(Z2[:, TOK * hd + BANK * ch:TOK * hd + BANK * ch + BANK], tz[i % 2], 1.0,
                                           bank[6 + i % 2], ALU.add, ALU.mult).then_inc(sg("z_ready"), 1)
                dve.wait_ge(sg("expA_ready"), c + 1)
                dve.wait_ge(sg("z_ready"), c * 16 + 16)

                def stage(t, T, q, free):
                    if free:
                        dve.wait_ge(sg("projected"), T + (t - 1))
                    s = SA[t % 2]
                    src = axis(XN3, d, q).rearrange("p i j -> p (i j)")
                    v.tensor_copy(s[64:128, 1:L], src[0:64, 0:L - 1])
                    v.tensor_copy(s[0:64, L:2 * L], src[64:128, :]).then_inc(sg("staged_shifted"), 1)

                def step(tau, T, known, q0=None):
                    if part_of(known, 1):
                        q = (q0 + (tau + 1)) if known is None else tau + 1
                        stage(tau + 1, T, q, later(known, 1, 2))
                    if part_of(known, 0):
                        p, r = tau % 2, tau % 4
                        dve.wait_ge(sg("tanh_ready"), T + (tau + 1))
                        if later(known, 0, 2):
                            dve.wait_ge(sg("am2_ready"), T + (tau - 1))
                            dve.wait_ge(sg("am1_ready"), T + (tau - 1))
                            dve.wait_ge(sg("xb_ready"), T + (tau - 1))
                        v.tensor_copy(DA[p][:, 8:24], bank[p][:, 200:216])
                        v.scalar_tensor_tensor(DA[p][:, 0:8], bank[p][:, 192:200], -1.0, expA, ALU.mult,
                                               ALU.mult).then_inc(sg("a_ready"), 1)
                        v.scalar_tensor_tensor(X2[p], TX[p][:, 0:128], 1.0, bank[p][:, 0:128], ALU.add,
                                               ALU.mult).then_inc(sg("x_ready"), 1)
                        if later(known, 0, 2):
                            dve.wait_ge(sg("scored"), T + (tau - 1))
                        bc, tb = bank[p][:, 128:192], TX[p][:, 128:192]
                        for b in range(NB):
                            h = slice(32 * b, 32 * b + 32)
                            v.scalar_tensor_tensor(BB[p][h, 64 * b:64 * b + 64], tb[h, :], 1.0, bc[h, :], ALU.add,
                                                   ALU.mult)
                        v.scalar_tensor_tensor(C2[p][0:64, :], tb[64:128, :], 1.0, bc[64:128, :], ALU.add,
                                               ALU.mult).then_inc(sg("bc_ready"), 1)
                        dve.wait_ge(sg("a_ready"), T + (tau + 1))
                        v.tensor_tensor(AM1[p].rearrange("p (h l) -> p h l", l=L),
                                        DA[p][:, 0:8].unsqueeze(2).broadcast_to([128, 8, L]),
                                        C("upto").unsqueeze(1).broadcast_to([128, 8, L]), ALU.mult).then_inc(
                            sg("am1_ready"), 1)
                    if part_of(known, -1):
                        p = (tau - 1) % 2
                        dve.wait_ge(sg("scored"), T + tau)
                        v.tensor_tensor(GM[p], bank[p][:, 256:320], C("diag2"), ALU.mult).then_inc(
                            sg("gm_ready"), 1)
                        dve.wait_ge(sg("gm_ready"), T + tau)
                        dve.wait_ge(sg("decay_ready"), T + tau)
                        if later(known, -1, 2):
                            dve.wait_ge(sg("y_psum"), T + (tau - 2))
                        v.tensor_tensor(MM[p].rearrange("p (h l) -> p h l", l=L),
                                        DK[p].rearrange("p (h l) -> p h l", l=L),
                                        GM[p].unsqueeze(1).broadcast_to([128, 8, L]), ALU.mult).then_inc(
                            sg("mixed"), 1)
                    if part_of(known, -2):
                        p = (tau - 2) % 2
                        q = (q0 + (tau - 2)) if known is None else tau - 2
                        dve.wait_ge(sg("y_psum"), T + (tau - 1))
                        if later(known, -2, 2):
                            dve.wait_ge(sg("out_psum"), T + (tau - 3))
                        z = Z24[:, :, :, bass.ds(q, 1)] if d == 0 else Z24[:, :, bass.ds(q, 1), :]
                        z = z.rearrange("p h i j -> p h (i j)")
                        v.tensor_tensor(YZ[p].rearrange("p (h l) -> p h l", l=L),
                                        bank[4 + p][:, 0:128].rearrange("p (h l) -> p h l", l=L), z,
                                        ALU.mult).then_inc(sg("gated"), 1)

                tiles(dve, c, -1, L + 2, step, lead=1)
                dve.wait_ge(sg("gate_scale"), c + 1)
                order(v.tensor_tensor(O, O, SS, ALU.mult))
                v.tensor_tensor(Y, Y, O, ALU.add).then_inc(sg("y_ready"), 1)
                dve.wait_ge(sg("y_ready"), y_value(m, n, d) + 1)
                v.tensor_copy(small[:, 60:61], small[:, 60:61]).then_inc(sg(f"block_done{d}"), 1)

            def entry(m):
                groupnorm(m + 2, Y, "y_ready")

            def leave(m):
                v.tensor_tensor(X, X, Y, ALU.add).then_inc(sg("x_added"), 1)
                dve.wait_ge(sg("x_added"), m + 1)

            v.memset(small[:, 60:61], 0.0)
            rounds(dve, entry, call, leave)
            v.tensor_copy(small[:, 61:62], X[:, 0:1]).then_inc(sg("x_final"), 1)
            for k in range(0, 8, 2):
                dve.wait_ge(sg("out_in_psum"), k + 1)
                v.tensor_copy(O[:, BANK * k:BANK * k + BANK], bank[k]).then_inc(sg("out_turned"), 1)


def _constants():
    import numpy as np
    p = np.arange(128)
    b, s = p // 64, p % 64
    l = np.arange(64)
    f = np.float32
    c = {}
    c["ident"] = np.eye(128)
    same = b[:, None] == b[None, :]
    c["mean64"] = same / 64.0
    c["pair"] = (p[:, None] // 2 == p[None, :] // 2) / (2.0 * TOK)
    c["later"] = same & (s[:, None] > s[None, :])
    c["earlier"] = same & (s[:, None] < s[None, :])
    bp = (p // 16) % 2
    c["ssum"] = (bp[:, None] == b[None, :]) / 128.0
    c["upto"] = s[:, None] <= l[None, :]
    c["from_"] = s[:, None] >= l[None, :]
    c["diag2"] = 1.0 + (s[:, None] == l[None, :])
    c["stack"] = s[:, None] == l[None, :]
    r = p % 32
    h8, hb = np.arange(8), np.arange(16)
    real = r[:, None] < 16
    c["seldt"] = np.concatenate([real & (r[:, None] % 8 == h8[None, :]),
                                 0.125 * (real & (r[:, None] % 8 == hb // 2) & (r[:, None] // 8 == hb % 2))], axis=1)
    c["maskb"] = 1.0 * (b[:, None] == hb[None, :] % 2)
    kb, kg = np.arange(8) // 4, np.arange(8) % 4
    c["maskdt"] = (r[:, None] < 16) & (r[:, None] // 8 == kb[None, :]) & (p[:, None] // 32 == kg[None, :])
    k16 = np.arange(16) // 8
    c["mask16"] = np.where((p[:, None] // 8) == k16[None, :], 0.0, -1e30)
    c["maskbc"] = np.where(b[:, None] == k16[None, :], 0.0, -1e30)
    c["ones"] = np.ones((128, 128))
    c["eps6"], c["eps6x4"], c["eps5"] = (np.full((128, 1), e) for e in (1e-6, 4e-6, 1e-5))
    pos = np.linspace(0.0, 15.0, 64).astype(f)
    lo = (5 * l) // 21
    frac = (pos - lo).astype(f)
    wc = np.zeros((16, 64), f)
    wc[lo, l] += (1.0 - frac)
    wc[np.minimum(lo + 1, 15), l] += frac
    interp = np.zeros((4, 128, 128), f)
    for hlo in range(4):
        for bb in range(2):
            interp[hlo, 64 * bb + 16 * hlo:64 * bb + 16 * hlo + 16, 64 * bb:64 * bb + 64] = wc
    c["interp"] = interp.transpose(1, 0, 2).reshape(128, 512)
    c["wy"] = np.broadcast_to(frac, (128, 64))
    packed = np.concatenate([np.asarray(c[n], f).reshape(128, w) for n, w in CONST_COLS], axis=1)
    pool = np.zeros((2, 8, 128, 128), f)
    for bb in range(2):
        for jj in range(8):
            for ch in range(64):
                pool[bb, jj, 64 * bb + ch, 16 * jj + ch // 4] = 1.0 / 16.0
    pool = pool.reshape(16, 128, 128).transpose(1, 0, 2).reshape(128, 2048)
    state = np.zeros((128, 2, 16, 128), f)
    for k in range(16):
        state[32 + k, 0, k] = 1.0
        state[64 + k, 1, k] = 1.0
    return packed, pool, state.reshape(128, 4096)


def _pack(cols, given):
    import numpy as np
    out = np.zeros((128, width(cols)), np.float32)
    at = spans(cols)
    for name, a in given.items():
        lo, hi = at[name]
        a = np.asarray(a)
        a = a[:, None] if a.ndim == 1 else a
        out[0:a.shape[0], lo:hi] = a
    return out


def _halves(wt):
    import numpy as np
    return np.concatenate([wt[0:128], wt[128:256]], axis=1)


def _stage0(w):
    g = {}
    for short, name in (("gq", "gcn_qw"), ("gk", "gcn_kw"), ("gv", "gcn_vw"), ("q", "qw"), ("k", "kw"), ("v", "vw")):
        g[short] = _halves(_permute(w[name].T))
    g["gw"] = _halves(w["gcn_weight"])
    g["gb"] = w["gcn_bias"].reshape(2, 128).T
    g["gvb"] = w["gcn_vb"].reshape(2, 128).T
    g["gqb"], g["gkb"], g["qb"], g["kb"] = w["gcn_qb"], w["gcn_kb"], w["qb"], w["kb"]
    g["vb"] = w["vb"][None, :]
    return _pack(L0_COLS, g)


def _permute(a):
    return a


def _stage1(w):
    import numpy as np
    g = {}
    win = w["W_in"].T
    g["winx_a"] = np.concatenate([win[:, 0:128]] * 2)
    taps = w["W_conv"][:, 0, :].T
    g["wca"] = np.concatenate([np.broadcast_to(taps[3], (64, 128)), np.broadcast_to(taps[2], (64, 128))])
    g["wcb"] = np.concatenate([np.broadcast_to(taps[1], (64, 128)), np.broadcast_to(taps[0], (64, 128))])
    g["wz"] = win[:, 128:256]
    wxp = np.zeros((128, 80), np.float32)
    wxp[:, 0:4] = w["W_xproj"][0:4].T
    wxp[:, 32:48] = w["W_xproj"][4:20].T
    wxp[:, 64:80] = w["W_xproj"][20:36].T
    g["wxp"] = wxp
    g["wdt"] = w["W_dt"].T
    g["bconv"], g["bdt"], g["alog"], g["dp"] = w["b_conv"], w["b_dt"], w["A_log"], w["D_param"]
    g["wout"] = w["W_out"].T
    g["gamma"], g["beta"] = np.concatenate([w["gamma"]] * 2), np.concatenate([w["beta"]] * 2)
    return _pack(L1_COLS, g)


def _block(norm_w, Win, Wconv, bconv, dt_bias, A_log, D, gn_w, Wout):
    import numpy as np
    g = {}
    g["wx"] = np.concatenate([Win[:, 128:256]] * 2)
    taps = Wconv.T

    def pair(k0, k1, row):
        return np.concatenate([np.broadcast_to(row[k0], (64, row.shape[1])),
                               np.broadcast_to(row[k1], (64, row.shape[1]))])
    g["cxa"], g["cxb"] = pair(3, 2, taps[:, 0:128]), pair(1, 0, taps[:, 0:128])
    spread = np.zeros((4, 2, 2, 32), np.float32)
    spread[:, :, :, 0:16] = taps[:, 128:160].reshape(4, 2, 1, 16)
    spread = spread.reshape(4, 128)
    g["cbca"], g["cbcb"] = pair(3, 2, spread), pair(1, 0, spread)
    for b in range(2):
        wb = np.zeros((64, 2, 2, 32), np.float32)
        wb[:, :, b, 0:16] = Win[:, 256:288].reshape(64, 2, 16)
        g[f"wbc{b}"] = np.concatenate([wb.reshape(64, 128)] * 2)
    g["bx"] = bconv[None, 0:128]
    bb = np.zeros((1, 2, 2, 32), np.float32)
    bb[..., 0:16] = bconv[128:160].reshape(1, 2, 1, 16)
    g["bbc"] = bb.reshape(1, 128)
    for hd in range(2):
        wz = np.zeros((2, 64, 4, 2, 16), np.float32)
        wo = np.zeros((4, 2, 16, 2, 64), np.float32)
        for b in range(2):
            wz[b, :, :, b] = Win[:, 64 * hd:64 * hd + 64].reshape(64, 4, 16)
            wo[:, b, :, b] = Wout[64 * hd:64 * hd + 64].reshape(4, 16, 64)
        g[f"wz{hd}"], g[f"wo{hd}"] = wz.reshape(128, 128), wo.reshape(128, 128)
    wdt = np.zeros((2, 64, 32), np.float32)
    bdt = np.zeros((4, 32), np.float32)
    for b in range(2):
        wdt[b, :, 8 * b:8 * b + 8] = Win[:, 288:296]
        bdt[:, 8 * b:8 * b + 8] = dt_bias
    g["wdt"], g["bdt"] = wdt.reshape(128, 32), bdt.reshape(128)
    g["alog"], g["dh"] = np.broadcast_to(A_log, (128, 8)), np.broadcast_to(D, (128, 8))
    g["nw"] = np.concatenate([norm_w] * 2)
    gw = gn_w.reshape(2, 4, 1, 16)
    g["gnw"] = np.broadcast_to(gw, (2, 4, 2, 16)).reshape(2, 128).T
    g["wo0"], g["wo1"] = g["wo0"], g["wo1"]
    return _pack(CALL_COLS, g)


def kernel(**inputs):
    import numpy as np
    import concourse.bacc as bacc
    from concourse.bass_utils import run_bass_kernel_spmd

    a = {k: np.asarray(v) for k, v in inputs.items()}
    names = ("norm_w", "Win", "Wconv", "bconv", "dt_bias", "A_log", "D", "gn_w", "Wout")
    calls = [_block(*(a[f"L{st}_conv_{ax}_{n}"][i] for n in names))
             for st in (2, 3) for i in range(2) for ax in ("t", "b")]
    consts, pool_sel, state_sel = _constants()
    arrays = {
        "x": np.ascontiguousarray(a["x"]), "consts": consts, "pool_sel": pool_sel, "state_sel": state_sel,
        "l0w": _stage0({k[8:]: v for k, v in a.items() if k.startswith("L0_conv_")}),
        "l1w": _stage1({k[8:]: v for k, v in a.items() if k.startswith("L1_conv_")}),
        "callw": np.stack(calls),
    }
    nc = bacc.Bacc("TRN2", target_bir_lowering=False, num_devices=1)
    args = [nc.dram_tensor(k, v.shape, mybir.dt.float32, kind="ExternalInput").ap() for k, v in arrays.items()]
    out = nc.dram_tensor("out", (2, 64, 64, 64), mybir.dt.float32, kind="ExternalOutput").ap()
    program(nc, *args, out)
    r = run_bass_kernel_spmd(nc, [arrays], core_ids=[0])
    return r.results[0]["out"]
```

```python
from contextlib import ExitStack

import concourse.bass as bass
from concourse import mybir

F32 = mybir.dt.float32
BF16 = mybir.dt.bfloat16
ALU = mybir.AluOpType
ACT = mybir.ActivationFunctionType
AX = mybir.AxisListType

NB, L, CH = 2, 64, 64
P = NB * CH
TOK = L * L
BANK = 512
NCHUNK = TOK // BANK
NH, HP, NS = 8, 16, 16
PADL = L + 3
S1 = 16
J1 = 4
NK1 = L // J1
SEQ1 = NB * J1
LOG1P = (2.00000000788, 0.666663159351, 0.400248537234, 0.279614188352, 0.281746572615)

CONST_COLS = [("ident", 128), ("mean64", 128), ("pair", 128), ("ssum", 128), ("between", 64),
              ("span", 64), ("diag2", 64), ("stack", 64), ("maskdt", 8), ("dtrow", 2),
              ("mask16", 16), ("maskbc", 16), ("ones", 128), ("eps6", 1), ("eps6x4", 1), ("eps5", 1),
              ("interp", 512), ("wy", 64)]
CALL_COLS = [("wx", 128), ("cxa", 128), ("cxb", 128), ("wbc", 128), ("cbca", 128), ("cbcb", 128),
             ("seldt_bx", 144), ("bbc", 1), ("wz0", 128), ("wz1", 128), ("wdt", 32), ("bdt", 1), ("alog", 16),
             ("dh", 8),
             ("nw", 1), ("gnw", 2), ("wo0", 128), ("wo1", 128)]
L0_COLS = [("gq", 128), ("gk", 128), ("gv", 512), ("gw", 512), ("gb", 2), ("gqb", 1), ("gkb", 1), ("gvb", 2),
           ("q", 128), ("qb", 1), ("k", 128), ("kb", 1), ("v", 512), ("vb", 256)]
L1_COLS = [("winx_a", 128), ("winx_b", 128), ("wca", 128), ("wcb", 128), ("wz", 128), ("wxp", 64), ("wdt", 128), ("bconv", 1),
           ("bdt", 1), ("alog", 16), ("dp", 1), ("wout", 64), ("gamma", 1), ("beta", 1)]


def width(cols):
    return sum(n for _, n in cols)


def spans(cols):
    at, out = 0, {}
    for name, n in cols:
        out[name] = (at, at + n)
        at += n
    return out


def program(nc, x, consts, pool_sel, state_sel, l0w, l1w, callw, out):
    ctx = ExitStack()
    with ctx:
        sems = {}

        def sb(name, cols):
            return ctx.enter_context(nc.sbuf_tensor(name, [128, cols], F32))[:, :]

        def sg(name):
            if name not in sems:
                sems[name] = ctx.enter_context(nc.semaphore(name))
            return sems[name]

        class Order:

            def __init__(self, eng, name, base=0):
                self.eng, self.name, self.base, self.n = eng, name, base, 0

            def __call__(self, ins):
                self.n += 1
                ins.then_inc(sg(self.name), 1)
                self.eng.wait_ge(sg(self.name), self.base + self.n)

        bank = [ctx.enter_context(nc.psum_tensor(f"bank{i}", [128, BANK], F32))[:, :] for i in range(8)]

        X = sb("X", TOK)
        Y = sb("Y", TOK)
        XN = sb("XN", TOK)
        Z2 = sb("Z2", 2 * TOK)
        O = sb("O", TOK)
        SS = sb("SS", TOK)
        SQ = sb("SQ", TOK)
        cst = sb("cst", width(CONST_COLS))
        raws = [sb(f"raw{i}", width(CALL_COLS)) for i in range(2)]
        FW = sb("folded_weights", 1312)
        small = sb("small", 64)
        ring4 = sb("ring4", 4 * 512)
        work = sb("work", 6400)
        Cs, Ws, W0s, W1s = spans(CONST_COLS), spans(CALL_COLS), spans(L0_COLS), spans(L1_COLS)

        def C(name, parts=128):
            a, b = Cs[name]
            return cst[0:parts, a:b]

        ident = C("ident")
        X3, XN3, O3, SS3 = (t.rearrange("p (i j) -> p i j", j=L) for t in (X, XN, O, SS))
        Z24 = Z2.rearrange("p (h i j) -> p h i j", h=2, j=L)

        def axis(t3, direction, q, n=1):
            return t3[:, :, bass.ds(q, n)] if direction == 0 else t3[:, bass.ds(q, n), :]

        taken = [0]

        def part(cols):
            taken[0] += cols
            assert taken[0] <= 6400
            return work[:, taken[0] - cols:taken[0]]

        SA = [part(NB * L) for _ in range(2)]
        SB = [part(NB * L) for _ in range(2)]
        DTB = [part(128) for _ in range(2)]
        TX = [part(192) for _ in range(2)]
        UB = [part(64) for _ in range(2)]
        BB = [part(128) for _ in range(2)]
        C2 = [part(64) for _ in range(2)]
        DA = [part(32) for _ in range(2)]
        AM = [[part(512) for _ in range(2)] for _ in range(2)]
        GM = [part(64) for _ in range(2)]
        YZ = [part(128) for _ in range(4)]
        YQ = [part(128) for _ in range(2)]
        DK = [part(512) for _ in range(2)]
        XB = [ring4[:, 512 * r:512 * r + 256] for r in range(4)]
        X2 = [ring4[:, 512 * r + 256:512 * r + 512] for r in range(4)]
        MM = [sb(f"scores_times_decays{i}", 512) for i in range(2)]
        DT = sb("DT", 1024)
        dtw = [SS[:, 1024 * i:1024 * i + 1024] for i in range(3)]
        tz = [SQ[:, 512 * i:512 * i + 512] for i in range(2)]

        wxa, wxb = FW[:, 0:128], FW[:, 128:256]
        wbc = [FW[:, 256 + 128 * t:384 + 128 * t] for t in range(2)]
        wog = [FW[:, 512 + 128 * h:640 + 128 * h] for h in range(2)]
        Dhalf = FW[:, 768:1280]
        expA, bbc_half = FW[:, 1280:1296], FW[:, 1296:1297]
        PDT, PX, PBC = slice(0, 16), slice(16, 144), slice(144, 208)

        w0, w1 = Y[:, 0:width(L0_COLS)], Y[:, 2320:2320 + width(L1_COLS)]
        assert width(L0_COLS) <= 2320 and 2320 + width(L1_COLS) <= TOK
        poolS, stateS = Z2[:, 0:2048], Z2[:, 2048:2048 + 4096]

        selBC = Z2[:, 6144:8192].bitcast(BF16)
        parts = work[:, 2560:2816].bitcast(BF16)
        mid = work[:, 2816:3072].bitcast(BF16)
        rest = work[:, 3072:3584]

        def W0(name, parts=128):
            a, b = W0s[name]
            return w0[0:parts, a:b]

        def W1(name, parts=128):
            a, b = W1s[name]
            return w1[0:parts, a:b]

        x_tok = x.rearrange("b i j c -> b (i j) c")
        out_tok = out.rearrange("b i j c -> b (i j) c")
        Otok = O.rearrange("p (t b c) -> p t b c", b=2, c=64)
        ctx.enter_context(nc.allow_non_contiguous_dma("token-major rows of 64 channels"))
        block = ctx.enter_context(nc.Block())

        def rounds(eng, mod_pre, call, mod_post):
            with eng.Fori(0, 2) as m:
                mod_pre(m)
                with eng.Fori(0, 2) as n:
                    for d in range(2):
                        call(m, n, d, eng.snap(m * 4 + n * 2 + d))
                mod_post(m)

        def tiles(eng, c, first, last, step, lead=0):
            T0 = eng.snap(c * L)
            for tau in range(first, 8):
                step(tau, T0, tau)
            with eng.Fori(0, 14 - lead) as it:
                q0 = eng.snap(it * 4)
                T = eng.snap(T0 + q0)
                for u in range(4):
                    step(u + 8, T, None, q0)
            for tau in range(L - 4 * lead, last):
                step(tau, T0, tau)

        def part_of(known, offset):
            return known is None or 0 <= known + offset < L

        def later(known, offset, k):
            return known is None or known + offset >= k

        def y_value(m, n, d):
            return m * 5 + n * 2 + d + 1

        @block.sync
        def _(sp):
            sp.dma_start(cst, consts).then_inc(sg("constants_loaded"), 16)
            for b in range(NB):
                sp.dma_start(Otok[:, :, b, :], x_tok[b].rearrange("(t p) c -> p t c", p=128)).then_inc(
                    sg("x_loaded"), 16)
            sp.dma_start(w0, l0w).then_inc(sg("stage0_weights_loaded"), 16)
            sp.dma_start(poolS, pool_sel).then_inc(sg("stage0_weights_loaded"), 16)
            sp.dma_start(w1, l1w).then_inc(sg("stage1_weights_loaded"), 16)
            sp.dma_start(stateS, state_sel).then_inc(sg("stage1_weights_loaded"), 16)
            for d in range(2):
                sp.dma_start(raws[d], callw[d]).then_inc(sg(f"block_weights_loaded{d}"), 16)

            with sp.Fori(0, 3) as r:
                for d in range(2):
                    sp.wait_ge(sg(f"block_done{d}"), r + 1)
                    sp.dma_start(raws[d], callw[bass.ds(r * 2 + d + 2, 1)].rearrange("a p n -> p (a n)")).then_inc(
                        sg(f"block_weights_loaded{d}"), 16)
            for b in range(NB):
                sp.wait_ge(sg("out_turned"), 8)
                sp.dma_start(out_tok[b].rearrange("(t p) c -> p t c", p=128), Otok[:, :, b, :]).then_inc(
                    sg("output_stored"), 16)
            sp.wait_ge(sg("output_stored"), 32)

        PE0 = ["xp", "qk", "adj", "adjT", "v", "support", "xpos", "query", "key", "at", "atT", "val", "y", "z"]
        DVE0 = ["xj", "xp", "xpre", "qk", "adj", "neg", "e1", "adjT", "v", "support", "xpos", "query", "key", "at",
                "neg2", "e2", "atT", "val", "y", "z"]
        ACT0 = ["exp", "exp2"]

        @block.tensor
        def _(pe):
            mm, tr = nc.tensor.matmul, nc.tensor.transpose

            def groupnorm(g):
                pe.wait_ge(sg("gn_sum"), g + 1)
                mm(bank[7][:, 0:1], C("pair"), small[:, 0:1], start=True, stop=True).then_inc(sg("gn_mean"), 1)
                pe.wait_ge(sg("gn_square"), g + 1)
                mm(bank[7][:, 8:9], C("pair"), small[:, 2:3], start=True, stop=True).then_inc(sg("gn_var"), 1)

            def turn_in():
                pe.wait_ge(sg("constants_loaded"), 16)
                pe.wait_ge(sg("x_loaded"), 32)
                for k in range(8):
                    for t in range(4):
                        a = BANK * k + 128 * t
                        last = tr(bank[k][:, 128 * t:128 * t + 128], O[:, a:a + 128], ident)
                    last.then_inc(sg("in_turned"), 1)

            def turn_out():
                pe.wait_ge(sg("x_final"), 1)
                for k in range(8):
                    for t in range(4):
                        a = BANK * k + 128 * t
                        last = tr(bank[k][:, 128 * t:128 * t + 128], X[:, a:a + 128], ident)
                    last.then_inc(sg("out_in_psum"), 1)

            def stage0():
                def need(name):
                    pe.wait_ge(sg("stage0_dve"), DVE0.index(name) + 1)

                def done(ins):
                    ins.then_inc(sg("stage0_pe"), 1)
                pe.wait_ge(sg("stage0_weights_loaded"), 32)
                need("xj")
                Xj = SQ[:, 0:1024].rearrange("p (i j) -> p i j", j=16)
                for hf in range(2):
                    for b in range(NB):
                        for jj in range(8):
                            r = b * 8 + jj
                            last = mm(bank[0][:, 128 * hf + 64 * b:128 * hf + 64 * b + 64],
                                      poolS[:, 128 * r:128 * r + 128], Xj[:, :, hf * 8 + jj],
                                      start=(jj == 0), stop=(jj == 7))
                done(last)
                xpT, xpre = SQ[:, 1024:1280], SQ[:, 1280:1312]
                need("xpre")
                for w, o in (("gq", 0), ("gk", 16)):
                    for hf in range(2):
                        last = mm(bank[1][0:64, o:o + 16], W0(w)[:, 64 * hf:64 * hf + 64],
                                  xpre[:, 16 * hf:16 * hf + 16], start=(hf == 0), stop=(hf == 1))
                done(last)
                need("qk")
                q, k = SQ[0:64, 1312:1328], SQ[0:64, 1328:1344]
                done(mm(bank[2][0:16, 0:16], k, q, start=True, stop=True))
                need("e1")
                done(tr(bank[3][0:16, 0:16], SQ[0:16, 1344:1360], ident[0:16, 0:16]))
                for ho in range(2):
                    for hf in range(2):
                        last = mm(bank[4][:, 16 * ho:16 * ho + 16],
                                  W0("gv")[:, 256 * hf + 128 * ho:256 * hf + 128 * ho + 128],
                                  xpre[:, 16 * hf:16 * hf + 16], start=(hf == 0), stop=(hf == 1))
                done(last)
                need("v")
                v = SQ[:, 1392:1424]
                for hf in range(2):
                    last = mm(bank[5][0:16, 0:256], v[:, 16 * hf:16 * hf + 16],
                              W0("gw")[:, 256 * hf:256 * hf + 256], start=(hf == 0), stop=(hf == 1))
                done(last)
                need("support")
                for ho in range(2):
                    last = mm(bank[6][:, 16 * ho:16 * ho + 16], SQ[0:16, 1424 + 128 * ho:1552 + 128 * ho],
                              SQ[0:16, 1376:1392], start=True, stop=True)
                done(last)
                need("xpos")
                xpos = SQ[:, 1680:1712]
                for hf in range(2):
                    last = mm(bank[1][0:64, 0:16], W0("q")[:, 64 * hf:64 * hf + 64],
                              xpos[:, 16 * hf:16 * hf + 16], start=(hf == 0), stop=(hf == 1))
                done(last)
                for hf in range(2):
                    last = mm(bank[2][0:64, 0:128], W0("k")[:, 64 * hf:64 * hf + 64],
                              xpT[:, 128 * hf:128 * hf + 128], start=(hf == 0), stop=(hf == 1))
                done(last)
                need("key")
                done(mm(bank[3][:, 0:16], SQ[0:64, 1728:1856], SQ[0:64, 1712:1728], start=True, stop=True))
                need("e2")
                done(tr(bank[4][0:16, 0:128], SQ[:, 1856:1872], ident))
                for hf in range(2):
                    mm(bank[5][0:16, 0:256], xpos[:, 16 * hf:16 * hf + 16], W0("v")[:, 256 * hf:256 * hf + 256],
                       start=(hf == 0), stop=False)
                done(mm(bank[5][0:16, 0:256], C("ones", 1)[:, 0:16], W0("vb", 1), start=False, stop=True))
                need("val")
                done(mm(bank[6][:, 0:256], SQ[0:16, 1888:2016], SQ[0:16, 2016:2272], start=True, stop=True))
                need("y")
                for hlo in range(4):
                    last = mm(bank[hlo // 2][:, 256 * (hlo % 2):256 * (hlo % 2) + 256],
                              C("interp")[:, 128 * hlo:128 * hlo + 128], SQ[:, 2272:2528], start=True, stop=True)
                done(last)

            def stage1():
                pe.wait_ge(sg("stage1_weights_loaded"), 32)
                st = SQ[:, 0:SEQ1 * PADL].rearrange("p (s l) -> p s l", l=PADL)
                u, xd, yz = SQ[:, 2048:2560], SQ[:, 3072:3584], work[:, 1024:1536]
                pe.wait_ge(sg("s1_selectors"), 1)
                with pe.Fori(0, NK1) as k:
                    pe.wait_ge(sg("s1_staged"), k + 1)
                    mm(bank[0], W1("winx_a"), st[:, :, 3:3 + L], start=True, stop=False)
                    mm(bank[0], W1("winx_b"), st[:, :, 1:1 + L], start=False, stop=True)
                    mm(bank[1], W1("wz"), st[:, :, 3:3 + L], start=True, stop=True).then_inc(sg("s1_front"), 1)
                    pe.wait_ge(sg("s1_u"), k + 1)
                    mm(bank[2][0:64, :], W1("wxp"), u, start=True, stop=True).then_inc(sg("s1_dbl"), 1)
                    pe.wait_ge(sg("s1_xd"), k + 1)
                    mm(bank[3], W1("wdt")[32:64, :], xd[32:64, :], start=True, stop=True).then_inc(sg("s1_dtp"), 1)
                    s0 = pe.snap(k * S1)
                    pe.wait_ge(sg("s1_split"), k + 1)
                    pe.wait_ge(sg("s1_split_mid"), k + 1)
                    for s in range(S1):
                        if s >= 2:
                            pe.wait_ge(sg("s1_dbu"), s0 + (s - 1))
                        mm(bank[4 + s % 2], selBC[0:96, 128 * s:128 * s + 128], parts[0:96, :], start=True,
                           stop=True).then_inc(sg("s1_B"), 1)
                        if s >= 2:
                            pe.wait_ge(sg("s1_hc"), s0 + (s - 1))
                        mm(bank[6 + s % 2], selBC[0:96, 2048 + 128 * s:2176 + 128 * s], parts[0:96, :], start=True,
                           stop=True).then_inc(sg("s1_C"), 1)
                    pe.wait_ge(sg("s1_gated"), k + 1)
                    for b in range(NB):
                        last = mm(bank[2][64 * b:64 * b + 64, 0:256], W1("wout"), yz[:, 256 * b:256 * b + 256],
                                  start=True, stop=True)
                    last.then_inc(sg("s1_out"), 1)
                for ch in range(NCHUNK):
                    pe.wait_ge(sg("s1_stored"), NK1)
                    if ch >= 2:
                        pe.wait_ge(sg("ln_centred"), ch - 1)
                    mm(bank[6 + ch % 2], C("mean64"), O[:, BANK * ch:BANK * ch + BANK], start=True,
                       stop=True).then_inc(sg("ln_mean"), 1)
                pe.wait_ge(sg("ln_square"), 1)
                for ch in range(NCHUNK):
                    if ch >= 2:
                        pe.wait_ge(sg("ln_log"), ch - 1)
                    mm(bank[6 + ch % 2], C("mean64"), SQ[:, BANK * ch:BANK * ch + BANK], start=True,
                       stop=True).then_inc(sg("ln_var"), 1)

            def call(m, n, d, c):
                raw = raws[d]

                def W(name):
                    a, b = Ws[name]
                    return raw[:, a:b]
                pe.wait_ge(sg("squared"), c + 1)
                for ch in range(NCHUNK):
                    if ch >= 2:
                        pe.wait_ge(sg("norm_log"), c * 8 + ch - 1)
                    mm(bank[6 + ch % 2], C("mean64"), SQ[:, BANK * ch:BANK * ch + BANK], start=True,
                       stop=True).then_inc(sg("norm_ms"), 1)
                pe.wait_ge(sg(f"block_weights_loaded{d}"), (m * 2 + n) * 16 + 16)
                pe.wait_ge(sg("normed"), c + 1)
                for hq in range(2):
                    for g in range(4):
                        if d == 0:
                            cols = XN3[:, 16 * g:16 * g + 16, 32 * hq:32 * hq + 32].rearrange("p i j -> p j i")
                        else:
                            cols = XN3[:, 32 * hq:32 * hq + 32, 16 * g:16 * g + 16]
                        last = mm(bank[4 + hq][32 * g:32 * g + 32, :], W("wdt"), cols, start=True, stop=True,
                                  tile_position=(0, 32 * g))
                last.then_inc(sg("dt_psum"), 1)
                for ch in range(NCHUNK):
                    for hd in range(2):
                        i = 2 * ch + hd
                        if i >= 2:
                            pe.wait_ge(sg("z_ready"), c * 16 + i - 1)
                        mm(bank[6 + i % 2], W(f"wz{hd}"), XN[:, BANK * ch:BANK * ch + BANK], start=True,
                           stop=True).then_inc(sg("z_psum"), 1)
                pe.wait_ge(sg("folded"), c + 1)
                pe.wait_ge(sg("dt_added"), c + 1)
                pe.wait_ge(sg("z_ready"), c * 16 + 16)

                def step(tau, T, known, q0=None):
                    if part_of(known, 0):
                        p = tau % 2
                        pe.wait_ge(sg("staged_straight"), T + (tau + 1))
                        pe.wait_ge(sg("staged_shifted"), T + (tau + 1))
                        if later(known, 0, 2):
                            pe.wait_ge(sg("x_ready"), T + (tau - 1))
                            pe.wait_ge(sg("bc_ready"), T + (tau - 1))
                            pe.wait_ge(sg("a_ready"), T + (tau - 1))
                        mm(bank[p][:, 0:144], DTB[p], W("seldt_bx"), start=True, stop=False, skip_group_check=True)
                        mm(bank[p][:, PX], SA[p], wxa, start=False, stop=False, skip_group_check=True)
                        mm(bank[p][:, PX], SB[p], wxb, start=False, stop=True, skip_group_check=True)
                        for t, src in ((0, SA[p]), (1, SB[p])):
                            for j in range(4):
                                last = mm(bank[p][32 * j:32 * j + 32, PBC], wbc[t][:, 32 * j:32 * j + 32],
                                          src[:, L * (j % 2):L * (j % 2) + L], start=(t == 0), stop=(t == 1),
                                          tile_position=(0, 32 * j), skip_group_check=True)
                        last.then_inc(sg("projected"), 1)
                    if part_of(known, -1):
                        p = (tau - 1) % 2
                        pe.wait_ge(sg("bc_ready"), T + tau)
                        pe.wait_ge(sg("am0_ready"), T + tau)
                        pe.wait_ge(sg("am1_ready"), T + tau)
                        if later(known, -1, 2):
                            pe.wait_ge(sg("gm_ready"), T + (tau - 2))
                            pe.wait_ge(sg("decay_ready"), T + (tau - 2))
                        for b in range(NB):
                            last = mm(bank[2 + p][64 * b:64 * b + 64, :], C("between"), AM[p][b], start=True,
                                      stop=True, tile_position=(0, 64 * b), skip_group_check=True)
                        last.then_inc(sg("decay_logs"), 1)
                        if later(known, -1, 2):
                            pe.wait_ge(sg("gated"), T + (tau - 2))
                        for j in range(4):
                            last = mm(bank[4 + p][32 * j:32 * j + 32, 128:192], BB[p][:, 32 * j:32 * j + 32], C2[p], start=True, stop=True,
                                      tile_position=(0, 32 * j), skip_group_check=True)
                        last.then_inc(sg("scored"), 1)
                    if part_of(known, -2):
                        p, r = (tau - 2) % 2, (tau - 2) % 4
                        y = bank[4 + p][:, 0:128]
                        pe.wait_ge(sg("xb_ready"), T + (tau - 1))
                        pe.wait_ge(sg("mixed"), T + (tau - 1))
                        for hd in range(2):
                            for xs, by, first_ in ((X2[r], Dhalf, True), (XB[r], MM[p], False)):
                                for h4 in range(4):
                                    h = 4 * hd + h4
                                    last = mm(y[32 * h4:32 * h4 + 32, 64 * hd:64 * hd + 64],
                                              xs[:, 32 * h:32 * h + 32], by[:, 64 * h:64 * h + 64],
                                              start=first_, stop=not first_, tile_position=(0, 32 * h4),
                                              skip_group_check=True)
                        last.then_inc(sg("y_psum"), 1)
                    if part_of(known, -4):
                        p = tau % 2
                        pe.wait_ge(sg("gated_squared"), T + (tau - 3))
                        if later(known, -4, 2):
                            pe.wait_ge(sg("tile_stored"), T + (tau - 5))
                        for at, ws_, src in ((0, wog, YZ[tau % 4]), (64, [C("ssum")] * 2, YQ[p])):
                            for hd, w_ in enumerate(ws_):
                                for j in range(4):
                                    last = mm(bank[6 + p][32 * j:32 * j + 32, at:at + 64],
                                              w_[:, 32 * j:32 * j + 32], src[:, 64 * hd:64 * hd + 64],
                                              start=(hd == 0), stop=(hd == 1), tile_position=(0, 32 * j),
                                              skip_group_check=True)
                        last.then_inc(sg("out_psum"), 1)

                tiles(pe, c, 0, L + 4, step)

            turn_in()
            groupnorm(0)
            stage0()
            groupnorm(1)
            stage1()
            rounds(pe, lambda m: groupnorm(m + 2), call, lambda m: None)
            turn_out()

        @block.scalar
        def _(act):
            A = nc.scalar.activation

            def groupnorm(g):
                act.wait_ge(sg("gn_centre"), g + 1)
                A(SQ, X, ACT.Square, bias=small[:, 1:2], accum_out=small[:, 2:3]).then_inc(sg("gn_square"), 1)
                act.wait_ge(sg("gn_var"), g + 1)
                A(small[:, 3:4], bank[7][:, 8:9], ACT.Ln, bias=C("eps5")).then_inc(sg("gn_log"), 1)
                act.wait_ge(sg("gn_log"), g + 1)
                A(small[:, 4:5], small[:, 3:4], ACT.Exp, scale=-0.5).then_inc(sg("gn_scale"), 1)

            def softplus_exp(prefix, v, w, base):
                act.wait_ge(sg(prefix + "_added"), base + 1)
                A(w, v, ACT.Abs).then_inc(sg(prefix + "_abs"), 1)
                act.wait_ge(sg(prefix + "_abs"), base + 1)
                A(w, w, ACT.Exp, scale=-1.0).then_inc(sg(prefix + "_exp"), 1)

            act.wait_ge(sg("constants_loaded"), 16)
            for k in range(1, 8, 2):
                act.wait_ge(sg("in_turned"), k + 1)
                A(X[:, BANK * k:BANK * k + BANK], bank[k], ACT.Copy).then_inc(sg("x_placed"), 1)
            groupnorm(0)
            act.wait_ge(sg("stage0_dve"), DVE0.index("neg") + 1)
            A(SQ[0:16, 1344:1360], SQ[0:16, 1344:1360], ACT.Exp, bias=small[0:16, 9:10],
              accum_out=small[0:16, 10:11]).then_inc(sg("stage0_act"), 1)
            act.wait_ge(sg("stage0_dve"), DVE0.index("neg2") + 1)
            A(SQ[:, 1856:1872], SQ[:, 1856:1872], ACT.Exp, bias=small[:, 13:14],
              accum_out=small[:, 14:15]).then_inc(sg("stage0_act"), 1)
            groupnorm(1)

            act.wait_ge(sg("stage1_weights_loaded"), 32)
            negA, hb = small[:, 32:48], small[:, 48:49]
            act.wait_ge(sg("s1_alog"), 1)
            A(negA, negA, ACT.Exp).then_inc(sg("s1_expA"), 1)
            act.wait_ge(sg("s1_consts"), 1)
            t, dt = SQ[:, 1536:2048], SQ[:, 3584:4096]
            w0_, w1_, w2_ = SS[:, 0:512], SS[:, 512:1024], SS[:, 1024:1536]
            dA = [SS[:, 2048 + 512 * i:2560 + 512 * i].rearrange("p (s l) -> p s l", l=L) for i in range(2)]
            with act.Fori(0, NK1) as k:
                act.wait_ge(sg("s1_front"), k + 1)
                A(t, bank[0], ACT.Tanh, bias=hb, scale=0.5).then_inc(sg("s1_tanh"), 1)
                A(w0_, bank[1], ACT.Tanh, scale=0.5).then_inc(sg("s1_tanhz"), 1)
                act.wait_ge(sg("s1_mid"), k + 1)
                A(parts[32:64, :], mid[0:32, :], ACT.Copy).then_inc(sg("s1_split_mid"), 1)
                act.wait_ge(sg("s1_z"), k + 1)
                softplus_exp("s1dt", dt, w0_, k)
                act.wait_ge(sg("s1dt_ready"), k + 1)
                s0 = act.snap(k * S1)
                for s in range(S1):
                    if s >= 2:
                        act.wait_ge(sg("s1_h"), s0 + (s - 1))
                    A(dA[s % 2][:, :, 1:L], dt.rearrange("p (s l) -> p s l", l=L)[:, :, 1:L], ACT.Exp,
                      scale=negA[:, s:s + 1]).then_inc(sg("s1_dA"), 1)
                act.wait_ge(sg("s1_out"), k + 1)
                A(O3[:, :, bass.ds(k * J1, J1)].rearrange("p i j -> p j i"),
                  bank[2][:, 0:256].rearrange("p (j i) -> p j i", i=L), ACT.Copy).then_inc(sg("s1_stored"), 1)
            act.wait_ge(sg("ln_centred"), NCHUNK)
            A(SQ, O, ACT.Square).then_inc(sg("ln_square"), 1)
            for ch in range(NCHUNK):
                act.wait_ge(sg("ln_var"), ch + 1)
                A(SS[:, BANK * ch:BANK * ch + BANK], bank[6 + ch % 2], ACT.Ln, bias=C("eps5")).then_inc(
                    sg("ln_log"), 1)
            act.wait_ge(sg("ln_log"), NCHUNK)
            A(SS, SS, ACT.Exp, scale=-0.5).then_inc(sg("ln_scale"), 1)

            def call(m, n, d, c):
                raw = raws[d]
                act.wait_ge(sg(f"block_weights_loaded{d}"), (m * 2 + n) * 16 + 16)
                act.wait_ge(sg("y_ready"), y_value(m, n, d))

                def W(name):
                    a, b = Ws[name]
                    return raw[:, a:b]
                A(expA, W("alog"), ACT.Exp).then_inc(sg("expA_ready"), 1)
                A(SQ, Y, ACT.Square).then_inc(sg("squared"), 1)
                for ch in range(NCHUNK):
                    act.wait_ge(sg("norm_ms"), c * 8 + (ch + 1))
                    A(O[:, BANK * ch:BANK * ch + BANK], bank[6 + ch % 2], ACT.Ln, bias=C("eps6")).then_inc(
                        sg("norm_log"), 1)
                act.wait_ge(sg("norm_log"), c * 8 + 8)
                A(O, O, ACT.Exp, scale=-0.5).then_inc(sg("norm_scale"), 1)
                softplus_exp("dt", DT, dtw[0], c)
                for i in range(16):
                    act.wait_ge(sg("z_psum"), c * 16 + (i + 1))
                    if i >= 2:
                        act.wait_ge(sg("z_ready"), c * 16 + (i - 1))
                    A(tz[i % 2], bank[6 + i % 2], ACT.Tanh, scale=0.5).then_inc(sg("z_tanh"), 1)

                act.wait_ge(sg("normed"), c + 1)
                act.wait_ge(sg("folded"), c + 1)
                act.wait_ge(sg("zeroed"), 1)

                def stage(t, T, q, free):
                    if free:
                        act.wait_ge(sg("projected"), T + (t - 1))
                    s = SA[t % 2]
                    src = axis(XN3, d, q).rearrange("p i j -> p (i j)")
                    A(s[0:64, 0:L], src[0:64, :], ACT.Copy)
                    A(s[64:128, L + 1:2 * L], src[64:128, 0:L - 1], ACT.Copy).then_inc(sg("staged_own"), 1)

                def step(tau, T, known, q0=None):
                    if part_of(known, 0):
                        p = tau % 2
                        act.wait_ge(sg("projected"), T + (tau + 1))
                        if later(known, 0, 2):
                            act.wait_ge(sg("x_ready"), T + (tau - 1))
                            act.wait_ge(sg("bc_ready"), T + (tau - 1))
                        A(TX[p][:, 128:192], bank[p][:, PBC], ACT.Tanh, bias=bbc_half, scale=0.5)
                        A(UB[p], bank[p][:, PBC], ACT.Identity, bias=W("bbc"))
                        A(TX[p][:, 0:128], bank[p][:, PX], ACT.Tanh, scale=0.5).then_inc(sg("tanh_ready"), 1)
                    if part_of(known, 1):
                        q = (q0 + (tau + 1)) if known is None else tau + 1
                        stage(tau + 1, T, q, later(known, 1, 2))
                    if part_of(known, -1):
                        p = (tau - 1) % 2
                        act.wait_ge(sg("decay_logs"), T + tau)
                        if later(known, -1, 2):
                            act.wait_ge(sg("mixed"), T + (tau - 2))
                        A(DK[p], bank[2 + p], ACT.Exp).then_inc(sg("decay_ready"), 1)
                    if part_of(known, -3):
                        act.wait_ge(sg("gated"), T + (tau - 2))
                        if later(known, -3, 2):
                            act.wait_ge(sg("out_psum"), T + (tau - 4))
                        A(YQ[(tau - 3) % 2], YZ[(tau - 3) % 4], ACT.Square).then_inc(sg("gated_squared"), 1)
                    if part_of(known, -5):
                        p = (tau - 5) % 2
                        q = (q0 + (tau - 5)) if known is None else tau - 5
                        act.wait_ge(sg("out_psum"), T + (tau - 4))
                        src = bank[6 + p][:, 0:128].rearrange("p (k l) -> p k l", k=2)
                        if d == 0:
                            A(O3[:, :, bass.ds(q, 1)], src[:, 0, :].unsqueeze(2), ACT.Copy)
                            A(SS3[:, :, bass.ds(q, 1)], src[:, 1, :].unsqueeze(2), ACT.Copy).then_inc(
                                sg("tile_stored"), 1)
                        else:
                            A(O3[:, bass.ds(q, 1), :], src[:, 0, :].unsqueeze(1), ACT.Copy)
                            A(SS3[:, bass.ds(q, 1), :], src[:, 1, :].unsqueeze(1), ACT.Copy).then_inc(
                                sg("tile_stored"), 1)

                tiles(act, c, -1, L + 5, step, lead=1)
                act.wait_ge(sg("tile_stored"), c * L + L)
                A(SS, SS, ACT.Ln, bias=C("eps6x4")).then_inc(sg("gate_log"), 1)
                act.wait_ge(sg("gate_log"), c + 1)
                A(SS, SS, ACT.Exp, scale=-0.5).then_inc(sg("gate_scale"), 1)

            rounds(act, lambda m: groupnorm(m + 2), call, lambda m: None)
            for k in range(1, 8, 2):
                act.wait_ge(sg("out_in_psum"), k + 1)
                A(O[:, BANK * k:BANK * k + BANK], bank[k], ACT.Copy).then_inc(sg("out_turned"), 1)

        @block.gpsimd
        def _(pool):
            g = nc.gpsimd
            pool.wait_ge(sg("constants_loaded"), 16)
            hc = [Y[:, 512 * i:512 * i + 512] for i in range(2)]
            acc = Y[:, 1024:1536]
            with pool.Fori(0, NK1) as k:
                s0 = pool.snap(k * S1)
                for s in range(S1):
                    pool.wait_ge(sg("s1_hc"), s0 + (s + 1))
                    if s == 0:
                        g.tensor_tensor(acc, hc[0], C("ones")[:, 0:1].broadcast_to([128, 512]), ALU.mult).then_inc(sg("s1_acc"), 1)
                    else:
                        pool.wait_ge(sg("s1_acc"), s0 + s)
                        g.tensor_tensor(acc, acc, hc[s % 2], ALU.add).then_inc(sg("s1_acc"), 1)
            pool.wait_ge(sg("s1_out"), NK1)
            for t in SA + SB + BB + C2 + X2:
                last = g.memset(t, 0.0)
            last.then_inc(sg("zeroed"), 1)
            pool.wait_ge(sg("zeroed"), 1)

            def call(m, n, d, c):
                pool.wait_ge(sg("normed"), c + 1)
                pool.wait_ge(sg("dt_ready"), c + 1)
                pool.wait_ge(sg("folded"), c + 1)

                def stage(t, T, q, free):
                    p = t % 2
                    if free:
                        pool.wait_ge(sg("projected"), T + (t - 1))
                    pool.wait_ge(sg("staged_own"), T + (t + 1))
                    pool.wait_ge(sg("staged_shifted"), T + (t + 1))
                    a, later_ = (x_[p].rearrange("p (b l) -> p b l", l=L) for x_ in (SA, SB))
                    g.tensor_tensor(later_[:, :, 2:L], a[:, :, 0:L - 2],
                                    C("ones")[:, 0:1].unsqueeze(2).broadcast_to([128, 2, L - 2]), ALU.mult)
                    dtq = DT.rearrange("p (q l) -> p q l", l=16)[:, bass.ds(q, 1), :]
                    g.tensor_tensor(DTB[p].rearrange("p (k l) -> p k l", l=16), dtq.broadcast_to([128, 8, 16]),
                                    C("maskdt").unsqueeze(2).broadcast_to([128, 8, 16]), ALU.mult).then_inc(
                        sg("staged_straight"), 1)

                def step(tau, T, known, q0=None):
                    if part_of(known, 1):
                        q = (q0 + (tau + 1)) if known is None else tau + 1
                        stage(tau + 1, T, q, later(known, 1, 2))
                    if part_of(known, 0):
                        p, r = tau % 2, tau % 4
                        pool.wait_ge(sg("a_ready"), T + (tau + 1))
                        if later(known, 0, 2):
                            pool.wait_ge(sg("decay_logs"), T + (tau - 1))
                        g.tensor_tensor(AM[p][1].rearrange("p (h l) -> p h l", l=L),
                                        DA[p][:, 0:16].rearrange("p (h b) -> p h b", b=2)[:, :, 1:2].broadcast_to(
                                            [128, 8, L]),
                                        C("span").unsqueeze(1).broadcast_to([128, 8, L]), ALU.mult).then_inc(
                            sg("am1_ready"), 1)
                        pool.wait_ge(sg("x_ready"), T + (tau + 1))
                        if later(known, 0, 4):
                            pool.wait_ge(sg("y_psum"), T + (tau - 3))
                        g.tensor_tensor(XB[r].rearrange("p (n e) -> p n e", e=HP),
                                        X2[r].rearrange("p (n e) -> p n e", e=HP),
                                        DA[p][:, 16:32].unsqueeze(2).broadcast_to([128, 16, HP]),
                                        ALU.mult).then_inc(sg("xb_ready"), 1)

                tiles(pool, c, -1, L, step, lead=1)

            rounds(pool, lambda m: None, call, lambda m: None)

        @block.vector
        def _(dve):
            v = nc.vector
            for k in range(0, 8, 2):
                dve.wait_ge(sg("in_turned"), k + 1)
                v.tensor_copy(X[:, BANK * k:BANK * k + BANK], bank[k]).then_inc(sg("x_placed"), 1)
            dve.wait_ge(sg("x_placed"), 8)

            def groupnorm(g, dst, ready):
                v.tensor_reduce(small[:, 0:1], X, AX.X, ALU.add).then_inc(sg("gn_sum"), 1)
                dve.wait_ge(sg("gn_mean"), g + 1)
                v.tensor_scalar(small[:, 1:2], bank[7][:, 0:1], -1.0, None, ALU.mult).then_inc(sg("gn_centre"), 1)
                dve.wait_ge(sg("gn_scale"), g + 1)
                v.tensor_scalar(dst, X, small[:, 1:2], small[:, 4:5], ALU.add, ALU.mult).then_inc(sg(ready), 1)

            groupnorm(0, XN, "xn0")

            n0 = [0]

            def done(ins, name):
                assert DVE0[n0[0]] == name
                n0[0] += 1
                ins.then_inc(sg("stage0_dve"), 1)

            def pe_did(name):
                dve.wait_ge(sg("stage0_pe"), PE0.index(name) + 1)

            def did(name):
                dve.wait_ge(sg("stage0_dve"), DVE0.index(name) + 1)
            order = Order(dve, "stage0_order")
            dve.wait_ge(sg("xn0"), 1)
            done(v.tensor_reduce(SQ[:, 0:1024], XN.rearrange("p (n f) -> p n f", f=4), AX.X, ALU.add), "xj")
            pe_did("xp")
            dve.wait_ge(sg("stage0_weights_loaded"), 32)
            xpT, xpre = SQ[:, 1024:1280], SQ[:, 1280:1312]
            done(v.tensor_copy(xpT, bank[0][:, 0:256]), "xp")
            did("xp")
            order(v.tensor_reduce(xpre, xpT.rearrange("p (n f) -> p n f", f=8), AX.X, ALU.add))
            done(v.tensor_scalar(xpre, xpre, 0.125, None, ALU.mult), "xpre")
            pe_did("qk")
            v.tensor_scalar(SQ[0:64, 1312:1328], bank[1][0:64, 0:16], W0("gqb", 64), None, ALU.add)
            done(v.tensor_scalar(SQ[0:64, 1328:1344], bank[1][0:64, 16:32], W0("gkb", 64), None, ALU.add), "qk")

            def softmax(tile, src, mask, cols, names):
                parts = tile.shape[0]
                mx, ng, sm, rc = (small[0:parts, cols + i:cols + i + 1] for i in range(4))
                done(v.tensor_tensor(tile, src, mask, ALU.add), names[0])
                did(names[0])
                order(v.tensor_reduce(mx, tile, AX.X, ALU.max))
                done(v.tensor_scalar(ng, mx, -1.0, None, ALU.mult), names[1])
                dve.wait_ge(sg("stage0_act"), ACT0.index(names[3]) + 1)
                order(v.reciprocal(rc, sm))
                done(v.tensor_scalar(tile, tile, rc, None, ALU.mult), names[2])
            pe_did("adj")
            softmax(SQ[0:16, 1344:1360], bank[2][0:16, 0:16], C("mask16", 16), 8, ("adj", "neg", "e1", "exp"))
            pe_did("adjT")
            done(v.tensor_copy(SQ[0:16, 1376:1392], bank[3][0:16, 0:16]), "adjT")
            pe_did("v")
            for ho in range(2):
                last = v.tensor_scalar(SQ[:, 1392 + 16 * ho:1408 + 16 * ho], bank[4][:, 16 * ho:16 * ho + 16],
                                       W0("gvb")[:, ho:ho + 1], None, ALU.add)
            done(last, "v")
            pe_did("support")
            done(v.tensor_copy(SQ[0:16, 1424:1680], bank[5][0:16, 0:256]), "support")
            pe_did("xpos")
            for ho in range(2):
                last = v.tensor_scalar(SQ[:, 1680 + 16 * ho:1696 + 16 * ho], bank[6][:, 16 * ho:16 * ho + 16],
                                       W0("gb")[:, ho:ho + 1], None, ALU.add)
            done(last, "xpos")
            pe_did("query")
            done(v.tensor_scalar(SQ[0:64, 1712:1728], bank[1][0:64, 0:16], W0("qb", 64), None, ALU.add), "query")
            pe_did("key")
            done(v.tensor_scalar(SQ[0:64, 1728:1856], bank[2][0:64, 0:128], W0("kb", 64), None, ALU.add), "key")
            pe_did("at")
            softmax(SQ[:, 1856:1872], bank[3][:, 0:16], C("maskbc"), 12, ("at", "neg2", "e2", "exp2"))
            pe_did("atT")
            done(v.tensor_copy(SQ[0:16, 1888:2016], bank[4][0:16, 0:128]), "atT")
            pe_did("val")
            done(v.tensor_copy(SQ[0:16, 2016:2272], bank[5][0:16, 0:256]), "val")
            pe_did("y")
            done(v.tensor_copy(SQ[:, 2272:2528], bank[6][:, 0:256]), "y")
            pe_did("z")
            Z = SS[:, 0:1024].rearrange("p (i h) -> p i h", h=16)
            D = SS[:, 1024:2048].rearrange("p (i h) -> p i h", h=16)
            Zv = SS[:, 0:1024].rearrange("p (n h) -> p n h", h=4)
            for hlo in range(4):
                last = v.tensor_copy(Zv[:, :, hlo], bank[hlo // 2][:, 256 * (hlo % 2):256 * (hlo % 2) + 256])
            done(last, "z")
            did("z")
            order(v.tensor_tensor(D[:, :, 0:15], Z[:, :, 1:16], Z[:, :, 0:15], ALU.subtract))
            up = O3[:, :, 0:63].rearrange("p i (a r) -> p i a r", a=3)
            wy = C("wy")[:, 0:63].rearrange("p (a r) -> p a r", a=3)
            D5 = D[:, :, 0:15].rearrange("p i (a k) -> p i a k", a=3)
            Z5 = Z[:, :, 0:15].rearrange("p i (a k) -> p i a k", a=3)
            dve.wait_ge(sg("in_turned"), 8)
            for k in range(5):
                rs = [r for r in range(21) if 5 * r // 21 == k]
                a, b = rs[0], rs[-1] + 1
                for ph in range(3):
                    d_ = D5[:, :, ph, k].unsqueeze(2).broadcast_to([128, L, b - a])
                    z_ = Z5[:, :, ph, k].unsqueeze(2).broadcast_to([128, L, b - a])
                    w_ = wy[:, ph, a:b].unsqueeze(1).broadcast_to([128, L, b - a])
                    order(v.tensor_tensor(up[:, :, ph, a:b], d_, w_, ALU.mult))
                    order(v.tensor_tensor(up[:, :, ph, a:b], up[:, :, ph, a:b], z_, ALU.add))
            order(v.tensor_copy(O3[:, :, 63:64], Z[:, :, 15:16]))
            order(v.tensor_tensor(X, X, O, ALU.add))
            groupnorm(1, XN, "xn1")
            dve.wait_ge(sg("xn1"), 1)

            dve.wait_ge(sg("stage1_weights_loaded"), 32)
            negA, hb = small[:, 32:48], small[:, 48:49]
            st = SQ[:, 0:SEQ1 * PADL].rearrange("p (s l) -> p s l", l=PADL)
            vv, t, u, z2, xd, dt = (SQ[:, 1024 + 512 * i:1536 + 512 * i] for i in range(6))
            w0_, w1_, w2_, dtu = (SS[:, 512 * i:512 * i + 512] for i in range(4))
            dA = [SS[:, 2048 + 512 * i:2560 + 512 * i] for i in range(2)]
            dbu = [SS[:, 3072 + 512 * i:3584 + 512 * i] for i in range(2)]
            hs = [work[:, 1536 + 512 * i:2048 + 512 * i] for i in range(2)]
            yz = work[:, 1024:1536]
            hc = [Y[:, 512 * i:512 * i + 512] for i in range(2)]
            acc = Y[:, 1024:1536]
            order = Order(dve, "s1_setup")
            v.tensor_scalar(negA, W1("alog"), 80.0, None, ALU.min).then_inc(sg("s1_alog"), 1)
            dve.wait_ge(sg("s1_expA"), 1)
            order(v.tensor_scalar(negA, negA, -1.0, None, ALU.mult))
            order(v.tensor_tensor(W1("winx_b"), W1("winx_a"), W1("wcb"), ALU.mult))
            order(v.tensor_tensor(W1("winx_a"), W1("winx_a"), W1("wca"), ALU.mult))
            v.tensor_copy(selBC, stateS).then_inc(sg("s1_selectors"), 1)
            v.memset(SQ[:, 0:SEQ1 * PADL], 0.0)
            v.memset(SS[:, 2048:3072], 0.0)
            order(v.tensor_scalar(hb, W1("bconv"), 0.5, None, ALU.mult))
            v.tensor_scalar(small[:, 49:50], hb, 1.0, None, ALU.mult).then_inc(sg("s1_consts"), 1)

            def softplus(prefix, base, x, e, r, y, ready, order):
                dve.wait_ge(sg(prefix + "_exp"), base + 1)
                order(v.tensor_scalar(r, e, 2.0, None, ALU.add))
                order(v.reciprocal(r, r))
                order(v.tensor_tensor(r, r, e, ALU.mult))
                order(v.tensor_tensor(y, r, r, ALU.mult))
                order(v.tensor_scalar(e, y, LOG1P[4], None, ALU.mult))
                for i in (3, 2, 1):
                    order(v.scalar_tensor_tensor(e, e, LOG1P[i], y, ALU.add, ALU.mult))
                order(v.scalar_tensor_tensor(e, e, LOG1P[0], r, ALU.add, ALU.mult))
                v.scalar_tensor_tensor(x, x, 0.0, e, ALU.max, ALU.add).then_inc(sg(ready), 1)

            with dve.Fori(0, NK1) as k:
                order = Order(dve, "s1_order", dve.snap(k * 14))
                cols = XN3[:, :, bass.ds(k * J1, J1)].rearrange("p i j -> p j i")
                for tp in range(2):
                    for b in range(NB):
                        last = v.tensor_copy(st[64 * tp:64 * tp + 64, J1 * b:J1 * b + J1, 3 + tp:3 + L],
                                             cols[64 * b:64 * b + 64, :, 0:L - tp])
                last.then_inc(sg("s1_staged"), 1)
                dve.wait_ge(sg("s1_front"), k + 1)
                dve.wait_ge(sg("s1_tanh"), k + 1)
                order(v.tensor_scalar(vv, bank[0], W1("bconv"), 0.5, ALU.add, ALU.mult))
                v.scalar_tensor_tensor(u, t, 1.0, vv, ALU.add, ALU.mult).then_inc(sg("s1_u"), 1)
                dve.wait_ge(sg("s1_tanhz"), k + 1)
                v.scalar_tensor_tensor(z2, w0_, 1.0, bank[1], ALU.add, ALU.mult).then_inc(sg("s1_z"), 1)
                dve.wait_ge(sg("s1_dbl"), k + 1)
                v.tensor_copy(xd[32:64, :], bank[2][32:64, :]).then_inc(sg("s1_xd"), 1)
                order(v.tensor_copy(parts[0:32, :], bank[2][0:32, :]))
                order(v.tensor_tensor(rest[0:32, :], bank[2][0:32, :], parts[0:32, :], ALU.subtract))
                v.tensor_copy(mid[0:32, :], rest[0:32, :]).then_inc(sg("s1_mid"), 1)
                dve.wait_ge(sg("s1_mid"), k + 1)
                v.tensor_tensor(parts[64:96, :], rest[0:32, :], mid[0:32, :], ALU.subtract).then_inc(
                    sg("s1_split"), 1)
                dve.wait_ge(sg("s1_dtp"), k + 1)
                v.tensor_scalar(dt, bank[3], W1("bdt"), None, ALU.add).then_inc(sg("s1dt_added"), 1)
                softplus("s1dt", k, dt, w0_, w1_, w2_, "s1dt_ready", order)
                dve.wait_ge(sg("s1dt_ready"), k + 1)
                order(v.tensor_tensor(dtu, dt, u, ALU.mult))
                s0 = dve.snap(k * S1)
                for s in range(-1, S1 + 1):
                    if s + 1 < S1:
                        dve.wait_ge(sg("s1_B"), s0 + (s + 2))
                        if s >= 1:
                            dve.wait_ge(sg("s1_h"), s0 + s)
                        v.tensor_tensor(dbu[(s + 1) % 2], dtu, bank[4 + (s + 1) % 2], ALU.mult).then_inc(
                            sg("s1_dbu"), 1)
                    if 0 <= s < S1:
                        dve.wait_ge(sg("s1_dbu"), s0 + (s + 1))
                        dve.wait_ge(sg("s1_dA"), s0 + (s + 1))
                        if s >= 2:
                            dve.wait_ge(sg("s1_hc"), s0 + (s - 1))
                        v.tensor_tensor_scan(hs[s % 2], dA[s % 2], dbu[s % 2], 0.0, ALU.mult, ALU.add).then_inc(
                            sg("s1_h"), 1)
                    if s >= 1:
                        dve.wait_ge(sg("s1_h"), s0 + s)
                        dve.wait_ge(sg("s1_C"), s0 + s)
                        if s >= 3:
                            dve.wait_ge(sg("s1_acc"), s0 + (s - 2))
                        v.tensor_tensor(hc[(s - 1) % 2], hs[(s - 1) % 2], bank[6 + (s - 1) % 2],
                                        ALU.mult).then_inc(sg("s1_hc"), 1)
                dve.wait_ge(sg("s1_acc"), s0 + S1)
                order(v.scalar_tensor_tensor(vv, u, W1("dp"), acc, ALU.mult, ALU.add))
                v.scalar_tensor_tensor(yz, vv, 0.5, z2, ALU.mult, ALU.mult).then_inc(sg("s1_gated"), 1)
            for ch in range(NCHUNK):
                dve.wait_ge(sg("ln_mean"), ch + 1)
                o = O[:, BANK * ch:BANK * ch + BANK]
                v.tensor_tensor(o, o, bank[6 + ch % 2], ALU.subtract).then_inc(sg("ln_centred"), 1)
            dve.wait_ge(sg("ln_centred"), NCHUNK)
            dve.wait_ge(sg("ln_scale"), 1)
            order = Order(dve, "ln_order")
            order(v.scalar_tensor_tensor(O, O, W1("gamma"), SS, ALU.mult, ALU.mult))
            order(v.scalar_tensor_tensor(X, O, W1("beta"), X, ALU.add, ALU.add))

            def call(m, n, d, c):
                raw = raws[d]

                def W(name):
                    a, b = Ws[name]
                    return raw[:, a:b]
                dve.wait_ge(sg("zeroed"), 1)
                dve.wait_ge(sg(f"block_weights_loaded{d}"), (m * 2 + n) * 16 + 16)
                v.tensor_tensor(wxa, W("wx"), W("cxa"), ALU.mult)
                v.tensor_tensor(wxb, W("wx"), W("cxb"), ALU.mult)
                for tp, cw in ((0, "cbca"), (1, "cbcb")):
                    v.tensor_tensor(wbc[tp], W("wbc"), W(cw), ALU.mult)
                for hd in range(2):
                    v.tensor_scalar(wog[hd], W(f"wo{hd}"), W("gnw")[:, hd:hd + 1], None, ALU.mult)
                v.tensor_scalar(bbc_half, W("bbc"), 0.5, None, ALU.mult)
                v.scalar_tensor_tensor(Dhalf.rearrange("p (h l) -> p h l", l=L),
                                       W("dh").unsqueeze(2).broadcast_to([128, 8, L]), 0.5,
                                       C("stack").unsqueeze(1).broadcast_to([128, 8, L]), ALU.mult,
                                       ALU.mult).then_inc(sg("folded"), 1)
                dve.wait_ge(sg("norm_scale"), c + 1)
                dve.wait_ge(sg("y_ready"), y_value(m, n, d))
                v.scalar_tensor_tensor(XN, Y, W("nw"), O, ALU.mult, ALU.mult).then_inc(sg("normed"), 1)
                dve.wait_ge(sg("dt_psum"), c + 1)
                for hq in range(2):
                    last = v.tensor_scalar(DT[:, 512 * hq:512 * hq + 512], bank[4 + hq], W("bdt"), None, ALU.add)
                last.then_inc(sg("dt_added"), 1)
                order = Order(dve, "block_order", dve.snap(c * 10))
                softplus("dt", c, DT, dtw[0], dtw[1], dtw[2], "dt_positive", order)
                dve.wait_ge(sg("dt_positive"), c + 1)
                v.tensor_scalar(DT, DT, C("dtrow")[:, 0:1], C("dtrow")[:, 1:2], ALU.mult, ALU.add).then_inc(
                    sg("dt_ready"), 1)
                dve.wait_ge(sg("normed"), c + 1)
                for i in range(16):
                    ch, hd = i // 2, i % 2
                    dve.wait_ge(sg("z_tanh"), c * 16 + (i + 1))
                    v.scalar_tensor_tensor(Z2[:, TOK * hd + BANK * ch:TOK * hd + BANK * ch + BANK], tz[i % 2], 1.0,
                                           bank[6 + i % 2], ALU.add, ALU.mult).then_inc(sg("z_ready"), 1)
                dve.wait_ge(sg("expA_ready"), c + 1)
                dve.wait_ge(sg("z_ready"), c * 16 + 16)

                def stage(t, T, q, free):
                    if free:
                        dve.wait_ge(sg("projected"), T + (t - 1))
                    s = SA[t % 2]
                    src = axis(XN3, d, q).rearrange("p i j -> p (i j)")
                    v.tensor_copy(s[64:128, 1:L], src[0:64, 0:L - 1])
                    v.tensor_copy(s[0:64, L:2 * L], src[64:128, :]).then_inc(sg("staged_shifted"), 1)

                def step(tau, T, known, q0=None):
                    if part_of(known, 1):
                        q = (q0 + (tau + 1)) if known is None else tau + 1
                        stage(tau + 1, T, q, later(known, 1, 2))
                    if part_of(known, 0):
                        p, r = tau % 2, tau % 4
                        dve.wait_ge(sg("tanh_ready"), T + (tau + 1))
                        if later(known, 0, 2):
                            dve.wait_ge(sg("am1_ready"), T + (tau - 1))
                            dve.wait_ge(sg("am0_ready"), T + (tau - 1))
                            dve.wait_ge(sg("xb_ready"), T + (tau - 1))
                        v.tensor_scalar(DA[p][:, 16:32], bank[p][:, PDT], 0.125, None, ALU.mult)
                        v.scalar_tensor_tensor(DA[p][:, 0:16], bank[p][:, PDT], -1.0, expA, ALU.mult,
                                               ALU.mult).then_inc(sg("a_ready"), 1)
                        if later(known, 0, 4):
                            dve.wait_ge(sg("y_psum"), T + (tau - 3))
                        for b in range(NB):
                            h = slice(64 * b, 64 * b + 64)
                            last = v.scalar_tensor_tensor(
                                X2[r].rearrange("p (h b e) -> p h b e", b=2, e=HP)[h, :, b, :],
                                TX[p][h, 0:128].rearrange("p (h e) -> p h e", e=HP), 1.0,
                                bank[p][h, PX].rearrange("p (h e) -> p h e", e=HP), ALU.add, ALU.mult)
                        last.then_inc(sg("x_ready"), 1)
                        if later(known, 0, 2):
                            dve.wait_ge(sg("scored"), T + (tau - 1))
                        bc, tb = UB[p], TX[p][:, 128:192]
                        for b in range(NB):
                            h = slice(32 * b, 32 * b + 32)
                            v.scalar_tensor_tensor(BB[p][h, 64 * b:64 * b + 64], tb[h, :], 1.0, bc[h, :], ALU.add,
                                                   ALU.mult)
                        v.scalar_tensor_tensor(C2[p][0:64, :], tb[64:128, :], 1.0, bc[64:128, :], ALU.add,
                                               ALU.mult).then_inc(sg("bc_ready"), 1)
                        dve.wait_ge(sg("a_ready"), T + (tau + 1))
                        v.tensor_tensor(AM[p][0].rearrange("p (h l) -> p h l", l=L),
                                        DA[p][:, 0:16].rearrange("p (h b) -> p h b", b=2)[:, :, 0:1].broadcast_to(
                                            [128, 8, L]),
                                        C("span").unsqueeze(1).broadcast_to([128, 8, L]), ALU.mult).then_inc(
                            sg("am0_ready"), 1)
                    if part_of(known, -1):
                        p = (tau - 1) % 2
                        dve.wait_ge(sg("scored"), T + tau)
                        v.tensor_tensor(GM[p], bank[4 + p][:, 128:192], C("diag2"), ALU.mult).then_inc(
                            sg("gm_ready"), 1)
                        dve.wait_ge(sg("gm_ready"), T + tau)
                        dve.wait_ge(sg("decay_ready"), T + tau)
                        if later(known, -1, 2):
                            dve.wait_ge(sg("y_psum"), T + (tau - 2))
                        v.tensor_tensor(MM[p].rearrange("p (h l) -> p h l", l=L),
                                        DK[p].rearrange("p (h l) -> p h l", l=L),
                                        GM[p].unsqueeze(1).broadcast_to([128, 8, L]), ALU.mult).then_inc(
                            sg("mixed"), 1)
                    if part_of(known, -2):
                        p = (tau - 2) % 2
                        q = (q0 + (tau - 2)) if known is None else tau - 2
                        dve.wait_ge(sg("y_psum"), T + (tau - 1))
                        if later(known, -2, 4):
                            dve.wait_ge(sg("out_psum"), T + (tau - 5))
                        z = Z24[:, :, :, bass.ds(q, 1)] if d == 0 else Z24[:, :, bass.ds(q, 1), :]
                        z = z.rearrange("p h i j -> p h (i j)")
                        v.tensor_tensor(YZ[(tau - 2) % 4].rearrange("p (h l) -> p h l", l=L),
                                        bank[4 + p][:, 0:128].rearrange("p (h l) -> p h l", l=L), z,
                                        ALU.mult).then_inc(sg("gated"), 1)

                tiles(dve, c, -1, L + 2, step, lead=1)
                dve.wait_ge(sg("gate_scale"), c + 1)
                order(v.tensor_tensor(O, O, SS, ALU.mult))
                v.tensor_tensor(Y, Y, O, ALU.add).then_inc(sg("y_ready"), 1)
                dve.wait_ge(sg("y_ready"), y_value(m, n, d) + 1)
                v.tensor_copy(small[:, 60:61], small[:, 60:61]).then_inc(sg(f"block_done{d}"), 1)

            def entry(m):
                groupnorm(m + 2, Y, "y_ready")

            def leave(m):
                v.tensor_tensor(X, X, Y, ALU.add).then_inc(sg("x_added"), 1)
                dve.wait_ge(sg("x_added"), m + 1)

            v.memset(small[:, 60:61], 0.0)
            rounds(dve, entry, call, leave)
            v.tensor_copy(small[:, 61:62], X[:, 0:1]).then_inc(sg("x_final"), 1)
            for k in range(0, 8, 2):
                dve.wait_ge(sg("out_in_psum"), k + 1)
                v.tensor_copy(O[:, BANK * k:BANK * k + BANK], bank[k]).then_inc(sg("out_turned"), 1)


def _constants():
    import numpy as np
    p = np.arange(128)
    b, s = p // 64, p % 64
    l = np.arange(64)
    f = np.float32
    c = {}
    c["ident"] = np.eye(128)
    same = b[:, None] == b[None, :]
    c["mean64"] = same / 64.0
    c["pair"] = (p[:, None] // 2 == p[None, :] // 2) / (2.0 * TOK)
    bp = (p // 16) % 2
    c["ssum"] = (bp[:, None] == b[None, :]) / 128.0
    c["between"] = np.where(b[:, None] == 0, s[:, None] > l[None, :], s[:, None] < l[None, :])
    c["span"] = np.where(b[:, None] == 0, s[:, None] <= l[None, :], s[:, None] >= l[None, :])
    c["diag2"] = 1.0 + (s[:, None] == l[None, :])
    c["stack"] = s[:, None] == l[None, :]
    r = p % 32
    c["maskdt"] = (r[:, None] <= 16) & (p[:, None] // 32 == np.arange(8)[None, :] % 4)
    c["dtrow"] = np.stack([r < 16, r == 16], axis=1)
    k16 = np.arange(16) // 8
    c["mask16"] = np.where((p[:, None] // 8) == k16[None, :], 0.0, -1e30)
    c["maskbc"] = np.where(b[:, None] == k16[None, :], 0.0, -1e30)
    c["ones"] = np.ones((128, 128))
    c["eps6"], c["eps6x4"], c["eps5"] = (np.full((128, 1), e) for e in (1e-6, 4e-6, 1e-5))
    pos = np.linspace(0.0, 15.0, 64).astype(f)
    lo = (5 * l) // 21
    frac = (pos - lo).astype(f)
    wc = np.zeros((16, 64), f)
    wc[lo, l] += (1.0 - frac)
    wc[np.minimum(lo + 1, 15), l] += frac
    interp = np.zeros((4, 128, 128), f)
    for hlo in range(4):
        for bb in range(2):
            interp[hlo, 64 * bb + 16 * hlo:64 * bb + 16 * hlo + 16, 64 * bb:64 * bb + 64] = wc
    c["interp"] = interp.transpose(1, 0, 2).reshape(128, 512)
    c["wy"] = np.broadcast_to(frac, (128, 64))
    packed = np.concatenate([np.asarray(c[n], f).reshape(128, w) for n, w in CONST_COLS], axis=1)
    pool = np.zeros((2, 8, 128, 128), f)
    for bb in range(2):
        for jj in range(8):
            for ch in range(64):
                pool[bb, jj, 64 * bb + ch, 16 * jj + ch // 4] = 1.0 / 16.0
    pool = pool.reshape(16, 128, 128).transpose(1, 0, 2).reshape(128, 2048)
    state = np.zeros((128, 2, 16, 128), f)
    for k in range(16):
        state[[k, 32 + k, 64 + k], 0, k] = 1.0
        state[[16 + k, 48 + k, 80 + k], 1, k] = 1.0
    return packed, pool, state.reshape(128, 4096)


def _pack(cols, given):
    import numpy as np
    out = np.zeros((128, width(cols)), np.float32)
    at = spans(cols)
    for name, a in given.items():
        lo, hi = at[name]
        a = np.asarray(a)
        a = a[:, None] if a.ndim == 1 else a
        out[0:a.shape[0], lo:hi] = a
    return out


def _halves(wt):
    import numpy as np
    return np.concatenate([wt[0:128], wt[128:256]], axis=1)


def _stage0(w):
    g = {}
    for short, name in (("gq", "gcn_qw"), ("gk", "gcn_kw"), ("gv", "gcn_vw"), ("q", "qw"), ("k", "kw"), ("v", "vw")):
        g[short] = _halves(w[name].T)
    g["gw"] = _halves(w["gcn_weight"])
    g["gb"] = w["gcn_bias"].reshape(2, 128).T
    g["gvb"] = w["gcn_vb"].reshape(2, 128).T
    g["gqb"], g["gkb"], g["qb"], g["kb"] = w["gcn_qb"], w["gcn_kb"], w["qb"], w["kb"]
    g["vb"] = w["vb"][None, :]
    return _pack(L0_COLS, g)


def _stage1(w):
    import numpy as np
    g = {}
    win = w["W_in"].T
    g["winx_a"] = np.concatenate([win[:, 0:128]] * 2)
    taps = w["W_conv"][:, 0, :].T
    g["wca"] = np.concatenate([np.broadcast_to(taps[3], (64, 128)), np.broadcast_to(taps[2], (64, 128))])
    g["wcb"] = np.concatenate([np.broadcast_to(taps[1], (64, 128)), np.broadcast_to(taps[0], (64, 128))])
    g["wz"] = win[:, 128:256]
    wxp = np.zeros((128, 64), np.float32)
    wxp[:, 0:32] = w["W_xproj"][4:36].T
    wxp[:, 32:36] = w["W_xproj"][0:4].T
    g["wxp"] = wxp
    wdt = np.zeros((128, 128), np.float32)
    wdt[32:36] = w["W_dt"].T
    g["wdt"] = wdt
    g["bconv"], g["bdt"], g["alog"], g["dp"] = w["b_conv"], w["b_dt"], w["A_log"], w["D_param"]
    g["wout"] = w["W_out"].T
    g["gamma"], g["beta"] = np.concatenate([w["gamma"]] * 2), np.concatenate([w["beta"]] * 2)
    return _pack(L1_COLS, g)


def _block(norm_w, Win, Wconv, bconv, dt_bias, A_log, D, gn_w, Wout):
    import numpy as np
    g = {}
    g["wx"] = np.concatenate([Win[:, 128:256]] * 2)
    taps = Wconv.T

    def pair(k0, k1, row):
        return np.concatenate([np.broadcast_to(row[k0], (64, row.shape[1])),
                               np.broadcast_to(row[k1], (64, row.shape[1]))])
    g["cxa"], g["cxb"] = pair(3, 2, taps[:, 0:128]), pair(1, 0, taps[:, 0:128])
    spread = np.zeros((4, 2, 2, 32), np.float32)
    spread[:, :, :, 0:16] = taps[:, 128:160].reshape(4, 2, 1, 16)
    spread = spread.reshape(4, 128)
    g["cbca"], g["cbcb"] = pair(3, 2, spread), pair(1, 0, spread)
    wb = np.zeros((64, 2, 2, 32), np.float32)
    wb[..., 0:16] = Win[:, 256:288].reshape(64, 2, 1, 16)
    g["wbc"] = np.concatenate([wb.reshape(64, 128)] * 2)
    sel = np.zeros((4, 32, 144), np.float32)
    for h in range(8):
        for b in range(2):
            sel[:, 8 * b + h, 2 * h + b] = 1.0
    sel[:, 16, 16:144] = bconv[0:128]
    g["seldt_bx"] = sel.reshape(128, 144)
    bb = np.zeros((2, 2, 32), np.float32)
    bb[..., 0:16] = bconv[128:160].reshape(2, 1, 16)
    g["bbc"] = bb.reshape(128)
    for hd in range(2):
        wz = np.zeros((2, 64, 4, 2, 16), np.float32)
        wo = np.zeros((4, 2, 16, 2, 64), np.float32)
        for b in range(2):
            wz[b, :, :, b] = Win[:, 64 * hd:64 * hd + 64].reshape(64, 4, 16)
            wo[:, b, :, b] = Wout[64 * hd:64 * hd + 64].reshape(4, 16, 64)
        g[f"wz{hd}"], g[f"wo{hd}"] = wz.reshape(128, 128), wo.reshape(128, 128)
    wdt = np.zeros((2, 64, 32), np.float32)
    bdt = np.zeros((4, 32), np.float32)
    for b in range(2):
        wdt[b, :, 8 * b:8 * b + 8] = Win[:, 288:296]
        bdt[:, 8 * b:8 * b + 8] = dt_bias
    g["wdt"], g["bdt"] = wdt.reshape(128, 32), bdt.reshape(128)
    g["alog"], g["dh"] = np.broadcast_to(np.repeat(A_log, 2), (128, 16)), np.broadcast_to(D, (128, 8))
    g["nw"] = np.concatenate([norm_w] * 2)
    gw = gn_w.reshape(2, 4, 1, 16)
    g["gnw"] = np.broadcast_to(gw, (2, 4, 2, 16)).reshape(2, 128).T
    return _pack(CALL_COLS, g)


def kernel(**inputs):
    import numpy as np
    import concourse.bacc as bacc
    from concourse.bass_utils import run_bass_kernel_spmd

    a = {k: np.asarray(v) for k, v in inputs.items()}
    names = ("norm_w", "Win", "Wconv", "bconv", "dt_bias", "A_log", "D", "gn_w", "Wout")
    calls = [_block(*(a[f"L{st}_conv_{ax}_{n}"][i] for n in names))
             for st in (2, 3) for i in range(2) for ax in ("t", "b")]
    consts, pool_sel, state_sel = _constants()
    arrays = {
        "x": np.ascontiguousarray(a["x"]), "consts": consts, "pool_sel": pool_sel, "state_sel": state_sel,
        "l0w": _stage0({k[8:]: v for k, v in a.items() if k.startswith("L0_conv_")}),
        "l1w": _stage1({k[8:]: v for k, v in a.items() if k.startswith("L1_conv_")}),
        "callw": np.stack(calls),
    }
    nc = bacc.Bacc("TRN2", target_bir_lowering=False, num_devices=1)
    args = [nc.dram_tensor(k, v.shape, mybir.dt.float32, kind="ExternalInput").ap() for k, v in arrays.items()]
    out = nc.dram_tensor("out", (2, 64, 64, 64), mybir.dt.float32, kind="ExternalOutput").ap()
    program(nc, *args, out)
    r = run_bass_kernel_spmd(nc, [arrays], core_ids=[0])
    return r.results[0]["out"]
```

```python
from contextlib import ExitStack

import concourse.bass as bass
from concourse import mybir

F32 = mybir.dt.float32
BF16 = mybir.dt.bfloat16
ALU = mybir.AluOpType
ACT = mybir.ActivationFunctionType
AX = mybir.AxisListType

NB, L, CH = 2, 64, 64
P = NB * CH
TOK = L * L
BANK = 512
NCHUNK = TOK // BANK
NGROUP = L // 8
NH, HP, NS = 8, 16, 16
PADL = L + 3
S1 = 16
J1 = 4
NK1 = L // J1
SEQ1 = NB * J1
WORK = 6400
LAST1 = S1 + 2
LN_EXP = "natural_log_exp_and_others"
LOG1P = (2.00000000788, 0.666663159351, 0.400248537234, 0.279614188352, 0.281746572615)

CONST_COLS = [("ident", 128), ("mean64", 128), ("pair", 128), ("ssum", 128), ("between", 64),
              ("span", 64), ("diag2", 64), ("stack", 64), ("maskdt", 8), ("dtrow", 2), ("two", 1),
              ("mask16", 16), ("maskbc", 16), ("ones", 128), ("eps6", 1), ("eps6x4", 1), ("eps5", 1),
              ("interp", 512), ("wy", 64)]
CALL_COLS = [("wx", 128), ("cxa", 128), ("cxb", 128), ("wbc", 128), ("cbca", 128), ("cbcb", 128),
             ("seldt_bx", 144), ("bbc", 1), ("wz0", 128), ("wz1", 128), ("wdt", 32), ("bdt", 1), ("alog", 16),
             ("dh", 8),
             ("nw", 1), ("gnw", 2), ("wo0", 128), ("wo1", 128)]
L0_COLS = [("gq", 128), ("gk", 128), ("gv", 512), ("gw", 512), ("gb", 2), ("gqb", 1), ("gkb", 1), ("gvb", 2),
           ("q", 128), ("qb", 1), ("k", 128), ("kb", 1), ("v", 512), ("vb", 256)]
L1_COLS = [("winx_a", 128), ("winx_b", 128), ("wca", 128), ("wcb", 128), ("wz", 128), ("wxp", 64), ("wdt", 128), ("bconv", 1),
           ("bdt", 1), ("alog", 16), ("dp", 1), ("wout", 64), ("gamma", 1), ("beta", 1)]


def width(cols):
    return sum(n for _, n in cols)


def spans(cols):
    at, out = 0, {}
    for name, n in cols:
        out[name] = (at, at + n)
        at += n
    return out


def program(nc, x, consts, pool_sel, state_sel, l0w, l1w, callw, out):
    ctx = ExitStack()
    with ctx:
        sems = {}

        def sb(name, cols):
            return ctx.enter_context(nc.sbuf_tensor(name, [128, cols], F32))[:, :]

        def sg(name):
            if name not in sems:
                sems[name] = ctx.enter_context(nc.semaphore(name))
            return sems[name]

        class Order:

            def __init__(self, eng, name, base=0):
                self.eng, self.name, self.base, self.n = eng, name, base, 0

            def __call__(self, ins):
                self.n += 1
                ins.then_inc(sg(self.name), 1)
                self.eng.wait_ge(sg(self.name), self.base + self.n)

        bank = [ctx.enter_context(nc.psum_tensor(f"bank{i}", [128, BANK], F32))[:, :] for i in range(8)]

        X = sb("X", TOK)
        Y = sb("Y", TOK)
        XN = sb("XN", TOK)
        Z2 = sb("Z2", 2 * TOK)
        O = sb("O", TOK)
        SS = sb("SS", TOK)
        SQ = sb("SQ", TOK)
        cst = sb("constants", width(CONST_COLS))
        raws = [sb(f"block_weights{i}", width(CALL_COLS)) for i in range(2)]
        FW = sb("folded_weights", 1440)
        small = sb("small", 64)
        ring4 = sb("ring4", 4 * 512)
        work = sb("work", WORK)
        Cs, Ws, W0s, W1s = spans(CONST_COLS), spans(CALL_COLS), spans(L0_COLS), spans(L1_COLS)

        def C(name, parts=128):
            a, b = Cs[name]
            return cst[0:parts, a:b]

        ident = C("ident")
        XN3, O3, Y3 = (t.rearrange("p (i j) -> p i j", j=L) for t in (XN, O, Y))
        Z24 = Z2.rearrange("p (h i j) -> p h i j", h=2, j=L)

        def axis(t3, direction, q):
            return t3[:, :, bass.ds(q, 1)] if direction == 0 else t3[:, bass.ds(q, 1), :]

        def axis_group(t3, direction, q):
            if direction == 0:
                return t3[:, :, bass.ds(q, 8)], lambda t: t.rearrange("p (i j) -> p i j", j=8)
            return t3[:, bass.ds(q, 8), :], lambda t: t.rearrange("p (i j) -> p i j", j=L)

        squares = [SQ[:, BANK * h:BANK * h + BANK] for h in range(2)]
        gate, grown = SS[:, 0:BANK], O[:, 0:BANK]

        taken = [0]

        def part(cols):
            taken[0] += cols
            assert taken[0] <= WORK
            return work[:, taken[0] - cols:taken[0]]

        SA = [part(NB * L) for _ in range(4)]
        SB = [part(NB * L) for _ in range(4)]
        DTB = [part(128) for _ in range(4)]
        TX = [part(192) for _ in range(2)]
        UB = [part(64) for _ in range(2)]
        BB = [part(128) for _ in range(2)]
        C2 = [part(64) for _ in range(2)]
        DA = [part(32) for _ in range(2)]
        AM = [[part(512) for _ in range(2)] for _ in range(2)]
        GM = [part(64) for _ in range(2)]
        DK = [part(512) for _ in range(2)]
        XB = [ring4[:, 512 * r:512 * r + 256] for r in range(4)]
        X2 = [ring4[:, 512 * r + 256:512 * r + 512] for r in range(4)]
        MM = [sb(f"scores_times_decays{i}", 512) for i in range(2)]
        DT = sb("DT", 1024)
        dtw = [SS[:, 1024 * i:1024 * i + 1024] for i in range(3)]
        tz = [SQ[:, 512 * i:512 * i + 512] for i in range(4)]

        wxa, wxb = FW[:, 0:128], FW[:, 128:256]
        wbc = [FW[:, 256 + 128 * t:384 + 128 * t] for t in range(2)]
        wog = [FW[:, 512 + 128 * h:640 + 128 * h] for h in range(2)]
        Dhalf = FW[:, 768:1280]
        expA, bbc_minus = small[:, 16:32], small[:, 56:57]
        dtx = FW[:, 1280:1440]
        PDT, PX, PBC = slice(0, 32), slice(32, 160), slice(160, 224)

        w0, w1 = Y[:, 0:width(L0_COLS)], Y[:, 2320:2320 + width(L1_COLS)]
        assert width(L0_COLS) <= 2320 and 2320 + width(L1_COLS) <= TOK
        poolS, stateS = Z2[:, 0:2048], Z2[:, 2048:2048 + 4096]

        selBC = Z2[:, 6144:8192].bitcast(BF16)
        parts = [work[:, a:a + 256].bitcast(BF16) for a in (2560, 5632)]
        dt1, u1, z1 = ([SQ[:, a:a + 512], work[:, b:b + 512]] for a, b in ((3584, 3584), (2048, 4096), (2560, 4608)))
        mid = work[:, 2816:3072].bitcast(BF16)
        rest = work[:, 3072:3584]

        def W0(name, parts=128):
            a, b = W0s[name]
            return w0[0:parts, a:b]

        def W1(name, parts=128):
            a, b = W1s[name]
            return w1[0:parts, a:b]

        x_tok = x.rearrange("b i j c -> b (i j) c")
        out_tok = out.rearrange("b i j c -> b (i j) c")
        Otok = O.rearrange("p (t b c) -> p t b c", b=2, c=64)
        ctx.enter_context(nc.allow_non_contiguous_dma("token-major rows of 64 channels"))
        block = ctx.enter_context(nc.Block())

        def rounds(eng, mod_pre, call, mod_post):
            with eng.Fori(0, 2) as m:
                mod_pre(m)
                with eng.Fori(0, 2) as n:
                    for d in range(2):
                        call(m, n, d, eng.snap(m * 4 + n * 2 + d))
                mod_post(m)

        def tiles(eng, c, first, last, step, lead=0):
            T0 = eng.snap(c * L)
            G0 = eng.snap(c * NGROUP)
            for tau in range(first, 8):
                step(tau, T0, tau, None, G0)
            with eng.Fori(0, 7 - lead) as it:
                q0 = eng.snap(it * 8)
                T = eng.snap(T0 + q0)
                G = eng.snap(G0 + it)
                for u in range(8):
                    step(u + 8, T, None, q0, G)
            for tau in range(L - 8 * lead, last):
                step(tau, T0, tau, None, G0)

        def group(tau, q0, at):
            q = tau - at - 8
            return (tau >= 8 and tau % 8 == at), (q if q0 is None else q0 + q)

        def part_of(known, offset):
            return known is None or 0 <= known + offset < L

        def later(known, offset, k):
            return known is None or known + offset >= k

        def chunk_pairs(eng, front, chunk):
            for s in range(LAST1):
                front(s, 0, 0)
            chunk(None, 0, True)
            with eng.Fori(0, NK1 // 2 - 1) as pair:
                for parity in range(2):
                    chunk(eng.snap(pair * 2 + parity), parity, True)
            chunk(NK1 - 2, 0, True)
            chunk(NK1 - 1, 1, False)

        def f_parity(k, parity):
            return 0 if k is None else 1 - parity

        def count(eng, e):
            return e if isinstance(e, int) else eng.snap(e)

        def y_value(m, n, d):
            return m * 5 + n * 2 + d + 1

        @block.sync
        def _(sp):
            sp.dma_start(cst, consts).then_inc(sg("constants_loaded"), 16)
            for b in range(NB):
                sp.dma_start(Otok[:, :, b, :], x_tok[b].rearrange("(t p) c -> p t c", p=128)).then_inc(
                    sg("x_loaded"), 16)
            sp.dma_start(w0, l0w).then_inc(sg("stage0_weights_loaded"), 16)
            sp.dma_start(poolS, pool_sel).then_inc(sg("stage0_weights_loaded"), 16)
            sp.dma_start(w1, l1w).then_inc(sg("stage1_weights_loaded"), 16)
            sp.dma_start(stateS, state_sel).then_inc(sg("stage1_weights_loaded"), 16)
            for d in range(2):
                sp.dma_start(raws[d], callw[d]).then_inc(sg(f"block_weights_loaded{d}"), 16)

            with sp.Fori(0, 3) as r:
                for d in range(2):
                    sp.wait_ge(sg(f"block_done{d}"), r + 1)
                    sp.dma_start(raws[d], callw[bass.ds(r * 2 + d + 2, 1)].rearrange("a p n -> p (a n)")).then_inc(
                        sg(f"block_weights_loaded{d}"), 16)
            for b in range(NB):
                sp.wait_ge(sg("out_turned"), 8)
                sp.dma_start(out_tok[b].rearrange("(t p) c -> p t c", p=128), Otok[:, :, b, :]).then_inc(
                    sg("output_stored"), 16)
            sp.wait_ge(sg("output_stored"), 32)

        PE0 = ["xp", "qk", "adj", "adjT", "v", "support", "xpos", "query", "key", "at", "atT", "val", "y", "z"]
        DVE0 = ["xj", "xp", "xpre", "qk", "adj", "neg", "e1", "adjT", "v", "support", "xpos", "query", "key", "at",
                "neg2", "e2", "atT", "val", "y", "z"]
        ACT0 = ["exp", "exp2"]

        @block.tensor
        def _(pe):
            mm, tr = nc.tensor.matmul, nc.tensor.transpose

            def groupnorm(g):
                pe.wait_ge(sg("gn_sum"), g + 1)
                mm(bank[7][:, 0:1], C("pair"), small[:, 0:1], start=True, stop=True).then_inc(sg("gn_mean"), 1)
                pe.wait_ge(sg("gn_square"), g + 1)
                mm(bank[7][:, 8:9], C("pair"), small[:, 2:3], start=True, stop=True).then_inc(sg("gn_var"), 1)

            def turn_in():
                pe.wait_ge(sg("constants_loaded"), 16)
                pe.wait_ge(sg("x_loaded"), 32)
                for k in range(8):
                    for t in range(4):
                        a = BANK * k + 128 * t
                        last = tr(bank[k][:, 128 * t:128 * t + 128], O[:, a:a + 128], ident)
                    last.then_inc(sg("in_turned"), 1)

            def turn_out():
                pe.wait_ge(sg("x_final"), 1)
                for k in range(8):
                    for t in range(4):
                        a = BANK * k + 128 * t
                        last = tr(bank[k][:, 128 * t:128 * t + 128], X[:, a:a + 128], ident)
                    last.then_inc(sg("out_in_psum"), 1)

            def stage0():
                def need(name):
                    pe.wait_ge(sg("stage0_dve"), DVE0.index(name) + 1)

                def done(ins):
                    ins.then_inc(sg("stage0_pe"), 1)
                pe.wait_ge(sg("stage0_weights_loaded"), 32)
                need("xj")
                Xj = SQ[:, 0:1024].rearrange("p (i j) -> p i j", j=16)
                for hf in range(2):
                    for b in range(NB):
                        for jj in range(8):
                            r = b * 8 + jj
                            last = mm(bank[0][:, 128 * hf + 64 * b:128 * hf + 64 * b + 64],
                                      poolS[:, 128 * r:128 * r + 128], Xj[:, :, hf * 8 + jj],
                                      start=(jj == 0), stop=(jj == 7))
                done(last)
                xpT, xpre = SQ[:, 1024:1280], SQ[:, 1280:1312]
                need("xpre")
                for w, o in (("gq", 0), ("gk", 16)):
                    for hf in range(2):
                        last = mm(bank[1][0:64, o:o + 16], W0(w)[:, 64 * hf:64 * hf + 64],
                                  xpre[:, 16 * hf:16 * hf + 16], start=(hf == 0), stop=(hf == 1))
                done(last)
                need("qk")
                q, k = SQ[0:64, 1312:1328], SQ[0:64, 1328:1344]
                done(mm(bank[2][0:16, 0:16], k, q, start=True, stop=True))
                need("e1")
                done(tr(bank[3][0:16, 0:16], SQ[0:16, 1344:1360], ident[0:16, 0:16]))
                for ho in range(2):
                    for hf in range(2):
                        last = mm(bank[4][:, 16 * ho:16 * ho + 16],
                                  W0("gv")[:, 256 * hf + 128 * ho:256 * hf + 128 * ho + 128],
                                  xpre[:, 16 * hf:16 * hf + 16], start=(hf == 0), stop=(hf == 1))
                done(last)
                need("v")
                v = SQ[:, 1392:1424]
                for hf in range(2):
                    last = mm(bank[5][0:16, 0:256], v[:, 16 * hf:16 * hf + 16],
                              W0("gw")[:, 256 * hf:256 * hf + 256], start=(hf == 0), stop=(hf == 1))
                done(last)
                need("support")
                for ho in range(2):
                    last = mm(bank[6][:, 16 * ho:16 * ho + 16], SQ[0:16, 1424 + 128 * ho:1552 + 128 * ho],
                              SQ[0:16, 1376:1392], start=True, stop=True)
                done(last)
                need("xpos")
                xpos = SQ[:, 1680:1712]
                for hf in range(2):
                    last = mm(bank[1][0:64, 0:16], W0("q")[:, 64 * hf:64 * hf + 64],
                              xpos[:, 16 * hf:16 * hf + 16], start=(hf == 0), stop=(hf == 1))
                done(last)
                for hf in range(2):
                    last = mm(bank[2][0:64, 0:128], W0("k")[:, 64 * hf:64 * hf + 64],
                              xpT[:, 128 * hf:128 * hf + 128], start=(hf == 0), stop=(hf == 1))
                done(last)
                need("key")
                done(mm(bank[3][:, 0:16], SQ[0:64, 1728:1856], SQ[0:64, 1712:1728], start=True, stop=True))
                need("e2")
                done(tr(bank[4][0:16, 0:128], SQ[:, 1856:1872], ident))
                for hf in range(2):
                    mm(bank[5][0:16, 0:256], xpos[:, 16 * hf:16 * hf + 16], W0("v")[:, 256 * hf:256 * hf + 256],
                       start=(hf == 0), stop=False)
                done(mm(bank[5][0:16, 0:256], C("ones", 1)[:, 0:16], W0("vb", 1), start=False, stop=True))
                need("val")
                done(mm(bank[6][:, 0:256], SQ[0:16, 1888:2016], SQ[0:16, 2016:2272], start=True, stop=True))
                need("y")
                for hlo in range(4):
                    last = mm(bank[hlo // 2][:, 256 * (hlo % 2):256 * (hlo % 2) + 256],
                              C("interp")[:, 128 * hlo:128 * hlo + 128], SQ[:, 2272:2528], start=True, stop=True)
                done(last)

            def stage1():
                pe.wait_ge(sg("stage1_weights_loaded"), 32)
                st = SQ[:, 0:SEQ1 * PADL].rearrange("p (s l) -> p s l", l=PADL)
                xd, yz = SQ[:, 3072:3584], work[:, 1024:1536]
                pe.wait_ge(sg("s1_selectors"), 1)

                def front(s, f, par):
                    if s == 3:
                        pe.wait_ge(sg("s1_staged"), f + 1)
                        mm(bank[0], W1("winx_a"), st[:, :, 3:3 + L], start=True, stop=False)
                        mm(bank[0], W1("winx_b"), st[:, :, 1:1 + L], start=False, stop=True)
                        mm(bank[1], W1("wz"), st[:, :, 3:3 + L], start=True, stop=True).then_inc(sg("s1_front"), 1)
                    if s == 8:
                        pe.wait_ge(sg("s1_u"), f + 1)
                        mm(bank[2][0:64, :], W1("wxp"), u1[par], start=True, stop=True).then_inc(sg("s1_dbl"), 1)
                    if s == 12:
                        pe.wait_ge(sg("s1_xd"), f + 1)
                        mm(bank[3], W1("wdt")[32:64, :], xd[32:64, :], start=True, stop=True).then_inc(
                            sg("s1_dtp"), 1)

                def state_B(s, s0, par):
                    if s0 is not None:
                        pe.wait_ge(sg("s1_dbu"), s0 + (s - 1))
                    one = 128 * (s % S1)
                    mm(bank[4 + s % 2], selBC[0:96, one:one + 128], parts[par][0:96, :], start=True,
                       stop=True).then_inc(sg("s1_B"), 1)

                def state_C(s, s0, par):
                    if s >= 2:
                        pe.wait_ge(sg("s1_hc"), s0 + (s - 1))
                    mm(bank[6 + s % 2], selBC[0:96, 2048 + 128 * s:2176 + 128 * s], parts[par][0:96, :], start=True,
                       stop=True).then_inc(sg("s1_C"), 1)

                def chunk(k, par, more):
                    if k is not None:
                        s0 = count(pe, k * S1)
                        for s in range(2, S1):
                            if more:
                                front(s, k + 1, 1 - par)
                            state_B(s, s0, par)
                            state_C(s - 2, s0, par)
                    if more:
                        f = 0 if k is None else k + 1
                        pe.wait_ge(sg("s1_split"), f + 1)
                        pe.wait_ge(sg("s1_split_mid"), f + 1)
                    for s in range(2):
                        if more:
                            state_B(s if k is None else S1 + s, None if k is None else s0, f_parity(k, par))
                        if k is not None:
                            state_C(S1 - 2 + s, s0, par)
                    if k is not None:
                        pe.wait_ge(sg("s1_gated"), k + 1)
                        for b in range(NB):
                            last = mm(bank[2][64 * b:64 * b + 64, 0:256], W1("wout"), yz[:, 256 * b:256 * b + 256],
                                      start=True, stop=True)
                        last.then_inc(sg("s1_out"), 1)

                chunk_pairs(pe, front, chunk)
                pe.wait_ge(sg("s1_stored"), NK1)
                for ch in range(NCHUNK):
                    mm(bank[ch], C("mean64"), O[:, BANK * ch:BANK * ch + BANK], start=True,
                       stop=True).then_inc(sg("ln_mean"), 1)
                for ch in range(NCHUNK):
                    pe.wait_ge(sg("ln_square"), ch + 1)
                    mm(bank[ch], C("mean64"), SQ[:, BANK * ch:BANK * ch + BANK], start=True,
                       stop=True).then_inc(sg("ln_var"), 1)

            def call(m, n, d, c):
                raw = raws[d]

                def W(name):
                    a, b = Ws[name]
                    return raw[:, a:b]
                for ch in range(NCHUNK):
                    pe.wait_ge(sg("squared"), c * NCHUNK + (ch + 1))
                    mm(bank[ch], C("mean64"), SQ[:, BANK * ch:BANK * ch + BANK], start=True,
                       stop=True).then_inc(sg("norm_ms"), 1)
                pe.wait_ge(sg(f"block_weights_loaded{d}"), (m * 2 + n) * 16 + 16)

                def z(i):
                    if i >= 4:
                        pe.wait_ge(sg("z_ready"), c * 16 + (i - 3))
                    else:
                        pe.wait_ge(sg("norm_log"), c * NCHUNK + (i + 1))
                        pe.wait_ge(sg("normed"), c * NCHUNK + (i // 2 + 1))
                    a = BANK * (i // 2)
                    mm(bank[i % 4], W(f"wz{i % 2}"), XN[:, a:a + BANK], start=True, stop=True).then_inc(
                        sg("z_psum"), 1)
                for i in range(4):
                    z(i)
                pe.wait_ge(sg("normed"), c * NCHUNK + NCHUNK)
                for hq in range(2):
                    for g in range(4):
                        if d == 0:
                            cols = XN3[:, 16 * g:16 * g + 16, 32 * hq:32 * hq + 32].rearrange("p i j -> p j i")
                        else:
                            cols = XN3[:, 32 * hq:32 * hq + 32, 16 * g:16 * g + 16]
                        last = mm(bank[4 + hq][32 * g:32 * g + 32, :], W("wdt"), cols, start=True, stop=True,
                                  tile_position=(0, 32 * g))
                last.then_inc(sg("dt_psum"), 1)
                for i in range(4, 16):
                    z(i)
                pe.wait_ge(sg("folded"), c + 1)
                pe.wait_ge(sg("dt_added"), c + 1)
                pe.wait_ge(sg("z_ready"), c * 16 + 16)

                def step(tau, T, known, q0, G):
                    if part_of(known, 0):
                        p, s = tau % 2, tau % 4
                        pe.wait_ge(sg("staged_straight"), T + (tau + 1))
                        pe.wait_ge(sg("staged_shifted"), T + (tau + 1))
                        if later(known, 0, 2):
                            pe.wait_ge(sg("x_ready"), T + (tau - 1))
                            pe.wait_ge(sg("bc_ready"), T + (tau - 1))
                        mm(bank[p][:, 0:160], DTB[s], dtx, start=True, stop=False, skip_group_check=True)
                        mm(bank[p][:, PX], SA[s], wxa, start=False, stop=False, skip_group_check=True)
                        mm(bank[p][:, PX], SB[s], wxb, start=False, stop=True, skip_group_check=True)
                        for t, src in ((0, SA[s]), (1, SB[s])):
                            for j in range(4):
                                last = mm(bank[p][32 * j:32 * j + 32, PBC], wbc[t][:, 32 * j:32 * j + 32],
                                          src[:, L * (j % 2):L * (j % 2) + L], start=(t == 0), stop=(t == 1),
                                          tile_position=(0, 32 * j), skip_group_check=True)
                        last.then_inc(sg("projected"), 1)
                    if part_of(known, -1):
                        p = (tau - 1) % 2
                        pe.wait_ge(sg("bc_ready"), T + tau)
                        pe.wait_ge(sg("am0_ready"), T + tau)
                        pe.wait_ge(sg("am1_ready"), T + tau)
                        if later(known, -1, 2):
                            pe.wait_ge(sg("gm_ready"), T + (tau - 2))
                            pe.wait_ge(sg("decay_ready"), T + (tau - 2))
                        for b in range(NB):
                            last = mm(bank[2 + p][64 * b:64 * b + 64, :], C("between"), AM[p][b], start=True,
                                      stop=True, tile_position=(0, 64 * b), skip_group_check=True)
                        last.then_inc(sg("decay_logs"), 1)
                        if later(known, -1, 2):
                            pe.wait_ge(sg("gated"), T + (tau - 2))
                        for j in range(4):
                            last = mm(bank[4 + p][32 * j:32 * j + 32, 128:192], BB[p][:, 32 * j:32 * j + 32], C2[p], start=True, stop=True,
                                      tile_position=(0, 32 * j), skip_group_check=True)
                        last.then_inc(sg("scored"), 1)
                    if part_of(known, -2):
                        p, r = (tau - 2) % 2, (tau - 2) % 4
                        y = bank[4 + p][:, 0:128]
                        pe.wait_ge(sg("xb_ready"), T + (tau - 1))
                        pe.wait_ge(sg("mixed"), T + (tau - 1))
                        for hd in range(2):
                            for xs, by, first_ in ((X2[r], Dhalf, True), (XB[r], MM[p], False)):
                                for h4 in range(4):
                                    h = 4 * hd + h4
                                    last = mm(y[32 * h4:32 * h4 + 32, 64 * hd:64 * hd + 64],
                                              xs[:, 32 * h:32 * h + 32], by[:, 64 * h:64 * h + 64],
                                              start=first_, stop=not first_, tile_position=(0, 32 * h4),
                                              skip_group_check=True)
                        last.then_inc(sg("y_psum"), 1)
                    for hd in range(2):
                        now, q = group(tau, q0, 2 + 3 * hd)
                        if now:
                            pe.wait_ge(sg("gated"), T + (tau - 2 - 3 * hd))
                            last = mm(bank[6], wog[hd], axis_group(Z24[:, hd], d, q)[0], start=(hd == 0),
                                      stop=(hd == 1))
                            if hd == 1:
                                last.then_inc(sg("out_psum"), 1)
                    now, _ = group(tau, q0, 4)
                    if now:
                        pe.wait_ge(sg("squares_added"), G + (tau // 8))
                        mm(bank[7], C("ssum"), squares[0], start=True, stop=True).then_inc(sg("squares_psum"), 1)

                tiles(pe, c, 0, L + 8, step)

            turn_in()
            groupnorm(0)
            stage0()
            groupnorm(1)
            stage1()
            rounds(pe, lambda m: groupnorm(m + 2), call, lambda m: None)
            turn_out()

        @block.scalar
        def _(act):
            A = nc.scalar.activation

            def groupnorm(g):
                act.wait_ge(sg("gn_centre"), g + 1)
                A(SQ, X, ACT.Square, bias=small[:, 1:2], accum_out=small[:, 2:3]).then_inc(sg("gn_square"), 1)
                act.wait_ge(sg("gn_var"), g + 1)
                A(small[:, 3:4], bank[7][:, 8:9], ACT.Ln, bias=C("eps5")).then_inc(sg("gn_log"), 1)
                act.wait_ge(sg("gn_log"), g + 1)
                A(small[:, 4:5], small[:, 3:4], ACT.Exp, scale=-0.5).then_inc(sg("gn_scale"), 1)

            def softplus_exp(prefix, v, e, r, base):
                act.wait_ge(sg(prefix + "_added"), base + 1)
                A(e, v, ACT.Abs).then_inc(sg(prefix + "_abs"), 1)
                act.wait_ge(sg(prefix + "_abs"), base + 1)
                A(e, e, ACT.Exp, scale=-1.0).then_inc(sg(prefix + "_e"), 1)
                act.wait_ge(sg(prefix + "_e"), base + 1)
                A(r, e, ACT.Ln, bias=C("two")).then_inc(sg(prefix + "_log"), 1)
                act.wait_ge(sg(prefix + "_log"), base + 1)
                A(r, r, ACT.Exp, scale=-1.0).then_inc(sg(prefix + "_exp"), 1)

            act.wait_ge(sg("constants_loaded"), 16)
            for k in range(1, 8, 2):
                act.wait_ge(sg("in_turned"), k + 1)
                A(X[:, BANK * k:BANK * k + BANK], bank[k], ACT.Copy).then_inc(sg("x_placed"), 1)
            groupnorm(0)
            act.wait_ge(sg("stage0_dve"), DVE0.index("neg") + 1)
            A(SQ[0:16, 1344:1360], SQ[0:16, 1344:1360], ACT.Exp, bias=small[0:16, 9:10],
              accum_out=small[0:16, 10:11]).then_inc(sg("stage0_act"), 1)
            act.wait_ge(sg("stage0_dve"), DVE0.index("neg2") + 1)
            A(SQ[:, 1856:1872], SQ[:, 1856:1872], ACT.Exp, bias=small[:, 13:14],
              accum_out=small[:, 14:15]).then_inc(sg("stage0_act"), 1)
            groupnorm(1)

            act.wait_ge(sg("stage1_weights_loaded"), 32)
            negA, hb = small[:, 32:48], small[:, 48:49]
            act.wait_ge(sg("s1_alog"), 1)
            A(negA, negA, ACT.Exp).then_inc(sg("s1_expA"), 1)
            act.wait_ge(sg("s1_consts"), 1)
            vv, t, xd = SQ[:, 1024:1536], SQ[:, 1536:2048], SQ[:, 3072:3584]
            w0_, w1_ = SS[:, 0:512], SS[:, 512:1024]
            dA = [SS[:, 2048 + 512 * i:2560 + 512 * i].rearrange("p (s l) -> p s l", l=L) for i in range(2)]

            def front(s, f, par):
                if s == 5:
                    act.wait_ge(sg("s1_front"), f + 1)
                    A(t, bank[0], ACT.Tanh, bias=hb, scale=0.5)
                    A(vv, bank[0], ACT.Identity, bias=hb, scale=0.5).then_inc(sg("s1_tanh"), 1)
                    A(w0_, bank[1], ACT.Tanh, scale=0.5).then_inc(sg("s1_tanhz"), 1)
                if s == 10:
                    act.wait_ge(sg("s1_dbl"), f + 1)
                    A(xd[32:64, :], bank[2][32:64, :], ACT.Copy).then_inc(sg("s1_xd"), 1)
                    A(parts[par][0:32, :], bank[2][0:32, :], ACT.Copy).then_inc(sg("s1_split_high"), 1)
                if s == 12:
                    act.wait_ge(sg("s1_mid"), f + 1)
                    A(parts[par][32:64, :], mid[0:32, :], ACT.Copy).then_inc(sg("s1_split_mid"), 1)
                if s == 13:
                    nc.scalar.preload_act_table_set(LN_EXP)
                    act.wait_ge(sg("s1_dtp"), f + 1)
                    A(dt1[par], bank[3], ACT.Identity, bias=W1("bdt")).then_inc(sg("s1dt_added"), 1)
                    act.wait_ge(sg("s1_z"), f + 1)
                    softplus_exp("s1dt", dt1[par], w0_, w1_, f)

            def state(s, s0, par):
                if s0 is not None:
                    act.wait_ge(sg("s1_h"), s0 + (s - 1))
                A(dA[s % 2][:, :, 1:L], dt1[par].rearrange("p (s l) -> p s l", l=L)[:, :, 1:L], ACT.Exp,
                  scale=negA[:, s % S1:s % S1 + 1]).then_inc(sg("s1_dA"), 1)

            def chunk(k, par, more):
                if k is not None:
                    s0 = count(act, k * S1)
                    for s in range(2, S1):
                        if more:
                            front(s, k + 1, 1 - par)
                        state(s, s0, par)
                if more:
                    act.wait_ge(sg("s1dt_ready"), (0 if k is None else k + 1) + 1)
                    for s in range(2):
                        state(s if k is None else S1 + s, None if k is None else s0, f_parity(k, par))
                if k is not None:
                    act.wait_ge(sg("s1_out"), k + 1)
                    A(O3[:, :, bass.ds(k * J1, J1)].rearrange("p i j -> p j i"),
                      bank[2][:, 0:256].rearrange("p (j i) -> p j i", i=L), ACT.Copy).then_inc(sg("s1_stored"), 1)

            chunk_pairs(act, front, chunk)
            chunks = [slice(BANK * ch, BANK * ch + BANK) for ch in range(NCHUNK)]
            for ch, at in enumerate(chunks):
                act.wait_ge(sg("ln_centred"), ch + 1)
                A(SQ[:, at], O[:, at], ACT.Square).then_inc(sg("ln_square"), 1)
            for ch, at in enumerate(chunks):
                act.wait_ge(sg("ln_var"), ch + 1)
                A(SS[:, at], bank[ch], ACT.Ln, bias=C("eps5")).then_inc(sg("ln_log"), 1)
                act.wait_ge(sg("ln_log"), ch + 1)
                A(SS[:, at], SS[:, at], ACT.Exp, scale=-0.5).then_inc(sg("ln_scale"), 1)

            def call(m, n, d, c):
                raw = raws[d]

                def W(name):
                    a, b = Ws[name]
                    return raw[:, a:b]
                nc.scalar.preload_act_table_set(LN_EXP)
                act.wait_ge(sg(f"block_weights_loaded{d}"), (m * 2 + n) * 16 + 16)
                A(expA, W("alog"), ACT.Exp).then_inc(sg("expA_ready"), 1)
                act.wait_ge(sg("y_ready"), y_value(m, n, d))
                for at in chunks:
                    A(SQ[:, at], Y[:, at], ACT.Square).then_inc(sg("squared"), 1)
                for ch, at in enumerate(chunks):
                    act.wait_ge(sg("norm_ms"), c * NCHUNK + (ch + 1))
                    A(O[:, at], bank[ch], ACT.Ln, bias=C("eps6")).then_inc(sg("norm_log"), 1)
                    act.wait_ge(sg("norm_log"), c * NCHUNK + (ch + 1))
                    A(O[:, at], O[:, at], ACT.Exp, scale=-0.5).then_inc(sg("norm_scale"), 1)
                for i in range(16):
                    if i == 4:
                        nc.scalar.preload_act_table_set(LN_EXP)
                        softplus_exp("dt", DT, dtw[0], dtw[1], c)
                    act.wait_ge(sg("z_psum"), c * 16 + (i + 1))
                    if i >= 4:
                        act.wait_ge(sg("z_ready"), c * 16 + (i - 3))
                    A(tz[i % 4], bank[i % 4], ACT.Tanh, scale=0.5).then_inc(sg("z_tanh"), 1)

                nc.scalar.preload_act_table_set(LN_EXP)
                act.wait_ge(sg("normed"), c * NCHUNK + NCHUNK)
                act.wait_ge(sg("folded"), c + 1)
                act.wait_ge(sg("zeroed"), 1)

                def stage(t, T, q, free):
                    if free:
                        act.wait_ge(sg("projected"), T + (t - 3))
                    s = SA[t % 4]
                    src = axis(XN3, d, q).rearrange("p i j -> p (i j)")
                    A(s[0:64, 0:L], src[0:64, :], ACT.Copy)
                    A(s[64:128, L + 1:2 * L], src[64:128, 0:L - 1], ACT.Copy).then_inc(sg("staged_own"), 1)

                def step(tau, T, known, q0, G):
                    if part_of(known, 0):
                        p = tau % 2
                        act.wait_ge(sg("projected"), T + (tau + 1))
                        if later(known, 0, 2):
                            act.wait_ge(sg("x_ready"), T + (tau - 1))
                            act.wait_ge(sg("bc_ready"), T + (tau - 1))
                        if later(known, 0, 2):
                            act.wait_ge(sg("am0_ready"), T + (tau - 1))
                            act.wait_ge(sg("xb_ready"), T + (tau - 1))
                        A(DA[p], bank[p][:, PDT], ACT.Copy).then_inc(sg("a_ready"), 1)
                        A(TX[p][:, 128:192], bank[p][:, PBC], ACT.Exp, bias=bbc_minus, scale=-1.0)
                        A(UB[p], bank[p][:, PBC], ACT.Identity, bias=W("bbc"))
                        A(TX[p][:, 0:128], bank[p][:, PX], ACT.Exp, scale=-1.0).then_inc(sg("sigmoid_exp"), 1)
                    if part_of(known, 2):
                        q = (q0 + (tau + 2)) if known is None else tau + 2
                        stage(tau + 2, T, q, later(known, 2, 4))
                    if part_of(known, 0):
                        act.wait_ge(sg("sigmoid_exp"), T + (tau + 1))
                        A(TX[p], TX[p], ACT.Ln, bias=C("ones")[:, 0:1]).then_inc(sg("sigmoid_log"), 1)
                        act.wait_ge(sg("sigmoid_log"), T + (tau + 1))
                        A(TX[p], TX[p], ACT.Exp, scale=-1.0).then_inc(sg("sigmoid_ready"), 1)
                    if part_of(known, -1):
                        p = (tau - 1) % 2
                        act.wait_ge(sg("decay_logs"), T + tau)
                        if later(known, -1, 2):
                            act.wait_ge(sg("mixed"), T + (tau - 2))
                        A(DK[p], bank[2 + p], ACT.Exp).then_inc(sg("decay_ready"), 1)
                    now, q = group(tau, q0, 2)
                    if now:
                        act.wait_ge(sg("gated"), T + (tau - 2))
                        for hd in range(2):
                            src, like = axis_group(Z24[:, hd], d, q)
                            last = A(like(squares[hd]), src, ACT.Square)
                        last.then_inc(sg("gated_squared"), 1)
                    now, q = group(tau, q0, 5)
                    if now:
                        act.wait_ge(sg("squares_psum"), G + (tau // 8))
                        A(gate, bank[7], ACT.Ln, bias=C("eps6x4")).then_inc(sg("gate_log"), 1)
                        act.wait_ge(sg("gate_log"), G + (tau // 8))
                        A(gate, gate, ACT.Exp, scale=-0.5).then_inc(sg("gate_scale"), 1)

                tiles(act, c, -2, L + 8, step, lead=1)

            rounds(act, lambda m: groupnorm(m + 2), call, lambda m: None)
            for k in range(1, 8, 2):
                act.wait_ge(sg("out_in_psum"), k + 1)
                A(O[:, BANK * k:BANK * k + BANK], bank[k], ACT.Copy).then_inc(sg("out_turned"), 1)

        @block.gpsimd
        def _(pool):
            g = nc.gpsimd
            pool.wait_ge(sg("constants_loaded"), 16)
            hc = [Y[:, 512 * i:512 * i + 512] for i in range(2)]
            acc = Y[:, 1024:1536]
            with pool.Fori(0, NK1) as k:
                s0 = pool.snap(k * S1)
                for s in range(S1):
                    pool.wait_ge(sg("s1_hc"), s0 + (s + 1))
                    if s == 0:
                        g.tensor_tensor(acc, hc[0], C("ones")[:, 0:1].broadcast_to([128, 512]), ALU.mult).then_inc(sg("s1_acc"), 1)
                    else:
                        pool.wait_ge(sg("s1_acc"), s0 + s)
                        g.tensor_tensor(acc, acc, hc[s % 2], ALU.add).then_inc(sg("s1_acc"), 1)
            pool.wait_ge(sg("s1_out"), NK1)
            for t in SA + SB + BB + C2 + X2:
                last = g.memset(t, 0.0)
            last.then_inc(sg("zeroed"), 1)
            pool.wait_ge(sg("zeroed"), 1)

            def call(m, n, d, c):
                pool.wait_ge(sg("normed"), c * NCHUNK + NCHUNK)
                pool.wait_ge(sg("dt_ready"), c + 1)
                pool.wait_ge(sg("folded"), c + 1)

                def stage(t, T, q, free):
                    p = t % 4
                    if free:
                        pool.wait_ge(sg("projected"), T + (t - 3))
                    pool.wait_ge(sg("staged_own"), T + (t + 1))
                    pool.wait_ge(sg("staged_shifted"), T + (t + 1))
                    a, later_ = (x_[p].rearrange("p (b l) -> p b l", l=L) for x_ in (SA, SB))
                    g.tensor_tensor(later_[:, :, 2:L], a[:, :, 0:L - 2],
                                    C("ones")[:, 0:1].unsqueeze(2).broadcast_to([128, 2, L - 2]), ALU.mult)
                    dtq = DT.rearrange("p (q l) -> p q l", l=16)[:, bass.ds(q, 1), :]
                    g.tensor_tensor(DTB[p].rearrange("p (k l) -> p k l", l=16), dtq.broadcast_to([128, 8, 16]),
                                    C("maskdt").unsqueeze(2).broadcast_to([128, 8, 16]), ALU.mult).then_inc(
                        sg("staged_straight"), 1)

                def step(tau, T, known, q0, G):
                    if part_of(known, 2):
                        q = (q0 + (tau + 2)) if known is None else tau + 2
                        stage(tau + 2, T, q, later(known, 2, 4))
                    if part_of(known, 0):
                        p, r = tau % 2, tau % 4
                        pool.wait_ge(sg("a_ready"), T + (tau + 1))
                        if later(known, 0, 2):
                            pool.wait_ge(sg("decay_logs"), T + (tau - 1))
                        g.tensor_tensor(AM[p][1].rearrange("p (h l) -> p h l", l=L),
                                        DA[p][:, 0:16].rearrange("p (h b) -> p h b", b=2)[:, :, 1:2].broadcast_to(
                                            [128, 8, L]),
                                        C("span").unsqueeze(1).broadcast_to([128, 8, L]), ALU.mult).then_inc(
                            sg("am1_ready"), 1)
                        pool.wait_ge(sg("x_ready"), T + (tau + 1))
                        if later(known, 0, 4):
                            pool.wait_ge(sg("y_psum"), T + (tau - 3))
                        g.tensor_tensor(XB[r].rearrange("p (n e) -> p n e", e=HP),
                                        X2[r].rearrange("p (n e) -> p n e", e=HP),
                                        DA[p][:, 16:32].unsqueeze(2).broadcast_to([128, 16, HP]),
                                        ALU.mult).then_inc(sg("xb_ready"), 1)

                    now, _ = group(tau, q0, 3)
                    if now:
                        pool.wait_ge(sg("gated_squared"), G + (tau // 8))
                        g.tensor_tensor(squares[0], squares[0], squares[1], ALU.add).then_inc(
                            sg("squares_added"), 1)

                tiles(pool, c, -2, L + 8, step, lead=1)

            rounds(pool, lambda m: None, call, lambda m: None)

        @block.vector
        def _(dve):
            v = nc.vector
            for k in range(0, 8, 2):
                dve.wait_ge(sg("in_turned"), k + 1)
                v.tensor_copy(X[:, BANK * k:BANK * k + BANK], bank[k]).then_inc(sg("x_placed"), 1)
            dve.wait_ge(sg("x_placed"), 8)

            def groupnorm(g, dst, ready):
                v.tensor_reduce(small[:, 0:1], X, AX.X, ALU.add).then_inc(sg("gn_sum"), 1)
                dve.wait_ge(sg("gn_mean"), g + 1)
                v.tensor_scalar(small[:, 1:2], bank[7][:, 0:1], -1.0, None, ALU.mult).then_inc(sg("gn_centre"), 1)
                dve.wait_ge(sg("gn_scale"), g + 1)
                v.tensor_scalar(dst, X, small[:, 1:2], small[:, 4:5], ALU.add, ALU.mult).then_inc(sg(ready), 1)

            groupnorm(0, XN, "xn0")

            n0 = [0]

            def done(ins, name):
                assert DVE0[n0[0]] == name
                n0[0] += 1
                ins.then_inc(sg("stage0_dve"), 1)

            def pe_did(name):
                dve.wait_ge(sg("stage0_pe"), PE0.index(name) + 1)

            def did(name):
                dve.wait_ge(sg("stage0_dve"), DVE0.index(name) + 1)
            order = Order(dve, "stage0_order")
            dve.wait_ge(sg("xn0"), 1)
            done(v.tensor_reduce(SQ[:, 0:1024], XN.rearrange("p (n f) -> p n f", f=4), AX.X, ALU.add), "xj")
            pe_did("xp")
            dve.wait_ge(sg("stage0_weights_loaded"), 32)
            xpT, xpre = SQ[:, 1024:1280], SQ[:, 1280:1312]
            done(v.tensor_copy(xpT, bank[0][:, 0:256]), "xp")
            did("xp")
            order(v.tensor_reduce(xpre, xpT.rearrange("p (n f) -> p n f", f=8), AX.X, ALU.add))
            done(v.tensor_scalar(xpre, xpre, 0.125, None, ALU.mult), "xpre")
            pe_did("qk")
            v.tensor_scalar(SQ[0:64, 1312:1328], bank[1][0:64, 0:16], W0("gqb", 64), None, ALU.add)
            done(v.tensor_scalar(SQ[0:64, 1328:1344], bank[1][0:64, 16:32], W0("gkb", 64), None, ALU.add), "qk")

            def softmax(tile, src, mask, cols, names):
                parts = tile.shape[0]
                mx, ng, sm, rc = (small[0:parts, cols + i:cols + i + 1] for i in range(4))
                done(v.tensor_tensor(tile, src, mask, ALU.add), names[0])
                did(names[0])
                order(v.tensor_reduce(mx, tile, AX.X, ALU.max))
                done(v.tensor_scalar(ng, mx, -1.0, None, ALU.mult), names[1])
                dve.wait_ge(sg("stage0_act"), ACT0.index(names[3]) + 1)
                order(v.reciprocal(rc, sm))
                done(v.tensor_scalar(tile, tile, rc, None, ALU.mult), names[2])
            pe_did("adj")
            softmax(SQ[0:16, 1344:1360], bank[2][0:16, 0:16], C("mask16", 16), 8, ("adj", "neg", "e1", "exp"))
            pe_did("adjT")
            done(v.tensor_copy(SQ[0:16, 1376:1392], bank[3][0:16, 0:16]), "adjT")
            pe_did("v")
            for ho in range(2):
                last = v.tensor_scalar(SQ[:, 1392 + 16 * ho:1408 + 16 * ho], bank[4][:, 16 * ho:16 * ho + 16],
                                       W0("gvb")[:, ho:ho + 1], None, ALU.add)
            done(last, "v")
            pe_did("support")
            done(v.tensor_copy(SQ[0:16, 1424:1680], bank[5][0:16, 0:256]), "support")
            pe_did("xpos")
            for ho in range(2):
                last = v.tensor_scalar(SQ[:, 1680 + 16 * ho:1696 + 16 * ho], bank[6][:, 16 * ho:16 * ho + 16],
                                       W0("gb")[:, ho:ho + 1], None, ALU.add)
            done(last, "xpos")
            pe_did("query")
            done(v.tensor_scalar(SQ[0:64, 1712:1728], bank[1][0:64, 0:16], W0("qb", 64), None, ALU.add), "query")
            pe_did("key")
            done(v.tensor_scalar(SQ[0:64, 1728:1856], bank[2][0:64, 0:128], W0("kb", 64), None, ALU.add), "key")
            pe_did("at")
            softmax(SQ[:, 1856:1872], bank[3][:, 0:16], C("maskbc"), 12, ("at", "neg2", "e2", "exp2"))
            pe_did("atT")
            done(v.tensor_copy(SQ[0:16, 1888:2016], bank[4][0:16, 0:128]), "atT")
            pe_did("val")
            done(v.tensor_copy(SQ[0:16, 2016:2272], bank[5][0:16, 0:256]), "val")
            pe_did("y")
            done(v.tensor_copy(SQ[:, 2272:2528], bank[6][:, 0:256]), "y")
            pe_did("z")
            Z = SS[:, 0:1024].rearrange("p (i h) -> p i h", h=16)
            D = SS[:, 1024:2048].rearrange("p (i h) -> p i h", h=16)
            Zv = SS[:, 0:1024].rearrange("p (n h) -> p n h", h=4)
            for hlo in range(4):
                last = v.tensor_copy(Zv[:, :, hlo], bank[hlo // 2][:, 256 * (hlo % 2):256 * (hlo % 2) + 256])
            done(last, "z")
            did("z")
            order(v.tensor_tensor(D[:, :, 0:15], Z[:, :, 1:16], Z[:, :, 0:15], ALU.subtract))
            up = O3[:, :, 0:63].rearrange("p i (a r) -> p i a r", a=3)
            wy = C("wy")[:, 0:63].rearrange("p (a r) -> p a r", a=3)
            D5 = D[:, :, 0:15].rearrange("p i (a k) -> p i a k", a=3)
            Z5 = Z[:, :, 0:15].rearrange("p i (a k) -> p i a k", a=3)
            dve.wait_ge(sg("in_turned"), 8)
            for k in range(5):
                rs = [r for r in range(21) if 5 * r // 21 == k]
                a, b = rs[0], rs[-1] + 1
                for ph in range(3):
                    d_ = D5[:, :, ph, k].unsqueeze(2).broadcast_to([128, L, b - a])
                    z_ = Z5[:, :, ph, k].unsqueeze(2).broadcast_to([128, L, b - a])
                    w_ = wy[:, ph, a:b].unsqueeze(1).broadcast_to([128, L, b - a])
                    order(v.tensor_tensor(up[:, :, ph, a:b], d_, w_, ALU.mult))
                    order(v.tensor_tensor(up[:, :, ph, a:b], up[:, :, ph, a:b], z_, ALU.add))
            order(v.tensor_copy(O3[:, :, 63:64], Z[:, :, 15:16]))
            order(v.tensor_tensor(X, X, O, ALU.add))
            groupnorm(1, XN, "xn1")
            dve.wait_ge(sg("xn1"), 1)

            dve.wait_ge(sg("stage1_weights_loaded"), 32)
            negA, hb = small[:, 32:48], small[:, 48:49]
            st = SQ[:, 0:SEQ1 * PADL].rearrange("p (s l) -> p s l", l=PADL)
            vv, t, total = SQ[:, 1024:1536], SQ[:, 1536:2048], work[:, 0:512]
            w0_, w1_, w2_, dtu = (SS[:, 512 * i:512 * i + 512] for i in range(4))
            dA = [SS[:, 2048 + 512 * i:2560 + 512 * i] for i in range(2)]
            dbu = [SS[:, 3072 + 512 * i:3584 + 512 * i] for i in range(2)]
            hs = [work[:, 1536 + 512 * i:2048 + 512 * i] for i in range(2)]
            yz = work[:, 1024:1536]
            hc = [Y[:, 512 * i:512 * i + 512] for i in range(2)]
            acc = Y[:, 1024:1536]
            order = Order(dve, "s1_setup")
            v.tensor_scalar(negA, W1("alog"), 80.0, None, ALU.min).then_inc(sg("s1_alog"), 1)
            dve.wait_ge(sg("s1_expA"), 1)
            order(v.tensor_scalar(negA, negA, -1.0, None, ALU.mult))
            order(v.tensor_tensor(W1("winx_b"), W1("winx_a"), W1("wcb"), ALU.mult))
            order(v.tensor_tensor(W1("winx_a"), W1("winx_a"), W1("wca"), ALU.mult))
            v.tensor_copy(selBC, stateS).then_inc(sg("s1_selectors"), 1)
            v.memset(SQ[:, 0:SEQ1 * PADL], 0.0)
            v.memset(SS[:, 2048:3072], 0.0)
            order(v.tensor_scalar(hb, W1("bconv"), 0.5, None, ALU.mult))
            v.tensor_scalar(small[:, 49:50], hb, 1.0, None, ALU.mult).then_inc(sg("s1_consts"), 1)

            def softplus(k, x, e, r, y, order):
                if k == 0:
                    order(v.tensor_tensor(r, r, e, ALU.mult))
                elif k == 1:
                    order(v.tensor_tensor(y, r, r, ALU.mult))
                elif k == 2:
                    order(v.tensor_scalar(e, y, LOG1P[4], None, ALU.mult))
                elif k < 6:
                    order(v.scalar_tensor_tensor(e, e, LOG1P[6 - k], y, ALU.add, ALU.mult))
                elif k == 6:
                    order(v.scalar_tensor_tensor(e, e, LOG1P[0], r, ALU.add, ALU.mult))
                else:
                    order(v.scalar_tensor_tensor(x, x, 0.0, e, ALU.max, ALU.add))

            def front(s, f, par):
                if s == 0:
                    cols = XN3[:, :, bass.ds(f * J1, J1)].rearrange("p i j -> p j i")
                    for tp in range(2):
                        for b in range(NB):
                            last = v.tensor_copy(st[64 * tp:64 * tp + 64, J1 * b:J1 * b + J1, 3 + tp:3 + L],
                                                 cols[64 * b:64 * b + 64, :, 0:L - tp])
                    last.then_inc(sg("s1_staged"), 1)
                if s == 5:
                    dve.wait_ge(sg("s1_tanh"), f + 1)
                    v.scalar_tensor_tensor(u1[par], t, 1.0, vv, ALU.add, ALU.mult).then_inc(sg("s1_u"), 1)
                    dve.wait_ge(sg("s1_tanhz"), f + 1)
                    v.scalar_tensor_tensor(z1[par], w0_, 1.0, bank[1], ALU.add, ALU.mult).then_inc(sg("s1_z"), 1)
                order = Order(dve, "s1_order", count(dve, f * 9) + (0 if s <= 9 else 1 + 3 * (s - 13)))
                if s == 9:
                    dve.wait_ge(sg("s1_split_high"), f + 1)
                    order(v.tensor_tensor(rest[0:32, :], bank[2][0:32, :], parts[par][0:32, :], ALU.subtract))
                    v.tensor_copy(mid[0:32, :], rest[0:32, :]).then_inc(sg("s1_mid"), 1)
                    dve.wait_ge(sg("s1_mid"), f + 1)
                    v.tensor_tensor(parts[par][64:96, :], rest[0:32, :], mid[0:32, :], ALU.subtract).then_inc(
                        sg("s1_split"), 1)
                if 13 <= s < 16:
                    if s == 13:
                        dve.wait_ge(sg("s1dt_exp"), f + 1)
                    for i in range(3 * (s - 13), min(3 * (s - 13) + 3, 8)):
                        softplus(i, dt1[par], w0_, w1_, w2_, order)
                if s == 15:
                    v.tensor_tensor(dtu, dt1[par], u1[par], ALU.mult).then_inc(sg("s1dt_ready"), 1)

            def weigh(s, s0):
                dve.wait_ge(sg("s1_B"), s0 + (s + 1))
                v.tensor_tensor(dbu[s % 2], dtu, bank[4 + s % 2], ALU.mult).then_inc(sg("s1_dbu"), 1)

            def read_out(s, s0):
                dve.wait_ge(sg("s1_h"), s0 + (s + 1))
                dve.wait_ge(sg("s1_C"), s0 + (s + 1))
                if s >= 2:
                    dve.wait_ge(sg("s1_acc"), s0 + (s - 1))
                v.tensor_tensor(hc[s % 2], hs[s % 2], bank[6 + s % 2], ALU.mult).then_inc(sg("s1_hc"), 1)

            def chunk(k, par, more):
                if k is not None:
                    s0 = count(dve, k * S1)
                    for s in range(S1):
                        if s + 1 < S1:
                            if s >= 1:
                                dve.wait_ge(sg("s1_h"), s0 + s)
                            weigh(s + 1, s0)
                        dve.wait_ge(sg("s1_dbu"), s0 + (s + 1))
                        dve.wait_ge(sg("s1_dA"), s0 + (s + 1))
                        if s >= 2:
                            dve.wait_ge(sg("s1_hc"), s0 + (s - 1))
                        v.tensor_tensor_scan(hs[s % 2], dA[s % 2], dbu[s % 2], 0.0, ALU.mult, ALU.add).then_inc(
                            sg("s1_h"), 1)
                        if s >= 1:
                            read_out(s - 1, s0)
                        if more:
                            front(s, k + 1, 1 - par)
                    read_out(S1 - 1, s0)
                if more:
                    dve.wait_ge(sg("s1dt_ready"), (0 if k is None else k + 1) + 1)
                    weigh(0 if k is None else S1, 0 if k is None else s0)
                if k is not None:
                    dve.wait_ge(sg("s1_acc"), s0 + S1)
                    v.scalar_tensor_tensor(total, u1[par], W1("dp"), acc, ALU.mult, ALU.add).then_inc(
                        sg("s1_total"), 1)
                    dve.wait_ge(sg("s1_total"), k + 1)
                    v.scalar_tensor_tensor(yz, total, 0.5, z1[par], ALU.mult, ALU.mult).then_inc(sg("s1_gated"), 1)

            chunk_pairs(dve, front, chunk)
            chunks = [slice(BANK * ch, BANK * ch + BANK) for ch in range(NCHUNK)]
            for ch, at in enumerate(chunks):
                dve.wait_ge(sg("ln_mean"), ch + 1)
                v.tensor_tensor(O[:, at], O[:, at], bank[ch], ALU.subtract).then_inc(sg("ln_centred"), 1)
            dve.wait_ge(sg("ln_centred"), NCHUNK)
            order = Order(dve, "ln_order")
            for ch, at in enumerate(chunks):
                dve.wait_ge(sg("ln_scale"), ch + 1)
                order(v.scalar_tensor_tensor(O[:, at], O[:, at], W1("gamma"), SS[:, at], ALU.mult, ALU.mult))
                order(v.scalar_tensor_tensor(X[:, at], O[:, at], W1("beta"), X[:, at], ALU.add, ALU.add))

            def call(m, n, d, c):
                raw = raws[d]

                def W(name):
                    a, b = Ws[name]
                    return raw[:, a:b]
                dve.wait_ge(sg("zeroed"), 1)
                dve.wait_ge(sg(f"block_weights_loaded{d}"), (m * 2 + n) * 16 + 16)
                v.tensor_tensor(wxa, W("wx"), W("cxa"), ALU.mult)
                v.tensor_tensor(wxb, W("wx"), W("cxb"), ALU.mult)
                for tp, cw in ((0, "cbca"), (1, "cbcb")):
                    v.tensor_tensor(wbc[tp], W("wbc"), W(cw), ALU.mult)
                for hd in range(2):
                    v.tensor_scalar(wog[hd], W(f"wo{hd}"), W("gnw")[:, hd:hd + 1], None, ALU.mult)
                v.tensor_scalar(bbc_minus, W("bbc"), -1.0, None, ALU.mult)
                v.tensor_copy(dtx[:, 32:160], W("seldt_bx")[:, 16:144])
                v.tensor_scalar(dtx[:, 16:32], W("seldt_bx")[:, 0:16], 0.125, None, ALU.mult)
                dve.wait_ge(sg("expA_ready"), c + 1)
                v.scalar_tensor_tensor(dtx[:, 0:16], W("seldt_bx")[:, 0:16], -1.0, expA, ALU.mult, ALU.mult)
                v.scalar_tensor_tensor(Dhalf.rearrange("p (h l) -> p h l", l=L),
                                       W("dh").unsqueeze(2).broadcast_to([128, 8, L]), 0.5,
                                       C("stack").unsqueeze(1).broadcast_to([128, 8, L]), ALU.mult,
                                       ALU.mult).then_inc(sg("folded"), 1)
                dve.wait_ge(sg("y_ready"), y_value(m, n, d))
                for ch in range(NCHUNK):
                    at = slice(BANK * ch, BANK * ch + BANK)
                    dve.wait_ge(sg("norm_scale"), c * NCHUNK + (ch + 1))
                    v.scalar_tensor_tensor(XN[:, at], Y[:, at], W("nw"), O[:, at], ALU.mult, ALU.mult).then_inc(
                        sg("normed"), 1)
                order = Order(dve, "block_order", dve.snap(c * 8))
                for i in range(16):
                    ch, hd = i // 2, i % 2
                    dve.wait_ge(sg("z_tanh"), c * 16 + (i + 1))
                    v.scalar_tensor_tensor(Z2[:, TOK * hd + BANK * ch:TOK * hd + BANK * ch + BANK], tz[i % 4], 1.0,
                                           bank[i % 4], ALU.add, ALU.mult).then_inc(sg("z_ready"), 1)
                    if i == 3:
                        dve.wait_ge(sg("dt_psum"), c + 1)
                        for hq in range(2):
                            last = v.tensor_scalar(DT[:, 512 * hq:512 * hq + 512], bank[4 + hq], W("bdt"), None,
                                                   ALU.add)
                        last.then_inc(sg("dt_added"), 1)
                        dve.wait_ge(sg("dt_exp"), c + 1)
                    if 4 <= i < 12:
                        softplus(i - 4, DT, dtw[0], dtw[1], dtw[2], order)
                    if i == 12:
                        v.tensor_scalar(DT, DT, C("dtrow")[:, 0:1], C("dtrow")[:, 1:2], ALU.mult, ALU.add).then_inc(
                            sg("dt_ready"), 1)
                dve.wait_ge(sg("z_ready"), c * 16 + 16)
                dve.wait_ge(sg("normed"), c * NCHUNK + NCHUNK)

                def stage(t, T, q, free):
                    if free:
                        dve.wait_ge(sg("projected"), T + (t - 3))
                    s = SA[t % 4]
                    src = axis(XN3, d, q).rearrange("p i j -> p (i j)")
                    v.tensor_copy(s[64:128, 1:L], src[0:64, 0:L - 1])
                    v.tensor_copy(s[0:64, L:2 * L], src[64:128, :]).then_inc(sg("staged_shifted"), 1)

                def step(tau, T, known, q0, G):
                    if part_of(known, 2):
                        q = (q0 + (tau + 2)) if known is None else tau + 2
                        stage(tau + 2, T, q, later(known, 2, 4))
                    if part_of(known, 0):
                        p, r = tau % 2, tau % 4
                        dve.wait_ge(sg("a_ready"), T + (tau + 1))
                        if later(known, 0, 2):
                            dve.wait_ge(sg("decay_logs"), T + (tau - 1))
                        v.tensor_tensor(AM[p][0].rearrange("p (h l) -> p h l", l=L),
                                        DA[p][:, 0:16].rearrange("p (h b) -> p h b", b=2)[:, :, 0:1].broadcast_to(
                                            [128, 8, L]),
                                        C("span").unsqueeze(1).broadcast_to([128, 8, L]), ALU.mult).then_inc(
                            sg("am0_ready"), 1)
                        dve.wait_ge(sg("sigmoid_ready"), T + (tau + 1))
                        if later(known, 0, 4):
                            dve.wait_ge(sg("y_psum"), T + (tau - 3))
                        for b in range(NB):
                            h = slice(64 * b, 64 * b + 64)
                            last = v.scalar_tensor_tensor(
                                X2[r].rearrange("p (h b e) -> p h b e", b=2, e=HP)[h, :, b, :],
                                TX[p][h, 0:128].rearrange("p (h e) -> p h e", e=HP), 2.0,
                                bank[p][h, PX].rearrange("p (h e) -> p h e", e=HP), ALU.mult, ALU.mult)
                        last.then_inc(sg("x_ready"), 1)
                        if later(known, 0, 2):
                            dve.wait_ge(sg("scored"), T + (tau - 1))
                        bc, tb = UB[p], TX[p][:, 128:192]
                        for b in range(NB):
                            h = slice(32 * b, 32 * b + 32)
                            v.scalar_tensor_tensor(BB[p][h, 64 * b:64 * b + 64], tb[h, :], 2.0, bc[h, :], ALU.mult,
                                                   ALU.mult)
                        v.scalar_tensor_tensor(C2[p][0:64, :], tb[64:128, :], 2.0, bc[64:128, :], ALU.mult,
                                               ALU.mult).then_inc(sg("bc_ready"), 1)
                    if part_of(known, -1):
                        p = (tau - 1) % 2
                        dve.wait_ge(sg("scored"), T + tau)
                        v.tensor_tensor(GM[p], bank[4 + p][:, 128:192], C("diag2"), ALU.mult).then_inc(
                            sg("gm_ready"), 1)
                        dve.wait_ge(sg("gm_ready"), T + tau)
                        dve.wait_ge(sg("decay_ready"), T + tau)
                        if later(known, -1, 2):
                            dve.wait_ge(sg("y_psum"), T + (tau - 2))
                        v.tensor_tensor(MM[p].rearrange("p (h l) -> p h l", l=L),
                                        DK[p].rearrange("p (h l) -> p h l", l=L),
                                        GM[p].unsqueeze(1).broadcast_to([128, 8, L]), ALU.mult).then_inc(
                            sg("mixed"), 1)
                    if part_of(known, -2):
                        p = (tau - 2) % 2
                        q = (q0 + (tau - 2)) if known is None else tau - 2
                        dve.wait_ge(sg("y_psum"), T + (tau - 1))
                        z = Z24[:, :, :, bass.ds(q, 1)] if d == 0 else Z24[:, :, bass.ds(q, 1), :]
                        z = z.rearrange("p h i j -> p h (i j)")
                        v.tensor_tensor(z,
                                        bank[4 + p][:, 0:128].rearrange("p (h l) -> p h l", l=L), z,
                                        ALU.mult).then_inc(sg("gated"), 1)

                    now, q = group(tau, q0, 6)
                    if now:
                        dve.wait_ge(sg("out_psum"), G + (tau // 8))
                        dve.wait_ge(sg("gate_scale"), G + (tau // 8))
                        v.tensor_tensor(grown, bank[6], gate, ALU.mult).then_inc(sg("scaled"), 1)
                        dve.wait_ge(sg("scaled"), G + (tau // 8))
                        yq, like = axis_group(Y3, d, q)
                        v.tensor_tensor(yq, yq, like(grown), ALU.add).then_inc(sg("grown"), 1)

                tiles(dve, c, -2, L + 8, step, lead=1)
                dve.wait_ge(sg("grown"), c * NGROUP + NGROUP)
                v.tensor_copy(small[:, 62:63], small[:, 60:61]).then_inc(sg("y_ready"), 1)
                dve.wait_ge(sg("y_ready"), y_value(m, n, d) + 1)
                v.tensor_copy(small[:, 60:61], small[:, 60:61]).then_inc(sg(f"block_done{d}"), 1)

            def entry(m):
                groupnorm(m + 2, Y, "y_ready")

            def leave(m):
                v.tensor_tensor(X, X, Y, ALU.add).then_inc(sg("x_added"), 1)
                dve.wait_ge(sg("x_added"), m + 1)

            v.memset(small[:, 60:61], 0.0)
            rounds(dve, entry, call, leave)
            v.tensor_copy(small[:, 61:62], X[:, 0:1]).then_inc(sg("x_final"), 1)
            for k in range(0, 8, 2):
                dve.wait_ge(sg("out_in_psum"), k + 1)
                v.tensor_copy(O[:, BANK * k:BANK * k + BANK], bank[k]).then_inc(sg("out_turned"), 1)


def _constants():
    import numpy as np
    p = np.arange(128)
    b, s = p // 64, p % 64
    l = np.arange(64)
    f = np.float32
    c = {}
    c["ident"] = np.eye(128)
    same = b[:, None] == b[None, :]
    c["mean64"] = same / 64.0
    c["pair"] = (p[:, None] // 2 == p[None, :] // 2) / (2.0 * TOK)
    bp = (p // 16) % 2
    c["ssum"] = (bp[:, None] == b[None, :]) / 128.0
    c["between"] = np.where(b[:, None] == 0, s[:, None] > l[None, :], s[:, None] < l[None, :])
    c["span"] = np.where(b[:, None] == 0, s[:, None] <= l[None, :], s[:, None] >= l[None, :])
    c["diag2"] = 1.0 + (s[:, None] == l[None, :])
    c["stack"] = s[:, None] == l[None, :]
    r = p % 32
    c["maskdt"] = (r[:, None] <= 16) & (p[:, None] // 32 == np.arange(8)[None, :] % 4)
    c["dtrow"] = np.stack([r < 16, r == 16], axis=1)
    c["two"] = np.full((128, 1), 2.0)
    k16 = np.arange(16) // 8
    c["mask16"] = np.where((p[:, None] // 8) == k16[None, :], 0.0, -1e30)
    c["maskbc"] = np.where(b[:, None] == k16[None, :], 0.0, -1e30)
    c["ones"] = np.ones((128, 128))
    c["eps6"], c["eps6x4"], c["eps5"] = (np.full((128, 1), e) for e in (1e-6, 4e-6, 1e-5))
    pos = np.linspace(0.0, 15.0, 64).astype(f)
    lo = (5 * l) // 21
    frac = (pos - lo).astype(f)
    wc = np.zeros((16, 64), f)
    wc[lo, l] += (1.0 - frac)
    wc[np.minimum(lo + 1, 15), l] += frac
    interp = np.zeros((4, 128, 128), f)
    for hlo in range(4):
        for bb in range(2):
            interp[hlo, 64 * bb + 16 * hlo:64 * bb + 16 * hlo + 16, 64 * bb:64 * bb + 64] = wc
    c["interp"] = interp.transpose(1, 0, 2).reshape(128, 512)
    c["wy"] = np.broadcast_to(frac, (128, 64))
    packed = np.concatenate([np.asarray(c[n], f).reshape(128, w) for n, w in CONST_COLS], axis=1)
    pool = np.zeros((2, 8, 128, 128), f)
    for bb in range(2):
        for jj in range(8):
            for ch in range(64):
                pool[bb, jj, 64 * bb + ch, 16 * jj + ch // 4] = 1.0 / 16.0
    pool = pool.reshape(16, 128, 128).transpose(1, 0, 2).reshape(128, 2048)
    state = np.zeros((128, 2, 16, 128), f)
    for k in range(16):
        state[[k, 32 + k, 64 + k], 0, k] = 1.0
        state[[16 + k, 48 + k, 80 + k], 1, k] = 1.0
    return packed, pool, state.reshape(128, 4096)


def _pack(cols, given):
    import numpy as np
    out = np.zeros((128, width(cols)), np.float32)
    at = spans(cols)
    for name, a in given.items():
        lo, hi = at[name]
        a = np.asarray(a)
        a = a[:, None] if a.ndim == 1 else a
        out[0:a.shape[0], lo:hi] = a
    return out


def _halves(wt):
    import numpy as np
    return np.concatenate([wt[0:128], wt[128:256]], axis=1)


def _stage0(w):
    g = {}
    for short, name in (("gq", "gcn_qw"), ("gk", "gcn_kw"), ("gv", "gcn_vw"), ("q", "qw"), ("k", "kw"), ("v", "vw")):
        g[short] = _halves(w[name].T)
    g["gw"] = _halves(w["gcn_weight"])
    g["gb"] = w["gcn_bias"].reshape(2, 128).T
    g["gvb"] = w["gcn_vb"].reshape(2, 128).T
    g["gqb"], g["gkb"], g["qb"], g["kb"] = w["gcn_qb"], w["gcn_kb"], w["qb"], w["kb"]
    g["vb"] = w["vb"][None, :]
    return _pack(L0_COLS, g)


def _stage1(w):
    import numpy as np
    g = {}
    win = w["W_in"].T
    g["winx_a"] = np.concatenate([win[:, 0:128]] * 2)
    taps = w["W_conv"][:, 0, :].T
    g["wca"] = np.concatenate([np.broadcast_to(taps[3], (64, 128)), np.broadcast_to(taps[2], (64, 128))])
    g["wcb"] = np.concatenate([np.broadcast_to(taps[1], (64, 128)), np.broadcast_to(taps[0], (64, 128))])
    g["wz"] = win[:, 128:256]
    wxp = np.zeros((128, 64), np.float32)
    wxp[:, 0:32] = w["W_xproj"][4:36].T
    wxp[:, 32:36] = w["W_xproj"][0:4].T
    g["wxp"] = wxp
    wdt = np.zeros((128, 128), np.float32)
    wdt[32:36] = w["W_dt"].T
    g["wdt"] = wdt
    g["bconv"], g["bdt"], g["alog"], g["dp"] = w["b_conv"], w["b_dt"], w["A_log"], w["D_param"]
    g["wout"] = w["W_out"].T
    g["gamma"], g["beta"] = np.concatenate([w["gamma"]] * 2), np.concatenate([w["beta"]] * 2)
    return _pack(L1_COLS, g)


def _block(norm_w, Win, Wconv, bconv, dt_bias, A_log, D, gn_w, Wout):
    import numpy as np
    g = {}
    g["wx"] = np.concatenate([Win[:, 128:256]] * 2)
    taps = Wconv.T

    def pair(k0, k1, row):
        return np.concatenate([np.broadcast_to(row[k0], (64, row.shape[1])),
                               np.broadcast_to(row[k1], (64, row.shape[1]))])
    g["cxa"], g["cxb"] = pair(3, 2, taps[:, 0:128]), pair(1, 0, taps[:, 0:128])
    spread = np.zeros((4, 2, 2, 32), np.float32)
    spread[:, :, :, 0:16] = taps[:, 128:160].reshape(4, 2, 1, 16)
    spread = spread.reshape(4, 128)
    g["cbca"], g["cbcb"] = pair(3, 2, spread), pair(1, 0, spread)
    wb = np.zeros((64, 2, 2, 32), np.float32)
    wb[..., 0:16] = Win[:, 256:288].reshape(64, 2, 1, 16)
    g["wbc"] = np.concatenate([wb.reshape(64, 128)] * 2)
    sel = np.zeros((4, 32, 144), np.float32)
    for h in range(8):
        for b in range(2):
            sel[:, 8 * b + h, 2 * h + b] = 1.0
    sel[:, 16, 16:144] = bconv[0:128]
    g["seldt_bx"] = sel.reshape(128, 144)
    bb = np.zeros((2, 2, 32), np.float32)
    bb[..., 0:16] = bconv[128:160].reshape(2, 1, 16)
    g["bbc"] = bb.reshape(128)
    for hd in range(2):
        wz = np.zeros((2, 64, 4, 2, 16), np.float32)
        wo = np.zeros((4, 2, 16, 2, 64), np.float32)
        for b in range(2):
            wz[b, :, :, b] = Win[:, 64 * hd:64 * hd + 64].reshape(64, 4, 16)
            wo[:, b, :, b] = Wout[64 * hd:64 * hd + 64].reshape(4, 16, 64)
        g[f"wz{hd}"], g[f"wo{hd}"] = wz.reshape(128, 128), wo.reshape(128, 128)
    wdt = np.zeros((2, 64, 32), np.float32)
    bdt = np.zeros((4, 32), np.float32)
    for b in range(2):
        wdt[b, :, 8 * b:8 * b + 8] = Win[:, 288:296]
        bdt[:, 8 * b:8 * b + 8] = dt_bias
    g["wdt"], g["bdt"] = wdt.reshape(128, 32), bdt.reshape(128)
    g["alog"], g["dh"] = np.broadcast_to(np.repeat(A_log, 2), (128, 16)), np.broadcast_to(D, (128, 8))
    g["nw"] = np.concatenate([norm_w] * 2)
    gw = gn_w.reshape(2, 4, 1, 16)
    g["gnw"] = np.broadcast_to(gw, (2, 4, 2, 16)).reshape(2, 128).T
    return _pack(CALL_COLS, g)


def kernel(**inputs):
    import numpy as np
    import concourse.bacc as bacc
    from concourse.bass_utils import run_bass_kernel_spmd

    a = {k: np.asarray(v) for k, v in inputs.items()}
    names = ("norm_w", "Win", "Wconv", "bconv", "dt_bias", "A_log", "D", "gn_w", "Wout")
    calls = [_block(*(a[f"L{st}_conv_{ax}_{n}"][i] for n in names))
             for st in (2, 3) for i in range(2) for ax in ("t", "b")]
    consts, pool_sel, state_sel = _constants()
    arrays = {
        "x": np.ascontiguousarray(a["x"]), "consts": consts, "pool_sel": pool_sel, "state_sel": state_sel,
        "l0w": _stage0({k[8:]: v for k, v in a.items() if k.startswith("L0_conv_")}),
        "l1w": _stage1({k[8:]: v for k, v in a.items() if k.startswith("L1_conv_")}),
        "callw": np.stack(calls),
    }
    nc = bacc.Bacc("TRN2", target_bir_lowering=False, num_devices=1)
    args = [nc.dram_tensor(k, v.shape, mybir.dt.float32, kind="ExternalInput").ap() for k, v in arrays.items()]
    out = nc.dram_tensor("out", (2, 64, 64, 64), mybir.dt.float32, kind="ExternalOutput").ap()
    program(nc, *args, out)
    r = run_bass_kernel_spmd(nc, [arrays], core_ids=[0])
    return r.results[0]["out"]
```
